# Optimizing a Trainium2 kernel written in Bass

```python
import numpy as np
import jax
import jax.numpy as jnp

def _softmax(x, axis=-1):
    return jax.nn.softmax(x, axis=axis)

def _gelu(x):
    return jax.nn.gelu(x, approximate=True)

def _silu(x):
    return jax.nn.silu(x)

def _sigmoid(x):
    return jax.nn.sigmoid(x)

def _layernorm(x, axis=-1, eps=1e-05):
    m = jnp.mean(x, axis=axis, keepdims=True)
    v = jnp.var(x, axis=axis, keepdims=True)
    return (x - m) / jnp.sqrt(v + eps)

def _scatter_add(tgt, idx, src, axis=0):
    return tgt.at[idx].add(src)

def _segment_sum(src, seg, n):
    return jax.ops.segment_sum(src, seg, n)
kernel_name = 'mk_seq_postln_d2_jaxref_r4_9e03ae'

def setup_inputs(seed: int=0):
    np.random.seed(seed)
    _w = jnp.asarray

    def _L0_attn_setup():
        import jax, jax.numpy as jnp
        import numpy as np
        B, S, DIN, DIM = (1, 1024, 256, 256)
        NH, NKV = (16, 4)
        HD = DIM // NH
        GS = NH // NKV
        key = jax.random.key(seed)
        ks = jax.random.split(key, 5)

        def w(k, shape, fan_in):
            return jax.random.normal(k, shape, jnp.float32) * fan_in ** (-0.5)
        return {'x': jax.random.normal(ks[0], (B, S, DIN), jnp.float32), 'wq': w(ks[1], (DIM, DIN), DIN), 'wk': w(ks[2], (NKV * HD, DIN), DIN), 'wv': w(ks[3], (NKV * HD, DIN), DIN), 'wo': w(ks[4], (DIM, DIM), DIM)}
    _L0_attn_in = _L0_attn_setup()

    def _L0_ffn_setup():
        import jax, jax.numpy as jnp
        import numpy as np
        B, S, H, F, E = (4, 512, 256, 1024, 8)
        key = jax.random.key(seed)
        ks = jax.random.split(key, 8)
        s = 1.0 / np.sqrt(H)
        sf = 1.0 / np.sqrt(F)
        return {'x': jax.random.normal(ks[0], (B, S, H), jnp.float32), 'wr': jax.random.uniform(ks[1], (H, E), jnp.float32, -s, s), 'br': jax.random.uniform(ks[2], (E,), jnp.float32, -s, s), 'w1': jax.random.uniform(ks[3], (E, H, F), jnp.float32, -s, s), 'b1': jax.random.uniform(ks[4], (E, F), jnp.float32, -s, s), 'w2': jax.random.uniform(ks[5], (E, F, H), jnp.float32, -sf, sf), 'b2': jax.random.uniform(ks[6], (E, H), jnp.float32, -sf, sf)}
    _L0_ffn_in = _L0_ffn_setup()

    def _L1_attn_setup():
        import jax, jax.numpy as jnp
        import numpy as np
        from jax import lax
        D_MODEL = 256
        D_STATE = 16
        D_CONV = 4
        EXPAND = 2
        D_INNER = EXPAND * D_MODEL
        DT_RANK = -(-D_MODEL // 16)
        BATCH = 2
        T = 256

        def _silu(u):
            return u * jax.nn.sigmoid(u)

        def _forward(x, W_in, conv_w, conv_b, W_xproj, W_dt, b_dt, A_log, D_param, W_out):
            B, Tlen, _ = x.shape
            xz = x @ W_in
            x_b, z = jnp.split(xz, 2, axis=-1)
            xpad = jnp.pad(x_b, ((0, 0), (D_CONV - 1, 0), (0, 0)))
            xc = conv_b
            for k in range(D_CONV):
                xc = xc + xpad[:, k:k + Tlen, :] * conv_w[:, k]
            xc = _silu(xc)
            proj = xc @ W_xproj
            delta_raw = proj[..., :DT_RANK]
            B_in = proj[..., DT_RANK:DT_RANK + D_STATE]
            C_in = proj[..., DT_RANK + D_STATE:]
            delta = jax.nn.softplus(delta_raw @ W_dt + b_dt)
            A = -jnp.exp(A_log)
            A_bar = jnp.exp(delta[..., None] * A)
            Bx = delta[..., None] * B_in[:, :, None, :] * xc[..., None]

            def step(h, ins):
                a_t, bx_t, c_t, xc_t = ins
                h = a_t * h + bx_t
                y_t = jnp.einsum('bds,bs->bd', h, c_t) + D_param * xc_t
                return (h, y_t)
            h0 = jnp.zeros((B, D_INNER, D_STATE), dtype=x.dtype)
            ins = (jnp.swapaxes(A_bar, 0, 1), jnp.swapaxes(Bx, 0, 1), jnp.swapaxes(C_in, 0, 1), jnp.swapaxes(xc, 0, 1))
            _, ys = lax.scan(step, h0, ins)
            y = jnp.swapaxes(ys, 0, 1) * _silu(z)
            return y @ W_out
        key = jax.random.key(seed)
        ks = jax.random.split(key, 9)
        s = 0.02
        x = jax.random.normal(ks[0], (BATCH, T, D_MODEL), dtype=jnp.float32)
        W_in = jax.random.normal(ks[1], (D_MODEL, 2 * D_INNER), dtype=jnp.float32) * s
        conv_w = jax.random.normal(ks[2], (D_INNER, D_CONV), dtype=jnp.float32) * 0.2
        conv_b = jax.random.normal(ks[3], (D_INNER,), dtype=jnp.float32) * 0.02
        W_xproj = jax.random.normal(ks[4], (D_INNER, DT_RANK + 2 * D_STATE), dtype=jnp.float32) * s
        W_dt = jax.random.normal(ks[5], (DT_RANK, D_INNER), dtype=jnp.float32) * s
        b_dt = jax.random.normal(ks[6], (D_INNER,), dtype=jnp.float32) * 0.02
        A_log = jnp.broadcast_to(jnp.log(jnp.arange(1, D_STATE + 1, dtype=jnp.float32)), (D_INNER, D_STATE)).copy()
        D_param = jnp.ones((D_INNER,), dtype=jnp.float32)
        W_out = jax.random.normal(ks[7], (D_INNER, D_MODEL), dtype=jnp.float32) * s
        return {'x': x, 'W_in': W_in, 'conv_w': conv_w, 'conv_b': conv_b, 'W_xproj': W_xproj, 'W_dt': W_dt, 'b_dt': b_dt, 'A_log': A_log, 'D_param': D_param, 'W_out': W_out}
    _L1_attn_in = _L1_attn_setup()

    def _L1_ffn_setup():
        import jax, jax.numpy as jnp
        import numpy as np
        EPS = 1e-05

        def _quantize(W):
            gamma = jnp.mean(jnp.abs(W))
            return jnp.clip(jnp.round(W / (gamma + EPS)), -1.0, 1.0)
        key = jax.random.key(seed)
        k_x, k_w1, k_b1, k_w2, k_b2 = jax.random.split(key, 5)
        n_embd = 256
        d_ff = 4 * n_embd
        B, S = (4, 1024)
        bound1 = 1.0 / np.sqrt(n_embd)
        bound2 = 1.0 / np.sqrt(d_ff)
        x = jax.random.normal(k_x, (B, S, n_embd), dtype=jnp.float32)
        W1 = jax.random.uniform(k_w1, (d_ff, n_embd), jnp.float32, -bound1, bound1)
        b1 = jax.random.uniform(k_b1, (d_ff,), jnp.float32, -bound1, bound1)
        W2 = jax.random.uniform(k_w2, (n_embd, d_ff), jnp.float32, -bound2, bound2)
        b2 = jax.random.uniform(k_b2, (n_embd,), jnp.float32, -bound2, bound2)
        return {'x': x, 'W1': W1, 'b1': b1, 'W2': W2, 'b2': b2}
    _L1_ffn_in = _L1_ffn_setup()
    _d = {'L0_attn_x': _L0_attn_in['x'], 'L0_attn_wq': _L0_attn_in['wq'], 'L0_attn_wk': _L0_attn_in['wk'], 'L0_attn_wv': _L0_attn_in['wv'], 'L0_attn_wo': _L0_attn_in['wo'], 'L0_ffn_wr': _L0_ffn_in['wr'], 'L0_ffn_br': _L0_ffn_in['br'], 'L0_ffn_w1': _L0_ffn_in['w1'], 'L0_ffn_b1': _L0_ffn_in['b1'], 'L0_ffn_w2': _L0_ffn_in['w2'], 'L0_ffn_b2': _L0_ffn_in['b2'], 'L1_attn_W_in': _L1_attn_in['W_in'], 'L1_attn_conv_w': _L1_attn_in['conv_w'], 'L1_attn_conv_b': _L1_attn_in['conv_b'], 'L1_attn_W_xproj': _L1_attn_in['W_xproj'], 'L1_attn_W_dt': _L1_attn_in['W_dt'], 'L1_attn_b_dt': _L1_attn_in['b_dt'], 'L1_attn_A_log': _L1_attn_in['A_log'], 'L1_attn_D_param': _L1_attn_in['D_param'], 'L1_attn_W_out': _L1_attn_in['W_out'], 'L1_ffn_W1': _L1_ffn_in['W1'], 'L1_ffn_b1': _L1_ffn_in['b1'], 'L1_ffn_W2': _L1_ffn_in['W2'], 'L1_ffn_b2': _L1_ffn_in['b2']}
    _x0 = _d['L0_attn_x']
    _d['L0_attn_x'] = jax.random.normal(jax.random.fold_in(jax.random.key(seed), 1), (2, 2048, 256), dtype=_x0.dtype)
    del _x0
    return _d

def reference(L0_attn_x, L0_attn_wq, L0_attn_wk, L0_attn_wv, L0_attn_wo, L0_ffn_wr, L0_ffn_br, L0_ffn_w1, L0_ffn_b1, L0_ffn_w2, L0_ffn_b2, L1_attn_W_in, L1_attn_conv_w, L1_attn_conv_b, L1_attn_W_xproj, L1_attn_W_dt, L1_attn_b_dt, L1_attn_A_log, L1_attn_D_param, L1_attn_W_out, L1_ffn_W1, L1_ffn_b1, L1_ffn_W2, L1_ffn_b2):

    def _L0_attn_ref(x, wq, wk, wv, wo):
        import jax, jax.numpy as jnp
        import numpy as np
        B, S, DIN, DIM = (1, 1024, 256, 256)
        NH, NKV = (16, 4)
        HD = DIM // NH
        GS = NH // NKV
        b, s, _ = x.shape
        q = (x @ wq.T).reshape(b, s, NKV, GS, HD)
        k = (x @ wk.T).reshape(b, s, NKV, HD)
        v = (x @ wv.T).reshape(b, s, NKV, HD)
        scale = jnp.asarray(HD ** 0.5, x.dtype)
        att = jnp.einsum('bsgmd,btgd->bgmst', q, k) / scale
        causal = jnp.triu(jnp.ones((s, s), bool), 1)
        att = jnp.where(causal, -jnp.inf, att)
        att = jax.nn.softmax(att, axis=-1)
        ctx = jnp.einsum('bgmst,btgd->bsgmd', att, v).reshape(b, s, DIM)
        return ctx @ wo.T

    def _L0_ffn_ref(x, wr, br, w1, b1, w2, b2):
        import jax, jax.numpy as jnp
        import numpy as np
        B, S, H, F, E = (4, 512, 256, 1024, 8)
        scores = jnp.einsum('bsh,he->bse', x, wr) + br
        expert_id = jnp.argmax(scores, axis=-1)
        h = jnp.einsum('bsh,ehf->ebsf', x, w1) + b1[:, None, None, :]
        h = jax.nn.gelu(h, approximate=False)
        y = jnp.einsum('ebsf,efh->ebsh', h, w2) + b2[:, None, None, :]
        one_hot = jax.nn.one_hot(expert_id, E, dtype=x.dtype)
        out = jnp.einsum('ebsh,bse->bsh', y, one_hot)
        return out

    def _L1_attn_ref(x, W_in, conv_w, conv_b, W_xproj, W_dt, b_dt, A_log, D_param, W_out):
        import jax, jax.numpy as jnp
        import numpy as np
        from jax import lax
        D_MODEL = 256
        D_STATE = 16
        D_CONV = 4
        EXPAND = 2
        D_INNER = EXPAND * D_MODEL
        DT_RANK = -(-D_MODEL // 16)
        BATCH = 2
        T = 256

        def _silu(u):
            return u * jax.nn.sigmoid(u)

        def _forward(x, W_in, conv_w, conv_b, W_xproj, W_dt, b_dt, A_log, D_param, W_out):
            B, Tlen, _ = x.shape
            xz = x @ W_in
            x_b, z = jnp.split(xz, 2, axis=-1)
            xpad = jnp.pad(x_b, ((0, 0), (D_CONV - 1, 0), (0, 0)))
            xc = conv_b
            for k in range(D_CONV):
                xc = xc + xpad[:, k:k + Tlen, :] * conv_w[:, k]
            xc = _silu(xc)
            proj = xc @ W_xproj
            delta_raw = proj[..., :DT_RANK]
            B_in = proj[..., DT_RANK:DT_RANK + D_STATE]
            C_in = proj[..., DT_RANK + D_STATE:]
            delta = jax.nn.softplus(delta_raw @ W_dt + b_dt)
            A = -jnp.exp(A_log)
            A_bar = jnp.exp(delta[..., None] * A)
            Bx = delta[..., None] * B_in[:, :, None, :] * xc[..., None]

            def step(h, ins):
                a_t, bx_t, c_t, xc_t = ins
                h = a_t * h + bx_t
                y_t = jnp.einsum('bds,bs->bd', h, c_t) + D_param * xc_t
                return (h, y_t)
            h0 = jnp.zeros((B, D_INNER, D_STATE), dtype=x.dtype)
            ins = (jnp.swapaxes(A_bar, 0, 1), jnp.swapaxes(Bx, 0, 1), jnp.swapaxes(C_in, 0, 1), jnp.swapaxes(xc, 0, 1))
            _, ys = lax.scan(step, h0, ins)
            y = jnp.swapaxes(ys, 0, 1) * _silu(z)
            return y @ W_out
        return _forward(x, W_in, conv_w, conv_b, W_xproj, W_dt, b_dt, A_log, D_param, W_out)

    def _L1_ffn_ref(x, W1, b1, W2, b2):
        import jax, jax.numpy as jnp
        import numpy as np
        EPS = 1e-05

        def _quantize(W):
            gamma = jnp.mean(jnp.abs(W))
            return jnp.clip(jnp.round(W / (gamma + EPS)), -1.0, 1.0)
        Wq1 = _quantize(W1)
        Wq2 = _quantize(W2)
        h = jax.nn.relu(jnp.einsum('bsd,fd->bsf', x, Wq1) + b1)
        out = jnp.einsum('bsf,df->bsd', h, Wq2) + b2
        return out
    x = L0_attn_x
    x = _layernorm(x + _L0_attn_ref(x, L0_attn_wq, L0_attn_wk, L0_attn_wv, L0_attn_wo), axis=-1)
    x = _layernorm(x + _L0_ffn_ref(x, L0_ffn_wr, L0_ffn_br, L0_ffn_w1, L0_ffn_b1, L0_ffn_w2, L0_ffn_b2), axis=-1)
    x = _layernorm(x + _L1_attn_ref(x, L1_attn_W_in, L1_attn_conv_w, L1_attn_conv_b, L1_attn_W_xproj, L1_attn_W_dt, L1_attn_b_dt, L1_attn_A_log, L1_attn_D_param, L1_attn_W_out), axis=-1)
    x = _layernorm(x + _L1_ffn_ref(x, L1_ffn_W1, L1_ffn_b1, L1_ffn_W2, L1_ffn_b2), axis=-1)
    return x

_drawn_inputs = setup_inputs


def setup_inputs(seed=0):
    import zlib

    import numpy as np

    out = dict(_drawn_inputs(seed))
    spreads = {'L1_attn_D_param': (1.0, 0.6)}
    factors = {'L0_ffn_b1': 4.727,
     'L0_ffn_b2': 3.276,
     'L1_attn_W_in': 8.0,
     'L1_attn_conv_w': 8.0,
     'L1_attn_conv_b': 8.0,
     'L1_attn_W_xproj': 8.0,
     'L1_attn_W_dt': 8.0,
     'L1_attn_b_dt': 8.0,
     'L1_attn_A_log': 8.0,
     'L1_attn_W_out': 8.0,
     'L1_ffn_b1': 21.621,
     'L1_ffn_b2': 64.0}
    for name, (base, spread) in spreads.items():
        noise = np.random.default_rng([zlib.crc32(name.encode()), seed]).standard_normal(out[name].shape)
        drawn = base * np.exp(spread * noise) if base else spread * noise
        out[name] = jnp.asarray(drawn.astype(out[name].dtype))
    for name, factor in factors.items():
        out[name] = (out[name] * factor).astype(out[name].dtype)
    return out
```

```python
from contextlib import ExitStack

import numpy as np
import concourse.bass as bass
from concourse import mybir

F32 = mybir.dt.float32
BF16 = mybir.dt.bfloat16
I32 = mybir.dt.int32
ALU = mybir.AluOpType
ACT = mybir.ActivationFunctionType
AX = mybir.AxisListType

P = 128
BATCH, SEQ, D = 2, 2048, 256
TOK = BATCH * SEQ
KD = D // P
SEG = 512
HEADS, GROUPS, HD = 16, 4, 16
GS = HEADS // GROUPS
MASKED = -1.0e30
EPS = 1e-5


class Space:

    def __init__(self, nc, ctx, tag):
        self.nc, self.ctx, self.tag, self.sems = nc, ctx, tag, []
        ctx.callback(self.close)

    def close(self):
        self.nc.clear_and_free_semaphores(self.sems)
        with self.nc.Block():
            pass

    def sb(self, name, shape, dt=F32):
        return self.ctx.enter_context(self.nc.sbuf_tensor(f"{self.tag}_{name}", shape, dt))

    def ps(self, name, shape, dt=F32):
        return self.ctx.enter_context(self.nc.psum_tensor(f"{self.tag}_{name}", shape, dt))

    def sem(self, name):
        self.sems.append(self.nc.alloc_semaphore(f"{self.tag}_{name}"))
        return self.sems[-1]


def project_phase(nc, xT, wq, wkv, qk_parts, v_rows):
    NSEG = TOK // SEG
    with ExitStack() as ctx:
        s = Space(nc, ctx, "proj")
        w_q = s.sb("wq", [P, KD, D])
        w_kv = s.sb("wkv", [P, KD, P])
        xin = s.sb("xin", [P, 2, KD, SEG])
        hi = s.sb("hi", [P, 2, 3, SEG], BF16)
        rest = s.sb("rest", [P, 2, 3, SEG])
        mid = s.sb("mid", [P, 2, 3, SEG], BF16)
        lo = s.sb("lo", [P, 2, 3, SEG], BF16)
        vout = s.sb("vout", [P, 2, 4, 64])
        qk_ps = s.ps("qk", [P, 2, 3, SEG])
        v_ps = s.ps("v", [P, 2, SEG])
        w_in, x_in = s.sem("w_in"), [s.sem("x_in0"), s.sem("x_in1")]
        qk_done, v_done = s.sem("qk_done"), s.sem("v_done")
        hi_done, rest_done, mid_done, lo_done = s.sem("hi"), s.sem("rest"), s.sem("mid"), s.sem("lo")
        v_copied, stored = s.sem("v_copied"), [s.sem("stored0"), s.sem("stored1")]

        with nc.Block() as block:
            @block.sync
            def _(sp):
                def load(n, u):
                    sp.dma_start(xin[:, u], xT.rearrange("(k p) n -> p k n", p=P)[:, :, bass.ds(n * SEG, SEG)]
                                 ).then_inc(x_in[u], 16)

                def store(n, u):
                    for part, (buf, done) in enumerate(((hi, hi_done), (mid, mid_done), (lo, lo_done))):
                        sp.wait_ge(done, n + 1)
                        sp.dma_start(qk_parts[part].rearrange("(c p) n -> p c n", p=P)[:, :, bass.ds(n * SEG, SEG)],
                                     buf[:, u]).then_inc(stored[u], 16)
                    sp.wait_ge(v_copied, n + 1)
                    sp.dma_start(v_rows.rearrange("(a p) n -> p a n", p=P)[:, bass.ds(n * 4, 4), :],
                                 vout[:, u]).then_inc(stored[u], 16)

                sp.dma_start(w_q[:], wq.rearrange("(k p) n -> p k n", p=P)).then_inc(w_in, 16)
                sp.dma_start(w_kv[:], wkv.rearrange("(k p) n -> p k n", p=P)).then_inc(w_in, 16)
                for u in range(2):
                    load(u, u)
                with sp.Fori(0, NSEG // 2 - 1) as i:
                    for u in range(2):
                        sp.wait_ge(v_done, i * 2 + u + 1)
                        load(i * 2 + u + 2, u)
                        store(i * 2 + u, u)
                for u in range(2):
                    store(NSEG - 2 + u, u)
                for u in range(2):
                    sp.wait_ge(stored[u], 64 * (NSEG // 2))

            @block.tensor
            def _(pe):
                def products(n, i, u):
                    pe.wait_ge(x_in[u], i * 16 + 16)
                    for c in range(3):
                        for k in range(KD):
                            w = w_q[:, k, c * P:(c + 1) * P] if c < 2 else w_kv[:, k, :]
                            mm = pe.matmul(qk_ps[:, u, c], w, xin[:, u, k], start=(k == 0), stop=(k == KD - 1))
                    mm.then_inc(qk_done, 1)
                    for a in range(4):
                        for k in range(KD):
                            mm = pe.matmul(v_ps[:, u, a * 64:(a + 1) * 64], xin[:, u, k, a * P:(a + 1) * P],
                                           w_kv[:, k, 64:128], start=(k == 0), stop=(k == KD - 1))
                    mm.then_inc(v_done, 1)

                pe.wait_ge(w_in, 32)
                for u in range(2):
                    products(u, 0, u)
                with pe.Fori(1, NSEG // 2) as i:
                    for u in range(2):
                        pe.wait_ge(rest_done, i * 2 + u - 1)
                        pe.wait_ge(v_copied, i * 2 + u - 1)
                        products(i * 2 + u, i, u)

            @block.scalar
            def _(act):
                def split(n, u):
                    act.wait_ge(qk_done, n + 1)
                    act.activation(hi[:, u], qk_ps[:, u], ACT.Copy).then_inc(hi_done, 1)
                    act.wait_ge(v_done, n + 1)
                    act.activation(vout[:, u], v_ps[:, u, 0:256].rearrange("p (a d) -> p a d", d=64),
                                   ACT.Copy).then_inc(v_copied, 1)
                    act.wait_ge(rest_done, n + 1)
                    act.activation(mid[:, u], rest[:, u], ACT.Copy).then_inc(mid_done, 1)

                for u in range(2):
                    split(u, u)
                with act.Fori(1, NSEG // 2) as i:
                    for u in range(2):
                        act.wait_ge(stored[u], i * 64)
                        split(i * 2 + u, u)

            @block.vector
            def _(dve):
                with dve.Fori(0, NSEG // 2) as i:
                    for u in range(2):
                        n = i * 2 + u
                        dve.wait_ge(hi_done, n + 1)
                        dve.tensor_tensor(rest[:, u], qk_ps[:, u], hi[:, u], ALU.subtract).then_inc(rest_done, 1)

            @block.gpsimd
            def _(pool):
                with pool.Fori(0, NSEG // 2) as i:
                    for u in range(2):
                        n = i * 2 + u
                        pool.wait_ge(mid_done, n + 1)
                        pool.tensor_tensor(lo[:, u], rest[:, u], mid[:, u], ALU.subtract).then_inc(lo_done, 1)


QUADS, SB_PER_QUAD = SEQ // SEG, SEG // P
SBLK = SEQ // P
NG = BATCH * GROUPS
QK_PAIRS = ((0, 0), (0, 1), (1, 0), (1, 1), (0, 2), (2, 0))
KROWS = len(QK_PAIRS) * HD
SROWS = KROWS + 3
PRING = 8
M_LEAD = 1.15
LOADS = 16 * (2 * len(QK_PAIRS) + 1)


def attention_phase(nc, qk_parts, v_rows, shift_rows, ctx_rows, ident_f, ident_b, tri_st, tri_ts):
    m_units = []
    for i in range(SBLK):
        T = (i + 1) * P
        if T <= SEG:
            m_units += [(i, (m, m + 1), 0, T) for m in (0, 2)]
        else:
            for m in range(GS):
                m_units += [(i, (m,), t, min(1024, T - t)) for t in range(0, T, 1024)]
    NM = len(m_units) + 1
    steps = [(q, t) for q in range(QUADS) for t in range((q + 1) * SB_PER_QUAD)]
    NSTEP = len(steps)
    NE = NSTEP * GS

    def cols(q, t):
        return max(0, t - q * SB_PER_QUAD) * P

    schedule, m_cost, e_cost, mi, turn_at = [], 0, 0, 0, None
    m_total = sum(len(h) * k + 120 for _, h, _, k in m_units)
    e_total = sum(GS * (SEG - cols(q, t) + 150) for q, t in steps)
    for e in range(NE):
        q, t = steps[e // GS]
        e_cost += SEG - cols(q, t) + 150
        schedule.append(("scores", e))
        if mi < len(m_units) and m_cost / m_total < M_LEAD * e_cost / e_total:
            m_cost += len(m_units[mi][1]) * m_units[mi][3] + 120
            schedule.append(("max", mi))
            mi += 1
        if mi == len(m_units) and turn_at is None:
            turn_at = len(schedule) + 6
        if e % GS == 2 and e > GS:
            schedule.append(("values", e // GS - 1))
            if steps[e // GS - 1][1] == (steps[e // GS - 1][0] + 1) * SB_PER_QUAD - 1:
                schedule.append(("norm", steps[e // GS - 1][0]))
    schedule += [("values", NSTEP - 1), ("norm", QUADS - 1)]
    schedule.insert(turn_at, ("turn", 0))
    only_max = [("max", u) for u in range(len(m_units))] + [("turn", 0)]

    with ExitStack() as ctx:
        s = Space(nc, ctx, "att")
        NB = 3
        qa = [s.sb(f"qa{j}", [P, GS, SEQ], BF16) for j in range(NB)]
        ka = [s.sb(f"ka{j}", [P, SEQ], BF16) for j in range(NB)]
        va = [s.sb(f"va{j}", [P, SBLK, 2 * HD]) for j in range(NB)]
        prob = s.sb("prob", [P, PRING, SEG])
        mx = s.sb("mx", [P, GS, SBLK, 2])
        mrow = s.sb("mrow", [P, P])
        sh = s.sb("sh", [GS * SBLK, 3, P], BF16)
        sh_rest = s.sb("sh_rest", [GS * SBLK, P])
        num = s.sb("num", [P, 2, SEG])
        mx_ps = s.ps("mx_ps", [P, 2, 1024])
        st_ps = s.ps("st_ps", [P, 3, SEG])
        acc_ps = s.ps("acc_ps", [P, SEG])

        consts = s.sem("consts")
        loaded = [s.sem(f"loaded{j}") for j in range(NB)]
        mx_filled, mx_read = s.sem("mx_filled"), s.sem("mx_read")
        row_max, sh_hi, sh_res, sh_mid, sh_done = (s.sem(n) for n in ("row_max", "sh_hi", "sh_res", "sh_mid", "sh_done"))
        sh_out, sh_in = s.sem("sh_out"), [s.sem(f"sh_in{j}") for j in range(NB)]
        st_filled, exp_done, pv_done = s.sem("st_filled"), s.sem("exp_done"), s.sem("pv_done")
        num_done = s.sem("num_done")
        out_stored = [s.sem("out_stored0"), s.sem("out_stored1")]

        def groups(loop, run):
            run(0, None, 0, None)
            with loop(0, 2) as r:
                for u in range(3):
                    run(r * 3 + u + 1, r * 3 + u, (u + 1) % NB, u)
            run(NG - 1, NG - 2, (NG - 1) % NB, (NG - 2) % NB)
            run(None, NG - 1, None, (NG - 1) % NB)

        def order(jm, je):
            if je is None:
                return only_max
            return [x for x in schedule if jm is not None or x[0] not in ("max", "turn")]

        with nc.Block() as block:
            @block.sync
            def _(sp):
                def load(j, u):
                    b_, g_ = j // GROUPS, j % GROUPS
                    tok = b_ * SEQ
                    for r, (qp, kp) in enumerate(QK_PAIRS):
                        sp.dma_start(qa[u][r * HD:(r + 1) * HD],
                                     qk_parts[qp, bass.ds(g_ * GS * HD, GS * HD), bass.ds(tok, SEQ)]
                                     .rearrange("(m d) n -> d m n", d=HD)).then_inc(loaded[u], 16)
                        sp.dma_start(ka[u][r * HD:(r + 1) * HD],
                                     qk_parts[kp, bass.ds(D + g_ * HD, HD), bass.ds(tok, SEQ)]
                                     ).then_inc(loaded[u], 16)
                    sp.dma_start(va[u][:, :, 0:HD],
                                 v_rows[bass.ds(tok, SEQ), bass.ds(g_ * HD, HD)]
                                 .rearrange("(a p) d -> p a d", p=P)).then_inc(loaded[u], 16)

                def shift(j, u):
                    sp.wait_ge(sh_done, j + 1)
                    sp.dma_start(shift_rows.rearrange("k a p -> a k p"), sh[:]).then_inc(sh_out, 16)
                    sp.wait_ge(sh_out, 16 * j + 16)
                    sp.dma_start(qa[u][KROWS:SROWS], shift_rows.rearrange("k (m i) p -> k m (i p)", m=GS)
                                 ).then_inc(sh_in[u], 16)

                def store(j, q):
                    b_, g_ = j // GROUPS, j % GROUPS
                    sp.wait_ge(num_done, j * QUADS + q + 2)
                    sp.dma_start(ctx_rows[g_, :, bass.ds(b_ * SEQ + q * SEG, SEG)] if isinstance(j, int) else
                                 ctx_rows[bass.ds(g_, 1), :, bass.ds(b_ * SEQ + q * SEG, SEG)]
                                 .rearrange("o p n -> (o p) n"), num[:, q % 2]).then_inc(out_stored[q % 2], 16)

                load(0, 0)
                load(1, 1)
                load(2, 2)

                def run(jm, je, um, ue):
                    if je is not None:
                        for q in range(QUADS - 1):
                            store(je, q)
                    if jm is not None:
                        shift(jm, um)
                    if je is not None:
                        store(je, QUADS - 1)
                        if je + NB < NG:
                            load(je + NB, ue)

                for r in range(NG + 1):
                    run(r if r < NG else None, r - 1 if r else None, r % NB, (r - 1) % NB)
                for u in range(2):
                    sp.wait_ge(out_stored[u], 16 + 16 * NG * QUADS // 2)

            @block.tensor
            def _(pe):
                def masked(ps, at, tri, stop=True):
                    return pe.matmul(ps[:, at:at + P], ident_b[:], tri[:], start=False, stop=stop)

                def max_unit(j, u, n):
                    i, heads, t0, T = m_units[n]
                    if n == 0:
                        pe.wait_ge(mx_read, j * NM + 1)
                    elif n >= 2:
                        pe.wait_ge(mx_read, j * NM + n)
                    for x, m in enumerate(heads):
                        for c in range(0, T, SEG):
                            w = min(SEG, T - c)
                            ps = mx_ps[:, n % 2, x * SEG + c:x * SEG + c + w]
                            diagonal = t0 + c + w == (i + 1) * P
                            mm = pe.matmul(ps, qa[u][0:KROWS, m, i * P:(i + 1) * P], ka[u][0:KROWS, t0 + c:t0 + c + w],
                                           start=True, stop=not diagonal)
                            if diagonal:
                                mm = masked(ps, w - P, tri_st)
                    mm.then_inc(mx_filled, 1)

                def turn_max(j):
                    pe.wait_ge(row_max, j + 1)
                    pe.wait_ge(mx_read, j * NM + NM - 1)
                    pe.transpose(mx_ps[:, 0, 0:P], mrow[:], ident_f[:]).then_inc(mx_filled, 1)

                def scores(j, u, e):
                    q, t = steps[e // GS]
                    c0, m = cols(q, t), e % GS
                    pe.wait_ge(exp_done, j * NE + (e - 2 if e >= 3 else 0) + 1)
                    ps = st_ps[:, e % 3, c0:SEG]
                    diagonal = t >= q * SB_PER_QUAD
                    mm = pe.matmul(ps, ka[u][0:SROWS, t * P:(t + 1) * P], qa[u][0:SROWS, m, q * SEG + c0:(q + 1) * SEG],
                                   start=True, stop=not diagonal)
                    if diagonal:
                        mm = masked(ps, 0, tri_ts)
                    mm.then_inc(st_filled, 1)

                def values(j, u, n):
                    q, t = steps[n]
                    c0 = cols(q, t)
                    if t == 0:
                        pe.wait_ge(num_done, j * QUADS + q + 1)
                    pe.wait_ge(exp_done, j * NE + (n + 1) * GS + 1)
                    for m in range(GS):
                        mm = pe.matmul(acc_ps[32 * m:32 * m + 32, c0:SEG], va[u][:, t, :],
                                       prob[:, (n * GS + m) % PRING, c0:SEG], start=(t == 0),
                                       stop=(t == (q + 1) * SB_PER_QUAD - 1))
                    mm.then_inc(pv_done, 1)

                def run(jm, je, um, ue):
                    if jm is not None:
                        pe.wait_ge(loaded[um], LOADS * (jm // NB + 1) if isinstance(jm, int) else LOADS * ((jm + 0) // NB + 1))
                    if je is not None:
                        pe.wait_ge(sh_in[ue], 16 * (je // NB + 1))
                    for kind, n in order(jm, je):
                        if kind == "max":
                            max_unit(jm, um, n)
                        elif kind == "turn":
                            turn_max(jm)
                        elif kind == "scores":
                            scores(je, ue, n)
                        elif kind == "values":
                            values(je, ue, n)

                pe.sem_inc(pv_done, 2)
                pe.wait_ge(consts, 3)
                groups(pe.Fori, run)

            @block.scalar
            def _(act):
                act.sem_inc(exp_done, 1)
                act.sem_inc(num_done, 1)
                for u in range(2):
                    act.sem_inc(out_stored[u], 16)

                def exps(j, e):
                    c0 = cols(*steps[e // GS])
                    if e % GS == 0:
                        act.wait_ge(pv_done, j * NSTEP + e // GS + 1)
                    act.wait_ge(st_filled, j * NE + e + 1)
                    act.activation(prob[:, e % PRING, c0:SEG], st_ps[:, e % 3, c0:SEG], ACT.Exp,
                                   scale=HD ** -0.5).then_inc(exp_done, 1)

                def norm(j, q):
                    act.wait_ge(pv_done, j * NSTEP + (q + 1) * (q + 2) * SB_PER_QUAD // 2 + 2)
                    act.wait_ge(out_stored[q % 2], (j * (QUADS // 2) + q // 2) * 16 + 16)
                    act.activation(num[:, q % 2], acc_ps[:], ACT.Copy).then_inc(num_done, 1)

                def run(jm, je, um, ue):
                    if je is not None:
                        for kind, n in order(jm, je):
                            if kind == "scores":
                                exps(je, n)
                            elif kind == "norm":
                                norm(je, n)

                groups(act.Fori, run)

            @block.vector
            def _(dve):
                dve.sem_inc(mx_read, 1)
                for u in range(NB):
                    dve.memset(ka[u][KROWS:SROWS], 1.0)
                    dve.memset(va[u][:, :, HD:2 * HD], 1.0)
                dve.memset(mrow[:], 0.0)
                dve.memset(mx[:], -3.0e38).then_inc(consts, 3)

                def max_unit(j, n):
                    i, heads, t0, T = m_units[n]
                    dve.wait_ge(mx_filled, j * NM + n + 1)
                    if len(heads) == 2:
                        src = mx_ps[:, n % 2].rearrange("p (h n) -> p h n", n=SEG)[:, :, 0:T]
                    else:
                        src = mx_ps[:, n % 2:n % 2 + 1, 0:T]
                    dve.tensor_reduce(mx[:, heads[0]:heads[-1] + 1, i, int(t0 > 0)], src, AX.X, ALU.max).then_inc(mx_read, 1)

                def shift(j):
                    dve.wait_ge(mx_read, j * NM + NM)
                    dve.tensor_reduce(mrow[:, 0:GS * SBLK], mx[:].rearrange("p m i c -> p (m i) c"), AX.X, ALU.max).then_inc(row_max, 1)
                    dve.wait_ge(mx_filled, j * NM + NM)
                    if not (isinstance(j, int) and j == 0):
                        dve.wait_ge(sh_out, 16 * j)
                    t = mx_ps[0:GS * SBLK, 0, 0:P]
                    dve.tensor_scalar(sh[:, 0], t, -1.0, None, ALU.mult).then_inc(sh_hi, 1)
                    dve.wait_ge(sh_hi, j + 1)
                    dve.scalar_tensor_tensor(sh_rest[:], t, -1.0, sh[:, 0], ALU.mult, ALU.subtract).then_inc(mx_read, 1)
                    dve.wait_ge(mx_read, j * NM + NM + 1)
                    dve.tensor_copy(sh[:, 1], sh_rest[:]).then_inc(sh_mid, 1)
                    dve.wait_ge(sh_mid, j + 1)
                    dve.tensor_tensor(sh[:, 2], sh_rest[:], sh[:, 1], ALU.subtract).then_inc(sh_done, 1)

                def run(jm, je, um, ue):
                    for kind, n in order(jm, je):
                        if kind == "max":
                            max_unit(jm, n)
                        elif kind == "turn":
                            shift(jm)

                groups(dve.Fori, run)


NSEG = TOK // SEG
TPS = SEG // P
TILES = TOK // P
E = 8


def denominators_phase(nc, ctx_rows, inv_rows):
    with ExitStack() as ctx:
        s = Space(nc, ctx, "den")
        den = s.sb("den", [P, SEG])
        inv = s.sb("inv", [P, SEG])
        den_in, inv_done, inv_out = s.sem("den_in"), s.sem("inv_done"), s.sem("inv_out")
        with nc.Block() as block:
            @block.sync
            def _(sp):
                rows = TOK // SEG
                for h in range(HEADS):
                    r = 32 * (h % GS) + HD
                    sp.dma_start(den[h * rows:(h + 1) * rows], ctx_rows[h // GS, r].rearrange("(a n) -> a n", n=SEG)
                                 ).then_inc(den_in, 16)
                sp.wait_ge(inv_done, 1)
                sp.dma_start(inv_rows.rearrange("h (a n) -> (h a) n", n=SEG), inv[:]).then_inc(inv_out, 16)
                sp.wait_ge(inv_out, 16)

            @block.vector
            def _(dve):
                dve.wait_ge(den_in, 16 * HEADS)
                dve.reciprocal(inv[:], den[:]).then_inc(inv_done, 1)


def out_project_phase(nc, ctx_rows, inv_rows, x_rows, wo, wr, br_sb, ident_f, scores_sb, x1_rows):
    with ExitStack() as ctx:
        s = Space(nc, ctx, "wo")
        w_o = s.sb("w_o", [P, GROUPS, D])
        w_r = s.sb("w_r", [P, KD, E])
        num = [s.sb(f"num{u}", [P, GROUPS, SEG]) for u in range(2)]
        inv = [s.sb(f"inv{u}", [P, GROUPS, SEG]) for u in range(2)]
        cn = [s.sb(f"cn{u}", [P, GROUPS, SEG]) for u in range(2)]
        xr = [s.sb(f"xr{u}", [P, TPS, D]) for u in range(2)]
        y = s.sb("y", [P, 2, TPS, D])
        stats = s.sb("stats", [P, 2, TPS, 6])
        mv = s.sb("mv", [P, 2, TPS, 2])
        var = s.sb("var", [P, 2, TPS])
        std = s.sb("std", [P, 2, TPS])
        rstd = s.sb("rstd", [P, 2, TPS])
        rough, nr, nr2 = (s.sb(n, [P, 2, TPS]) for n in ("rough", "nr", "nr2"))
        st_seen, newton = s.sem("st_seen"), s.sem("newton")
        x1 = s.sb("x1", [P, 2, TPS, D])
        x1T = s.sb("x1T", [P, 2, KD, SEG])
        y_ps = s.ps("y_ps", [P, 2, SEG])
        t_ps = s.ps("t_ps", [P, KD, SEG])
        r_ps = s.ps("r_ps", [P, 2, SEG])
        w_in, seg_in, seg_free = s.sem("w_in"), [s.sem("seg_in0"), s.sem("seg_in1")], s.sem("seg_free")
        cn_done, y_done, sum_done, st_done, mv_done, var_done, std_done, rstd_done, x1_done = (
            s.sem(n) for n in ("cn", "y", "sum", "st", "mv", "var", "std", "rstd", "x1"))
        t_done, xT_done, r_done, r_read = (s.sem(n) for n in ("t", "xT", "r", "r_read"))
        stored = [s.sem("stored0"), s.sem("stored1")]

        with nc.Block() as block:
            @block.sync
            def _(sp):
                def load(n, u):
                    sp.dma_start(num[u][:], ctx_rows[:, :, bass.ds(n * SEG, SEG)].rearrange("g p n -> p g n")
                                 ).then_inc(seg_in[u], 16)
                    for m in range(GS):
                        sp.dma_start(inv[u][32 * m:32 * m + 32],
                                     inv_rows.rearrange("(g m) n -> m g n", m=GS)[m:m + 1, :, bass.ds(n * SEG, SEG)]
                                     .broadcast_to([32, GROUPS, SEG])).then_inc(seg_in[u], 16)
                    sp.dma_start(xr[u][:], x_rows[bass.ds(n * SEG, SEG)].rearrange("(a p) d -> p a d", p=P)
                                 ).then_inc(seg_in[u], 16)

                def store(n, u):
                    sp.wait_ge(x1_done, (n + 1) * TPS)
                    sp.dma_start(x1_rows[bass.ds(n * SEG, SEG)].rearrange("(a p) d -> p a d", p=P), x1[:, u]
                                 ).then_inc(stored[u], 16)

                sp.dma_start(w_o[:], wo.rearrange("g p n -> p g n")).then_inc(w_in, 16)
                sp.dma_start(w_r[:], wr.rearrange("(k p) e -> p k e", p=P)).then_inc(w_in, 16)
                load(0, 0)
                load(1, 1)
                with sp.Fori(0, NSEG // 2 - 1) as i:
                    for u in range(2):
                        sp.wait_ge(sum_done, i * 2 + u + 1)
                        load(i * 2 + u + 2, u)
                        store(i * 2 + u, u)
                for u in range(2):
                    store(NSEG - 2 + u, u)
                for u in range(2):
                    sp.wait_ge(stored[u], 16 * NSEG // 2)

            @block.vector
            def _(dve):
                def scale(n, u, i):
                    dve.wait_ge(seg_in[u], i * 96 + 96)
                    dve.tensor_tensor(cn[u][:], num[u][:], inv[u][:], ALU.mult).then_inc(cn_done, 1)

                def norm(n, u, i):
                    dve.wait_ge(y_done, n + 1)
                    dve.tensor_tensor(y[:, u], y_ps[:].rearrange("p c (a d) -> p (c a) d", d=D), xr[u][:], ALU.add
                                      ).then_inc(sum_done, 1)
                    dve.wait_ge(sum_done, n + 1)
                    for a in range(TPS):
                        dve.bn_stats(stats[:, u, a], y[:, u, a]).then_inc(st_done, 1)
                    dve.wait_ge(st_done, n * TPS + TPS)
                    dve.sem_inc(st_seen, 1)
                    for a in range(TPS):
                        dve.bn_aggr(mv[:, u, a], stats[:, u, a]).then_inc(mv_done, 1)
                    dve.wait_ge(mv_done, n * TPS + TPS)
                    dve.tensor_scalar(var[:, u], mv[:, u, :, 1], EPS, None, ALU.add).then_inc(var_done, 1)
                    dve.wait_ge(std_done, n + 1)
                    dve.reciprocal(rough[:, u], std[:, u]).then_inc(newton, 1)
                    dve.wait_ge(newton, n * 4 + 1)
                    dve.tensor_tensor(nr[:, u], var[:, u], rough[:, u], ALU.mult).then_inc(newton, 1)
                    dve.wait_ge(newton, n * 4 + 2)
                    dve.tensor_tensor(nr2[:, u], nr[:, u], rough[:, u], ALU.mult).then_inc(newton, 1)
                    dve.wait_ge(newton, n * 4 + 3)
                    dve.tensor_scalar(nr[:, u], nr2[:, u], -0.5, 1.5, ALU.mult, ALU.add).then_inc(newton, 1)
                    dve.wait_ge(newton, n * 4 + 4)
                    dve.tensor_tensor(rstd[:, u], rough[:, u], nr[:, u], ALU.mult).then_inc(rstd_done, 1)
                    dve.wait_ge(rstd_done, n + 1)
                    for a in range(TPS):
                        dve.tensor_scalar(x1[:, u, a], y[:, u, a], mv[:, u, a, 0:1], rstd[:, u, a:a + 1],
                                          ALU.subtract, ALU.mult).then_inc(x1_done, 1)

                def route(n, u):
                    dve.wait_ge(r_done, n + 1)
                    dve.tensor_tensor(scores_sb[:, bass.ds(n * TPS, TPS), :],
                                      r_ps[:, u, 0:TPS * E].rearrange("p (a e) -> p a e", e=E),
                                      br_sb[:], ALU.add).then_inc(r_read, 1)

                scale(0, 0, 0)
                scale(1, 1, 0)
                norm(0, 0, 0)
                norm(1, 1, 0)
                with dve.Fori(1, NSEG // 2) as i:
                    for u in range(2):
                        scale(i * 2 + u, u, i)
                        route(i * 2 + u - 2, u)
                        dve.wait_ge(stored[u], i * 16)
                        norm(i * 2 + u, u, i)
                for u in range(2):
                    route(NSEG - 2 + u, u)

            @block.tensor
            def _(pe):
                def out(n, u):
                    pe.wait_ge(cn_done, n + 1)
                    for a in range(TPS):
                        for g in range(GROUPS):
                            mm = pe.matmul(y_ps[:, a // 2, (a % 2) * D:(a % 2 + 1) * D], cn[u][:, g, a * P:(a + 1) * P],
                                           w_o[:, g], start=(g == 0), stop=(g == GROUPS - 1))
                    mm.then_inc(y_done, 1)

                def turn(n, u):
                    pe.wait_ge(x1_done, n * TPS + TPS)
                    for k in range(KD):
                        for a in range(TPS):
                            mm = pe.transpose(t_ps[:, k, a * P:(a + 1) * P], x1[:, u, a, k * P:(k + 1) * P], ident_f[:])
                    mm.then_inc(t_done, 1)

                def route(n, u):
                    pe.wait_ge(xT_done, n + 1)
                    for a in range(TPS):
                        for k in range(KD):
                            mm = pe.matmul(r_ps[:, u, a * E:(a + 1) * E], x1T[:, u, k, a * P:(a + 1) * P], w_r[:, k],
                                           start=(k == 0), stop=(k == KD - 1))
                    mm.then_inc(r_done, 1)

                pe.wait_ge(w_in, 32)
                out(0, 0)
                with pe.Fori(0, NSEG // 2 - 1) as i:
                    for u in range(2):
                        n = i * 2 + u
                        pe.wait_ge(sum_done, n + 1)
                        out(n + 1, 1 - u)
                        turn(n, u)
                        route(n, u)
                pe.wait_ge(sum_done, NSEG - 1)
                out(NSEG - 1, 1)
                for u in range(2):
                    turn(NSEG - 2 + u, u)
                    route(NSEG - 2 + u, u)

            @block.scalar
            def _(act):
                with act.Fori(0, NSEG // 2) as i:
                    for u in range(2):
                        n = i * 2 + u
                        act.wait_ge(var_done, n + 1)
                        act.activation(std[:, u], var[:, u], ACT.Sqrt).then_inc(std_done, 1)
                        act.wait_ge(t_done, n + 1)
                        act.activation(x1T[:, u], t_ps[:], ACT.Copy).then_inc(xT_done, 1)


def routing_phase(nc, scores_sb, pos_sb, owner_sb, ident_b, before, ones_b, slots_iota, ranks, n_slots):
    with ExitStack() as ctx:
        s = Space(nc, ctx, "route")
        best = s.sb("best", [P, TILES])
        hit = s.sb("hit", [P, TILES, E])
        first = s.sb("first", [P, TILES])
        chosen = s.sb("chosen", [P, TILES, E])
        chosen_b = s.sb("chosen_b", [P, TILES, E], BF16)
        total = s.sb("total", [P, TILES, E])
        upto = s.sb("upto", [P, TILES, E])
        one = s.sb("one", [P, TILES])
        cnt = s.sb("cnt", [P, E], I32)
        cnt2 = s.sb("cnt2", [P, E], I32)
        tiles = s.sb("tiles", [P, E])
        end = s.sb("end", [P, E])
        start = s.sb("start", [P, E])
        row = s.sb("row", [P, TILES, E])
        posf = s.sb("posf", [P, TILES])
        own = [s.sb(f"own{i}", [1, n_slots]) for i in range(2)]
        before_ps = s.ps("before_ps", [P, SEG])
        total_ps = s.ps("total_ps", [P, SEG])
        chain, counted, chosen_done = s.sem("chain"), s.sem("counted"), s.sem("chosen")

        with nc.Block() as block:
            @block.tensor
            def _(pe):
                pe.wait_ge(chosen_done, 1)
                c = chosen_b[:].rearrange("p t e -> p (t e)")
                pe.matmul(before_ps[:, 0:TILES * E], before[:], c, start=True, stop=True).then_inc(counted, 1)
                pe.matmul(total_ps[:, 0:TILES * E], ones_b[:], c, start=True, stop=True).then_inc(counted, 1)

            @block.vector
            def _(dve):
                n = [0]

                def then(ins):
                    n[0] += 1
                    ins.then_inc(chain, 1)
                    dve.wait_ge(chain, n[0])

                def over_e(ap):
                    return ap.unsqueeze(2).broadcast_to([P, TILES, E])

                then(dve.tensor_reduce(best[:], scores_sb[:], AX.X, ALU.max))
                then(dve.tensor_tensor(hit[:], scores_sb[:], over_e(best[:]), ALU.is_ge))
                then(dve.tensor_tensor(hit[:], hit[:], ranks[:].unsqueeze(1).broadcast_to([P, TILES, E]), ALU.mult))
                then(dve.tensor_reduce(first[:], hit[:], AX.X, ALU.max))
                then(dve.tensor_tensor(chosen[:], hit[:], over_e(first[:]), ALU.is_equal))
                dve.tensor_copy(chosen_b[:], chosen[:]).then_inc(chosen_done, 1)
                then(dve.memset(one[:], 1.0))
                dve.wait_ge(counted, 2)
                then(dve.tensor_copy(total[:].rearrange("p t e -> p (t e)"), total_ps[:, 0:TILES * E]))
                for e in range(E):
                    i = dve.tensor_tensor_scan(upto[:, :, e], one[:], total[:, :, e], 0.0, ALU.mult, ALU.add)
                then(i)
                then(dve.tensor_scalar(cnt[:], upto[:, TILES - 1, :], float(P - 1), None, ALU.add))
                then(dve.tensor_scalar(cnt2[:], cnt[:], 7, None, ALU.logical_shift_right))
                then(dve.tensor_copy(tiles[:], cnt2[:]))
                then(dve.tensor_tensor_scan(end[:], one[:, 0:E], tiles[:], 0.0, ALU.mult, ALU.add))
                then(dve.tensor_tensor(start[:], end[:], tiles[:], ALU.subtract))
                then(dve.tensor_scalar(start[:], start[:], float(P), None, ALU.mult))
                then(dve.tensor_tensor(row[:], upto[:], total[:], ALU.subtract))
                then(dve.tensor_tensor(row[:], row[:], start[:].unsqueeze(1).broadcast_to([P, TILES, E]), ALU.add))
                then(dve.tensor_tensor(row[:].rearrange("p t e -> p (t e)"), row[:].rearrange("p t e -> p (t e)"),
                                       before_ps[:, 0:TILES * E], ALU.add))
                then(dve.tensor_tensor(row[:], row[:], chosen[:], ALU.mult))
                then(dve.tensor_reduce(posf[:], row[:], AX.X, ALU.add))
                then(dve.tensor_copy(pos_sb[:], posf[:]))
                then(dve.tensor_scalar(own[0][:], slots_iota[:], end[0:1, 0:1], None, ALU.is_ge))
                for e in range(1, E):
                    then(dve.scalar_tensor_tensor(own[e % 2][:], slots_iota[:], end[0:1, e:e + 1], own[(e - 1) % 2][:],
                                                  ALU.is_ge, ALU.add))
                then(dve.tensor_scalar(own[0][:], own[1][:], float(E - 1), None, ALU.min))
                then(dve.tensor_copy(owner_sb[:], own[0][:]))


F = 1024
FK = F // P


def scatter_phase(nc, x1_rows, pos_sb, sorted_rows, sorted_zeroed, zeroed_value):
    with ExitStack() as ctx:
        s = Space(nc, ctx, "scat")
        x1 = s.sb("x1", [P, TILES, D])
        x_in, placed = s.sem("x_in"), s.sem("placed")
        with nc.Block() as block:
            @block.sync
            def _(sp):
                sp.dma_start(x1[:], x1_rows.rearrange("(t p) d -> p t d", p=P)).then_inc(x_in, 16)

            @block.gpsimd
            def _(pool):
                pool.wait_ge(x_in, 16)
                pool.wait_ge(sorted_zeroed, zeroed_value)
                for t in range(TILES):
                    pool.indirect_dma_start(sorted_rows, bass.IndirectOffsetOnAxis(pos_sb[:, t:t + 1], 0),
                                            x1[:, t], None).then_inc(placed, 16)
                pool.wait_ge(placed, 16 * TILES)


def experts_phase(nc, n_slots, sorted_rows, done_rows, owner_sb, w1, w2, b1, b2, weights_in, weights_value, ident_f):
    with ExitStack() as ctx:
        s = Space(nc, ctx, "moe")
        x = s.sb("x", [P, 2, D])
        xT = s.sb("xT", [P, 2, KD, P])
        hb = s.sb("hb", [P, 2, F])
        h = s.sb("h", [P, 2, F])
        hT = s.sb("hT", [P, 2, FK, P])
        y = s.sb("y", [P, 2, D])
        x_ps = s.ps("x_ps", [P, SEG])
        h_ps = s.ps("h_ps", [P, 2, F])
        hT_ps = s.ps("hT_ps", [P, 2, SEG])
        y_ps = s.ps("y_ps", [P, SEG])
        x_in = [s.sem("x_in0"), s.sem("x_in1")]
        x_turned, xT_done, up_done, bias_done, h_done, h_turned, hT_lo, hT_hi, down_done, y_done = (
            s.sem(n) for n in ("x_turned", "xT", "up", "bias", "h", "h_turned", "hT_lo", "hT_hi", "down", "y"))
        y_out = [s.sem("y_out0"), s.sem("y_out1")]
        N = n_slots
        assert N % 2 == 0

        with nc.Block() as block:
            @block.sync
            def _(sp):
                def load(row, u):
                    sp.dma_start(x[:, u], sorted_rows[bass.ds(row, P)]).then_inc(x_in[u], 16)

                def store(j, row, u):
                    sp.wait_ge(y_done, j + 2)
                    sp.dma_start(done_rows[bass.ds(row, P)], y[:, u]).then_inc(y_out[u], 16)

                load(0, 0)
                load(P, 1)
                with sp.Fori(0, N // 2 - 1) as i:
                    for u in range(2):
                        row, row2 = sp.snap(i * 2 * P + u * P), sp.snap(i * 2 * P + (u + 2) * P)
                        sp.wait_ge(x_turned, i * 2 + u + 1)
                        load(row2, u)
                        store(i * 2 + u, row, u)
                for u in range(2):
                    store(N - 2 + u, (N - 2 + u) * P, u)
                for u in range(2):
                    sp.wait_ge(y_out[u], 16 + 16 * N // 2)

            @block.tensor
            def _(pe):
                def turn_x(j, u, i):
                    pe.wait_ge(x_in[u], i * 16 + 16)
                    for k in range(KD):
                        mm = pe.transpose(x_ps[:, k * P:(k + 1) * P], x[:, u, k * P:(k + 1) * P], ident_f[:])
                    mm.then_inc(x_turned, 1)

                def up(j, u):
                    e = pe.value_load(owner_sb[0:1, bass.ds(j, 1)], min_val=0, max_val=E - 1)
                    pe.wait_ge(xT_done, j + 1)
                    for c in range(F // SEG):
                        for k in range(KD):
                            mm = pe.matmul(h_ps[:, u, c * SEG:(c + 1) * SEG], xT[:, u, k],
                                           w1[:, bass.ds(e * KD + k, 1), c * SEG:(c + 1) * SEG].rearrange("p o n -> p (o n)"),
                                           start=(k == 0), stop=(k == KD - 1))
                    mm.then_inc(up_done, 1)

                def turn_h(j, u):
                    pe.wait_ge(h_done, j + 1)
                    for c in range(FK):
                        mm = pe.transpose(hT_ps[:, c // 4, (c % 4) * P:(c % 4 + 1) * P], h[:, u, c * P:(c + 1) * P], ident_f[:])
                        if c % 4 == 3:
                            mm.then_inc(h_turned, 1)

                def down(j, u):
                    e = pe.value_load(owner_sb[0:1, bass.ds(j, 1)], min_val=0, max_val=E - 1)
                    pe.wait_ge(y_done, j + 1)
                    for c in range(FK):
                        if c % 4 == 0:
                            pe.wait_ge(hT_hi if c else hT_lo, j + 1)
                        mm = pe.matmul(y_ps[:, 0:D], hT[:, u, c],
                                       w2[:, bass.ds(e * FK + c, 1), :].rearrange("p o n -> p (o n)"),
                                       start=(c == 0), stop=(c == FK - 1))
                    mm.then_inc(down_done, 1)

                def cycle(j, u, i, up_next, turn_next):
                    turn_h(j, u)
                    if up_next:
                        up(j + 1, 1 - u)
                    if turn_next:
                        turn_x(j + 2, u, i + 1)
                    down(j, u)

                pe.wait_ge(weights_in, weights_value)
                turn_x(0, 0, 0)
                up(0, 0)
                turn_x(1, 1, 0)
                with pe.Fori(0, N // 2 - 1) as i:
                    for u in range(2):
                        cycle(i * 2 + u, u, i, True, True)
                cycle(N - 2, 0, 0, True, False)
                cycle(N - 1, 1, 0, False, False)

            @block.scalar
            def _(act):
                def copy_x(j, u):
                    act.wait_ge(x_turned, j + 1)
                    act.activation(xT[:, u].rearrange("p k n -> p (k n)"), x_ps[:, 0:KD * P], ACT.Copy).then_inc(xT_done, 1)

                def copy_h(j, u):
                    act.wait_ge(h_turned, j * 2 + 1)
                    act.activation(hT[:, u, 0:4].rearrange("p c n -> p (c n)"), hT_ps[:, 0], ACT.Copy).then_inc(hT_lo, 1)

                def gelu(j, u):
                    act.wait_ge(bias_done, j + 1)
                    act.activation(h[:, u], hb[:, u], ACT.Gelu).then_inc(h_done, 1)

                copy_x(0, 0)
                copy_x(1, 1)
                gelu(0, 0)
                with act.Fori(0, N // 2 - 1) as i:
                    for u in range(2):
                        j = i * 2 + u
                        copy_h(j, u)
                        copy_x(j + 2, u)
                        gelu(j + 1, 1 - u)
                copy_h(N - 2, 0)
                gelu(N - 1, 1)
                copy_h(N - 1, 1)

            @block.vector
            def _(dve):
                def bias(j, u):
                    e = dve.value_load(owner_sb[0:1, bass.ds(j, 1)], min_val=0, max_val=E - 1)
                    dve.wait_ge(up_done, j + 1)
                    dve.tensor_tensor(hb[:, u], h_ps[:, u], b1[:, bass.ds(e, 1), :].rearrange("p o n -> p (o n)"), ALU.add
                                      ).then_inc(bias_done, 1)

                def copy_h(j, u):
                    dve.wait_ge(h_turned, j * 2 + 2)
                    dve.tensor_copy(hT[:, u, 4:8].rearrange("p c n -> p (c n)"), hT_ps[:, 1]).then_inc(hT_hi, 1)

                def out(j, u, i):
                    e = dve.value_load(owner_sb[0:1, bass.ds(j, 1)], min_val=0, max_val=E - 1)
                    dve.wait_ge(down_done, j + 1)
                    dve.wait_ge(y_out[u], i * 16 + 16)
                    dve.tensor_tensor(y[:, u], y_ps[:, 0:D], b2[:, bass.ds(e, 1), :].rearrange("p o n -> p (o n)"), ALU.add
                                      ).then_inc(y_done, 1)

                dve.sem_inc(y_done, 1)
                for u in range(2):
                    dve.sem_inc(y_out[u], 16)
                dve.wait_ge(weights_in, weights_value)
                bias(0, 0)
                with dve.Fori(0, N // 2 - 1) as i:
                    for u in range(2):
                        j = i * 2 + u
                        copy_h(j, u)
                        bias(j + 1, 1 - u)
                        out(j, u, i)
                copy_h(N - 2, 0)
                bias(N - 1, 1)
                out(N - 2, 0, N // 2 - 1)
                copy_h(N - 1, 1)
                out(N - 1, 1, N // 2 - 1)


def layernorm_buffers(s, width):
    b = {"stats": s.sb("ln_stats", [P, 2, width, 6]), "mv": s.sb("ln_mv", [P, 2, width, 2])}
    for n in ("var", "std", "rough", "nr", "nr2", "rstd"):
        b[n] = s.sb(f"ln_{n}", [P, 2, width])
    for n in ("st_done", "st_seen", "mv_done", "var_done", "std_done", "newton", "rstd_done", "out_done"):
        b[n] = s.sem(f"ln_{n}")
    return b


def layernorm(dve, b, n, u, y, out, width):
    layernorm_stats(dve, b, n, u, y, width)
    layernorm_apply(dve, b, n, u, y, out, width)


def layernorm_stats(dve, b, n, u, y, width):
    for a in range(width):
        dve.bn_stats(b["stats"][:, u, a], y[:, a]).then_inc(b["st_done"], 1)
    dve.wait_ge(b["st_done"], n * width + width)
    dve.sem_inc(b["st_seen"], 1)
    for a in range(width):
        dve.bn_aggr(b["mv"][:, u, a], b["stats"][:, u, a]).then_inc(b["mv_done"], 1)
    dve.wait_ge(b["mv_done"], n * width + width)
    dve.tensor_scalar(b["var"][:, u], b["mv"][:, u, :, 1], EPS, None, ALU.add).then_inc(b["var_done"], 1)


def layernorm_apply(dve, b, n, u, y, out, width):
    var, rough, nr, nr2, rstd = (b[x][:, u] for x in ("var", "rough", "nr", "nr2", "rstd"))
    dve.wait_ge(b["std_done"], n + 1)
    dve.reciprocal(rough, b["std"][:, u]).then_inc(b["newton"], 1)
    dve.wait_ge(b["newton"], n * 4 + 1)
    dve.tensor_tensor(nr, var, rough, ALU.mult).then_inc(b["newton"], 1)
    dve.wait_ge(b["newton"], n * 4 + 2)
    dve.tensor_tensor(nr2, nr, rough, ALU.mult).then_inc(b["newton"], 1)
    dve.wait_ge(b["newton"], n * 4 + 3)
    dve.tensor_scalar(nr, nr2, -0.5, 1.5, ALU.mult, ALU.add).then_inc(b["newton"], 1)
    dve.wait_ge(b["newton"], n * 4 + 4)
    dve.tensor_tensor(rstd, rough, nr, ALU.mult).then_inc(b["rstd_done"], 1)
    dve.wait_ge(b["rstd_done"], n + 1)
    for a in range(width):
        dve.tensor_scalar(out[:, a], y[:, a], b["mv"][:, u, a, 0:1], b["rstd"][:, u, a:a + 1],
                          ALU.subtract, ALU.mult).then_inc(b["out_done"], 1)


def layernorm_root(act, b, n, u):
    act.wait_ge(b["var_done"], n + 1)
    act.activation(b["std"][:, u], b["var"][:, u], ACT.Sqrt).then_inc(b["std_done"], 1)


def combine_phase(nc, x1_rows, done_rows, pos_sb, ident_f, x2_rows, x2T_rows):
    with ExitStack() as ctx:
        s = Space(nc, ctx, "comb")
        y = s.sb("y", [P, 2, TPS, D])
        x1 = s.sb("x1", [P, 2, TPS, D])
        sm = s.sb("sm", [P, 2, TPS, D])
        x2 = s.sb("x2", [P, 2, TPS, D])
        x2T = s.sb("x2T", [P, 2, KD, SEG])
        ln = layernorm_buffers(s, TPS)
        t_ps = s.ps("t_ps", [P, 2, KD, SEG])
        y_in, x_in = [s.sem("y_in0"), s.sem("y_in1")], [s.sem("x_in0"), s.sem("x_in1")]
        sum_done, turned, copied = s.sem("sum_done"), s.sem("turned"), s.sem("copied")
        stored = [s.sem("stored0"), s.sem("stored1")]
        with nc.Block() as block:
            @block.gpsimd
            def _(pool):
                for n in range(NSEG):
                    u = n % 2
                    if n >= 2:
                        pool.wait_ge(sum_done, n - 1)
                    for a in range(TPS):
                        t = n * TPS + a
                        pool.indirect_dma_start(y[:, u, a], None, done_rows,
                                                bass.IndirectOffsetOnAxis(pos_sb[:, t:t + 1], 0)).then_inc(y_in[u], 16)

            @block.sync
            def _(sp):
                def load(n, u):
                    sp.dma_start(x1[:, u], x1_rows[bass.ds(n * SEG, SEG)].rearrange("(a p) d -> p a d", p=P)
                                 ).then_inc(x_in[u], 16)

                def store(n, u):
                    sp.wait_ge(copied, n + 1)
                    sp.dma_start(x2_rows[bass.ds(n * SEG, SEG)].rearrange("(a p) d -> p a d", p=P), x2[:, u]
                                 ).then_inc(stored[u], 16)
                    sp.dma_start(x2T_rows.rearrange("(k p) n -> p k n", p=P)[:, :, bass.ds(n * SEG, SEG)], x2T[:, u]
                                 ).then_inc(stored[u], 16)

                load(0, 0)
                load(1, 1)
                with sp.Fori(0, NSEG // 2 - 1) as i:
                    for u in range(2):
                        sp.wait_ge(sum_done, i * 2 + u + 1)
                        load(i * 2 + u + 2, u)
                        store(i * 2 + u, u)
                for u in range(2):
                    store(NSEG - 2 + u, u)
                for u in range(2):
                    sp.wait_ge(stored[u], 32 * NSEG // 2)

            @block.vector
            def _(dve):
                def norm(n, u, i):
                    dve.wait_ge(y_in[u], (i + 1) * 16 * TPS)
                    dve.wait_ge(x_in[u], (i + 1) * 16)
                    dve.tensor_tensor(sm[:, u], y[:, u], x1[:, u], ALU.add).then_inc(sum_done, 1)
                    dve.wait_ge(sum_done, n + 1)
                    layernorm(dve, ln, n, u, sm[:, u], x2[:, u], TPS)

                for u in range(2):
                    norm(u, u, 0)
                with dve.Fori(1, NSEG // 2) as i:
                    for u in range(2):
                        dve.wait_ge(stored[u], i * 32)
                        norm(i * 2 + u, u, i)

            @block.tensor
            def _(pe):
                def turn(n, u):
                    pe.wait_ge(ln["out_done"], n * TPS + TPS)
                    for k in range(KD):
                        for a in range(TPS):
                            mm = pe.transpose(t_ps[:, u, k, a * P:(a + 1) * P], x2[:, u, a, k * P:(k + 1) * P], ident_f[:])
                    mm.then_inc(turned, 1)

                for u in range(2):
                    turn(u, u)
                with pe.Fori(1, NSEG // 2) as i:
                    for u in range(2):
                        pe.wait_ge(copied, i * 2 + u - 1)
                        turn(i * 2 + u, u)

            @block.scalar
            def _(act):
                def step(n, u):
                    layernorm_root(act, ln, n, u)
                    act.wait_ge(turned, n + 1)
                    act.activation(x2T[:, u], t_ps[:, u], ACT.Copy).then_inc(copied, 1)

                for u in range(2):
                    step(u, u)
                with act.Fori(1, NSEG // 2) as i:
                    for u in range(2):
                        act.wait_ge(stored[u], i * 32)
                        step(i * 2 + u, u)


DI, DS, DR, DC = 512, 16, 16, 4
CH = DI // P
UNITS = DS * CH
RING = 8
HRING = 4
BRING = 4
BCROWS = 2 * DS


def mamba_phase(nc, x2_rows, x2T_rows, x3_rows, w_in_d, conv_w_d, conv_b_d, w_x_d, w_dt_d, b_dt_d, a_log_d, d_d,
                w_out_d, keep_d, sel_d, ident_f):
    AT = {
        "PE": [(1, "X", 0), (3, "X", 1), (5, "X", 2), (7, "X", 3), (9, "Z", 0), (11, "Z", 1), (13, "Z", 2), (15, "Z", 3),
               (21, "P", 0), (26, "T", 0), (28, "T", 1), (30, "T", 2), (32, "T", 3), (48, "O", 0), (51, "O", 1)],
        "ACT": [(10, "X", 0), (12, "X", 1), (14, "X", 2), (16, "X", 3), (18, "Z", 0), (20, "Z", 1), (22, "Z", 2),
                (24, "Z", 3), (27, "silu", 0), (31, "P", 0), (36, "T", 0), (38, "T", 1), (40, "T", 2), (42, "T", 3),
                (44, "exp", 0), (47, "ln", 0), (61, "root", 0)],
        "DVE": [(11, "conv", 0), (13, "conv", 1), (15, "conv", 2), (24, "P", 0), (42, "soft", 0), (44, "soft", 1),
                (46, "soft", 2), (50, "O", 0), (53, "O", 1), (54, "LN", 0), (57, "LN", 1)],
        "Pool": [(10, "yz", 0), (11, "yz", 1), (12, "yz", 2), (13, "yz", 3), (57, "u", 0), (58, "u", 1), (59, "u", 2),
                 (60, "u", 3)],
    }
    BEHIND = ("O", "LN", "root", "yz")

    with ExitStack() as ctx:
        s = Space(nc, ctx, "ssm")
        w_in = s.sb("w_in", [P, KD, 2 * DI])
        conv_w = s.sb("conv_w", [P, CH, DC])
        conv_b = s.sb("conv_b", [P, CH])
        w_x = s.sb("w_x", [P, CH, BCROWS + DR])
        w_dt = s.sb("w_dt", [BCROWS + DR, DI])
        b_dt = s.sb("b_dt", [P, CH])
        a_log = s.sb("a_log", [P, CH, DS])
        a_exp = s.sb("a_exp", [P, CH, DS])
        a_neg = s.sb("a_neg", [P, CH, DS])
        d_par = s.sb("d_par", [P, CH])
        w_out = s.sb("w_out", [P, CH, D])
        keep = s.sb("keep", [P, NSEG])
        sel = s.sb("sel", [3 * BCROWS, BCROWS, P], BF16)
        xT = s.sb("xT", [P, KD, SEG])
        x2 = s.sb("x2", [P, TPS, D])
        xb = s.sb("xb", [P, CH, DC - 1 + SEG])
        xc = [s.sb(f"xc{v}", [P, CH, SEG]) for v in range(2)]
        sz = [s.sb(f"sz{v}", [P, CH, SEG]) for v in range(2)]
        delta = [s.sb(f"delta{v}", [P, CH, SEG]) for v in range(2)]
        du = [s.sb(f"du{v}", [P, CH, SEG]) for v in range(2)]
        bc = [s.sb(f"bc{v}", [3 * BCROWS, SEG], BF16) for v in range(2)]
        bc_rest = s.sb("bc_rest", [BCROWS, SEG])
        bc_mid = s.sb("bc_mid", [BCROWS, SEG], BF16)
        d_raw = s.sb("d_raw", [BCROWS + DR, SEG])
        pre = s.sb("pre", [P, CH, SEG])
        ex = s.sb("ex", [P, CH, SEG])
        decay = s.sb("decay", [P, RING, SEG])
        drive = s.sb("drive", [P, RING, SEG])
        h = s.sb("h", [P, RING, SEG])
        hc = s.sb("hc", [P, HRING, SEG])
        b_sb = s.sb("b_sb", [P, BRING, SEG])
        carry = s.sb("carry", [P, UNITS])
        yt = s.sb("yt", [P, CH, SEG])
        sm = s.sb("sm", [P, TPS, D])
        ln = layernorm_buffers(s, TPS)
        f_ps = s.ps("f_ps", [P, SEG])
        b_ps = s.ps("b_ps", [P, SEG])
        c_ps = s.ps("c_ps", [P, 2, SEG])
        y_ps = s.ps("y_ps", [P, CH, SEG])

        weights, ready = s.sem("weights"), s.sem("ready")
        xT_in, x2_in, stored = s.sem("xT_in"), s.sem("x2_in"), s.sem("stored")
        (x_filled, x_copied, halo_done, conv_done, z_filled, z_copied, silu_done, p_filled, hi_done, rest_done,
         mid_done, lo_done, raw_done, t_filled, pre_done, abs_done, exp_done, one_done, ln_done, soft_done,
         u_done, o_filled, sum_done) = (s.sem(n) for n in (
             "x_filled", "x_copied", "halo", "conv", "z_filled", "z_copied", "silu", "p_filled", "hi", "rest", "mid",
             "lo", "raw", "t_filled", "pre", "abs", "exp", "one", "ln_one", "soft", "u", "o_filled", "sum"))
        (b_filled, c_filled, b_copied, decay_done, drive_done, scan_done, hc_done, add_done, carry_done, skip_done,
         yz_done) = (s.sem(n) for n in ("b_filled", "c_filled", "b_copied", "decay", "drive", "scan", "hc", "add", "carry",
                                        "skip", "yz"))

        def bodies(loop, body, engine):
            for _, *x in AT[engine]:
                if x[0] not in BEHIND:
                    body.ahead(x, 0, 0)
            body.start()
            segment(body, engine, 0, 0, False, True)
            with loop(0, NSEG // 2 - 1) as r:
                segment(body, engine, r * 2 + 1, 1, True, True)
                segment(body, engine, r * 2 + 2, 0, True, True)
            segment(body, engine, NSEG - 1, 1, True, False)
            for _, *x in AT[engine]:
                if x[0] in BEHIND:
                    body.behind(x, NSEG - 1, 1)

        def segment(body, engine, n, v, behind, ahead):
            for k in range(UNITS):
                body.unit(n, v, k, ahead)
                for at, *x in AT[engine]:
                    if at == k and x[0] in BEHIND and behind:
                        body.behind(x, n - 1, 1 - v)
                    if at == k and x[0] not in BEHIND and ahead:
                        body.ahead(x, n + 1, 1 - v)
            body.finish(n, v)

        class Nothing:
            def start(self): pass
            def unit(self, n, v, k, more): pass
            def ahead(self, x, n, v): pass
            def behind(self, x, n, v): pass
            def finish(self, n, v): pass

        with nc.Block() as block:
            @block.sync
            def _(sp):
                for t, d in ((w_in[:], w_in_d.rearrange("(k p) n -> p k n", p=P)),
                             (conv_w[:], conv_w_d.rearrange("(c p) k -> p c k", p=P)),
                             (conv_b[:], conv_b_d),
                             (w_x[:], w_x_d.rearrange("(c p) n -> p c n", p=P)),
                             (w_dt[BCROWS:BCROWS + DR], w_dt_d),
                             (b_dt[:], b_dt_d),
                             (a_log[:], a_log_d.rearrange("(c p) s -> p c s", p=P)),
                             (d_par[:], d_d),
                             (w_out[:], w_out_d.rearrange("(c p) n -> p c n", p=P)),
                             (keep[:], keep_d), (sel[:], sel_d)):
                    sp.dma_start(t, d).then_inc(weights, 16)

                def load_xT(n):
                    sp.dma_start(xT[:], x2T_rows.rearrange("(k p) n -> p k n", p=P)[:, :, bass.ds(n * SEG, SEG)]
                                 ).then_inc(xT_in, 16)

                def load_x2(n):
                    sp.dma_start(x2[:], x2_rows[bass.ds(n * SEG, SEG)].rearrange("(a p) d -> p a d", p=P)
                                 ).then_inc(x2_in, 16)

                def store(n):
                    sp.wait_ge(ln["out_done"], n * TPS + TPS)
                    sp.dma_start(x3_rows[bass.ds(n * SEG, SEG)].rearrange("(a p) d -> p a d", p=P), sm[:]
                                 ).then_inc(stored, 16)

                sp.sem_inc(stored, 16)
                load_xT(0)
                load_x2(0)
                sp.wait_ge(z_filled, CH)
                load_xT(1)
                with sp.Fori(0, NSEG - 2) as n:
                    sp.wait_ge(z_filled, n * CH + 2 * CH)
                    load_xT(n + 2)
                    store(n)
                    load_x2(n + 1)
                store(NSEG - 2)
                load_x2(NSEG - 1)
                store(NSEG - 1)
                sp.wait_ge(stored, 16 * NSEG + 16)

            @block.tensor
            def _(pe):
                class Body(Nothing):
                    def start(self):
                        pe.wait_ge(lo_done, 1)
                        self.spread_c(0, 0, 0)
                        for st in range(4):
                            self.spread_b(0, 0, st)

                    def unit(self, n, v, k, more):
                        st = k // CH
                        if k % CH == 0 and st + 1 < DS:
                            self.spread_c(n, v, st + 1)
                        elif k % CH == 0 and more:
                            self.spread_c(n + 1, 1 - v, 0)
                        elif k % CH == 1 and st + 4 < DS:
                            self.spread_b(n, v, st + 4)
                        elif k % CH == 1 and more:
                            if st + 4 == DS:
                                pe.wait_ge(lo_done, n + 2)
                            self.spread_b(n + 1, 1 - v, st + 4 - DS)
                        if k >= 2:
                            self.add(n, k - 2)

                    def spread_b(self, n, v, st):
                        pe.wait_ge(b_copied, n * DS + st + 1)
                        pe.matmul(b_ps[:], sel[:, st], bc[v][:], start=True, stop=True).then_inc(b_filled, 1)

                    def spread_c(self, n, v, st):
                        pe.wait_ge(hc_done, n * UNITS + st * CH + CH)
                        pe.matmul(c_ps[:, st % 2], sel[:, DS + st], bc[v][:], start=True, stop=True).then_inc(c_filled, 1)

                    def add(self, n, k):
                        st, c = k // CH, k % CH
                        pe.wait_ge(hc_done, n * UNITS + k + 1 + RING)
                        if st == 0 and not (isinstance(n, int) and n == 0):
                            pe.wait_ge(skip_done, n * CH + c + 1 - CH)
                        pe.matmul(y_ps[:, c], ident_f[:], hc[:, k % HRING], start=(st == 0), stop=(st == DS - 1)
                                  ).then_inc(add_done, 1)

                    def finish(self, n, v):
                        for k in (UNITS - 2, UNITS - 1):
                            self.add(n, k)

                    def ahead(self, x, n, v):
                        kind, c = x
                        first = isinstance(n, int) and n == 0
                        if kind in ("X", "Z"):
                            if kind == "X":
                                pe.wait_ge(xT_in, n * 16 + 16)
                                if c:
                                    pe.wait_ge(x_copied, n * 2 * CH + 2 * c)
                                elif not first:
                                    pe.wait_ge(pre_done, n * CH)
                                    if not isinstance(n, int):
                                        pe.wait_ge(sum_done, n * 2 - 3)
                            else:
                                pe.wait_ge(z_copied if c else x_copied, n * CH + c if c else n * 2 * CH + 2 * CH)
                            col = (CH * (kind == "Z") + c) * P
                            for k in range(KD):
                                mm = pe.matmul(f_ps[:], w_in[:, k, col:col + P], xT[:, k], start=(k == 0), stop=(k == KD - 1))
                            mm.then_inc(x_filled if kind == "X" else z_filled, 1)
                        elif kind == "P":
                            pe.wait_ge(z_copied, n * CH + CH)
                            pe.wait_ge(silu_done, n * 2 + 2)
                            for k in range(CH):
                                mm = pe.matmul(f_ps[0:BCROWS + DR], w_x[:, k], xc[v][:, k], start=(k == 0), stop=(k == CH - 1))
                            mm.then_inc(p_filled, 1)
                        elif kind == "T":
                            if c == 0:
                                pe.wait_ge(rest_done, n + 1)
                                pe.wait_ge(raw_done, n + 1)
                            else:
                                pe.wait_ge(pre_done, n * CH + c)
                            pe.matmul(f_ps[:], w_dt[BCROWS:BCROWS + DR, c * P:(c + 1) * P], d_raw[BCROWS:BCROWS + DR],
                                      start=True, stop=True).then_inc(t_filled, 1)

                    def behind(self, x, n, v):
                        kind, half = x
                        if kind == "O":
                            if half == 0:
                                pe.wait_ge(yz_done, n * CH + CH)
                                if isinstance(n, int):
                                    pe.wait_ge(sum_done, 2 * n + 1)
                                else:
                                    pe.wait_ge(pre_done, n * CH + 3 * CH)
                            else:
                                pe.wait_ge(sum_done, n * 2 + 2)
                            for a in (0, 1):
                                t = 2 * half + a
                                for k in range(CH):
                                    mm = pe.matmul(f_ps[:, a * D:(a + 1) * D], yt[:, k, t * P:(t + 1) * P], w_out[:, k],
                                                   start=(k == 0), stop=(k == CH - 1))
                            mm.then_inc(o_filled, 1)

                pe.wait_ge(weights, 16 * 11)
                pe.sem_inc(add_done, HRING)
                bodies(pe.Fori, Body(), "PE")

            @block.scalar
            def _(act):
                class Body(Nothing):
                    def start(self):
                        self.copy_b(0, 0)

                    def unit(self, n, v, k, more):
                        st, c = k // CH, k % CH
                        if c == 0:
                            if st == 0:
                                act.wait_ge(soft_done, n * 3 + 3)
                            if st + 1 < DS:
                                self.copy_b(n, st + 1)
                            elif more:
                                self.copy_b(n + 1, 0)
                        act.wait_ge(scan_done, n * UNITS + k + 1)
                        act.activation(decay[:, k % RING], delta[v][:, c], ACT.Exp, scale=a_neg[:, c, st:st + 1]
                                       ).then_inc(decay_done, 1)

                    def copy_b(self, n, st):
                        act.wait_ge(b_filled, n * DS + st + 1)
                        act.wait_ge(drive_done, n * UNITS + st * CH + CH)
                        act.activation(b_sb[:, st % BRING], b_ps[:], ACT.Copy).then_inc(b_copied, 1)

                    def ahead(self, x, n, v):
                        kind, c = x
                        first = isinstance(n, int) and n == 0
                        if kind == "X":
                            if c == 0:
                                act.wait_ge(halo_done, n + 1)
                            act.wait_ge(x_filled, n * CH + c + 1)
                            act.activation(xb[:, c, DC - 1:], f_ps[:], ACT.Copy).then_inc(x_copied, 1)
                            if c == 0 and not first and not (isinstance(n, int) and n == 1):
                                act.wait_ge(skip_done, n * CH - CH)
                            act.activation(xc[v][:, c], f_ps[:], ACT.Identity, bias=conv_b[:, c:c + 1],
                                           scale=conv_w[:, c, DC - 1:DC]).then_inc(x_copied, 1)
                        elif kind == "Z":
                            if c == 0 and not first and not (isinstance(n, int) and n == 1):
                                act.wait_ge(yz_done, n * CH - CH)
                            act.wait_ge(z_filled, n * CH + c + 1)
                            act.activation(sz[v][:, c], f_ps[:], ACT.Copy).then_inc(z_copied, 1)
                        elif kind == "silu":
                            act.wait_ge(z_copied, n * CH + CH)
                            act.activation(sz[v][:], sz[v][:], ACT.Silu).then_inc(silu_done, 1)
                            act.wait_ge(conv_done, n * (DC - 1) * CH + (DC - 1) * CH)
                            act.activation(xc[v][:], xc[v][:], ACT.Silu).then_inc(silu_done, 1)
                        elif kind == "P":
                            act.wait_ge(p_filled, n + 1)
                            act.activation(bc[v][0:BCROWS], f_ps[0:BCROWS], ACT.Copy).then_inc(hi_done, 1)
                            act.activation(d_raw[BCROWS:BCROWS + DR], f_ps[BCROWS:BCROWS + DR], ACT.Copy).then_inc(raw_done, 1)
                        elif kind == "T":
                            act.wait_ge(t_filled, n * CH + c + 1)
                            act.activation(pre[:, c], f_ps[:], ACT.Identity, bias=b_dt[:, c:c + 1]).then_inc(pre_done, 1)
                        elif kind == "exp":
                            act.wait_ge(pre_done, n * CH + CH)
                            act.activation(ex[:], pre[:], ACT.Abs).then_inc(abs_done, 1)
                            act.wait_ge(abs_done, n + 1)
                            act.activation(ex[:], ex[:], ACT.Exp, scale=-1.0).then_inc(exp_done, 1)
                            act.wait_ge(exp_done, n + 1)
                            act.activation(du[v][:], ex[:], ACT.Copy, bias=1.0).then_inc(one_done, 1)
                        elif kind == "ln":
                            act.wait_ge(one_done, n + 1)
                            act.activation(delta[v][:], du[v][:], ACT.Ln).then_inc(ln_done, 1)

                    def behind(self, x, n, v):
                        if x[0] == "root":
                            layernorm_root(act, ln, n, v)

                act.wait_ge(weights, 16 * 11)
                act.activation(a_exp[:], a_log[:], ACT.Exp).then_inc(ready, 1)
                act.sem_inc(b_copied, 1)
                act.wait_ge(ready, 3)
                bodies(act.Fori, Body(), "ACT")

            @block.vector
            def _(dve):
                class Body(Nothing):
                    def unit(self, n, v, k, more):
                        st, c = k // CH, k % CH
                        first = isinstance(n, int) and n == 0
                        if c == 0 and not first:
                            dve.wait_ge(carry_done, n * DS + st + 1 - DS)
                        dve.wait_ge(decay_done, n * UNITS + k + 1)
                        dve.wait_ge(drive_done, n * UNITS + k + 1 + BRING * CH)
                        dve.tensor_tensor_scan(h[:, k % RING], decay[:, k % RING], drive[:, k % RING],
                                               0.0 if first else carry[:, k:k + 1], ALU.mult, ALU.add).then_inc(scan_done, 1)
                        if k >= 1:
                            self.weigh(n, k - 1)

                    def weigh(self, n, k):
                        st, c = k // CH, k % CH
                        dve.wait_ge(scan_done, n * UNITS + k + 1 + RING)
                        if c == 0:
                            dve.wait_ge(c_filled, n * DS + st + 1)
                        dve.wait_ge(add_done, n * UNITS + k + 1)
                        dve.tensor_tensor(hc[:, k % HRING], h[:, k % RING], c_ps[:, st % 2], ALU.mult).then_inc(hc_done, 1)
                        if c == CH - 1:
                            r = (k - c) % RING
                            dve.tensor_scalar(carry[:, k - c:k + 1], h[:, r:r + CH, SEG - 1], keep[:, bass.ds(n, 1)], None,
                                              ALU.mult).then_inc(carry_done, 1)

                    def finish(self, n, v):
                        self.weigh(n, UNITS - 1)
                        for c in range(CH):
                            dve.wait_ge(add_done, n * UNITS + UNITS - CH + c + 1 + HRING)
                            if c == 0 and not (isinstance(n, int) and n == 0):
                                dve.wait_ge(o_filled, n * 2)
                            dve.scalar_tensor_tensor(yt[:, c], xc[v][:, c], d_par[:, c:c + 1], y_ps[:, c], ALU.mult, ALU.add
                                                     ).then_inc(skip_done, 1)

                    def ahead(self, x, n, v):
                        kind, c = x
                        if kind == "conv":
                            tap = c
                            for c in range(CH):
                                if tap == 0:
                                    dve.wait_ge(x_copied, (n * CH + c) * 2 + 2)
                                else:
                                    dve.wait_ge(conv_done, (n * (DC - 1) + tap - 1) * CH + c + 1)
                                dve.scalar_tensor_tensor(xc[v][:, c], xb[:, c, tap:tap + SEG], conv_w[:, c, tap:tap + 1],
                                                         xc[v][:, c], ALU.mult, ALU.add).then_inc(conv_done, 1)
                            if tap == DC - 2:
                                dve.wait_ge(conv_done, (n + 1) * (DC - 1) * CH)
                                dve.tensor_scalar(xb[:, :, 0:DC - 1], xb[:, :, SEG:SEG + DC - 1], keep[:, bass.ds(n, 1)], None,
                                                  ALU.mult).then_inc(halo_done, 1)
                        elif kind == "P":
                            dve.wait_ge(hi_done, n + 1)
                            dve.tensor_tensor(bc_rest[:], f_ps[0:BCROWS], bc[v][0:BCROWS], ALU.subtract).then_inc(rest_done, 1)
                            dve.wait_ge(rest_done, n + 1)
                            dve.tensor_copy(bc_mid[:], bc_rest[:]).then_inc(mid_done, 1)
                            dve.tensor_copy(bc[v][BCROWS:2 * BCROWS], bc_rest[:]).then_inc(mid_done, 1)
                            dve.wait_ge(mid_done, n * 2 + 2)
                            dve.tensor_tensor(bc[v][2 * BCROWS:], bc_rest[:], bc_mid[:], ALU.subtract).then_inc(lo_done, 1)
                        elif kind == "soft":
                            if c == 0:
                                dve.wait_ge(ln_done, n + 1)
                                dve.scalar_tensor_tensor(du[v][:], du[v][:], 1.0, ex[:], ALU.subtract, ALU.subtract
                                                         ).then_inc(soft_done, 1)
                            elif c == 1:
                                dve.wait_ge(soft_done, n * 3 + 1)
                                dve.scalar_tensor_tensor(pre[:], pre[:], 0.0, du[v][:], ALU.max, ALU.subtract
                                                         ).then_inc(soft_done, 1)
                            else:
                                dve.wait_ge(soft_done, n * 3 + 2)
                                dve.tensor_tensor(delta[v][:], delta[v][:], pre[:], ALU.add).then_inc(soft_done, 1)

                    def behind(self, x, n, v):
                        kind, half = x
                        if kind == "O":
                            if half == 0:
                                dve.wait_ge(x2_in, n * 16 + 16)
                                dve.wait_ge(stored, n * 16 + 16)
                            dve.wait_ge(o_filled, n * 2 + half + 1)
                            dve.tensor_tensor(sm[:, 2 * half:2 * half + 2], f_ps[:].rearrange("p (a d) -> p a d", d=D),
                                              x2[:, 2 * half:2 * half + 2], ALU.add).then_inc(sum_done, 1)
                        elif half == 0:
                            dve.wait_ge(sum_done, n * 2 + 3)
                            layernorm_stats(dve, ln, n, v, sm[:], TPS)
                        else:
                            layernorm_apply(dve, ln, n, v, sm[:], sm[:], TPS)

                dve.wait_ge(weights, 16 * 11)
                dve.memset(xb[:, :, 0:DC - 1], 0.0).then_inc(halo_done, 1)
                dve.wait_ge(ready, 1)
                dve.tensor_scalar(a_neg[:], a_exp[:], -1.0, None, ALU.mult).then_inc(ready, 2)
                dve.sem_inc(scan_done, RING)
                dve.sem_inc(sum_done, 1)
                dve.sem_inc(hc_done, RING)
                bodies(dve.Fori, Body(), "DVE")

            @block.gpsimd
            def _(pool):
                class Body(Nothing):
                    def unit(self, n, v, k, more):
                        st, c = k // CH, k % CH
                        if k == 0:
                            pool.wait_ge(u_done, n * CH + CH)
                        if c == 0:
                            pool.wait_ge(b_copied, n * DS + st + 2)
                        pool.wait_ge(scan_done, n * UNITS + k + 1)
                        pool.tensor_tensor(drive[:, k % RING], du[v][:, c], b_sb[:, st % BRING], ALU.mult).then_inc(drive_done, 1)

                    def ahead(self, x, n, v):
                        c = x[1]
                        if c == 0:
                            pool.wait_ge(soft_done, n * 3 + 3)
                        pool.tensor_tensor(du[v][:, c], delta[v][:, c], xc[v][:, c], ALU.mult).then_inc(u_done, 1)

                    def behind(self, x, n, v):
                        c = x[1]
                        pool.wait_ge(skip_done, n * CH + c + 1)
                        pool.tensor_tensor(yt[:, c], yt[:, c], sz[v][:, c], ALU.mult).then_inc(yz_done, 1)

                pool.sem_inc(drive_done, BRING * CH)
                bodies(pool.Fori, Body(), "Pool")


ROUND = 1.5 * 2.0 ** 23
HBANKS = 4


def ffn_phase(nc, x3_rows, w1T_d, w2T_d, b1_d, b2_d, ident_f, out_rows):
    with ExitStack() as ctx:
        s = Space(nc, ctx, "ffn")
        w1 = s.sb("w1", [P, KD, F])
        w2 = s.sb("w2", [P, FK, D])
        mag = s.sb("mag", [P, 2, KD * F])
        part = s.sb("part", [P, 2])
        ones = s.sb("ones", [P, P])
        gamma = s.sb("gamma", [P, 2])
        scale = s.sb("scale", [P, 2])
        b1 = s.sb("b1", [P, FK])
        b2 = s.sb("b2", [P, D])
        x = s.sb("x", [P, 2, TPS, D])
        xb = s.sb("xb", [P, 2, TPS, D])
        xT = s.sb("xT", [P, KD, SEG])
        h = s.sb("h", [P, FK, SEG])
        sm = s.sb("sm", [P, 2, TPS, D])
        out = s.sb("out", [P, 2, TPS, D])
        ln = layernorm_buffers(s, TPS)
        t_ps = s.ps("t_ps", [P, KD, SEG])
        h_ps = s.ps("h_ps", [P, HBANKS, SEG])
        y_ps = s.ps("y_ps", [P, 2, SEG])
        w_in, mag_done, part_done, total_done, quant, quantised = (
            s.sem(n) for n in ("w_in", "mag", "part", "total", "quant", "quantised"))
        x_in, stored = [s.sem("x_in0"), s.sem("x_in1")], [s.sem("stored0"), s.sem("stored1")]
        turned, xT_done, up_done, relu_done, down_done, biased, sum_done = (
            s.sem(n) for n in ("turned", "xT", "up", "relu", "down", "biased", "sum"))

        with nc.Block() as block:
            @block.sync
            def _(sp):
                def load(n, u):
                    sp.dma_start(x[:, u], x3_rows[bass.ds(n * SEG, SEG)].rearrange("(a p) d -> p a d", p=P)
                                 ).then_inc(x_in[u], 16)

                def store(n, u):
                    sp.wait_ge(ln["out_done"], (n + 1) * TPS)
                    sp.dma_start(out_rows[bass.ds(n * SEG, SEG)].rearrange("(a p) d -> p a d", p=P), out[:, u]
                                 ).then_inc(stored[u], 16)

                sp.dma_start(w1[:], w1T_d.rearrange("(k p) n -> p k n", p=P)).then_inc(w_in, 16)
                sp.dma_start(w2[:], w2T_d.rearrange("(k p) n -> p k n", p=P)).then_inc(w_in, 16)
                sp.dma_start(b1[:], b1_d).then_inc(w_in, 16)
                sp.dma_start(b2[:], b2_d.partition_broadcast(P)).then_inc(w_in, 16)
                load(0, 0)
                load(1, 1)
                with sp.Fori(0, NSEG // 2 - 1) as i:
                    for u in range(2):
                        n = i * 2 + u
                        sp.wait_ge(turned, n + 1)
                        sp.wait_ge(biased, n + 1)
                        load(n + 2, u)
                        store(n, u)
                for u in range(2):
                    store(NSEG - 2 + u, u)
                for u in range(2):
                    sp.wait_ge(stored[u], 16 * NSEG // 2)

            @block.tensor
            def _(pe):
                def turn(n, i, u):
                    pe.wait_ge(x_in[u], i * 16 + 16)
                    for k in range(KD):
                        for a in range(TPS):
                            mm = pe.transpose(t_ps[:, k, a * P:(a + 1) * P], x[:, u, a, k * P:(k + 1) * P], ident_f[:])
                    mm.then_inc(turned, 1)

                def up(n):
                    pe.wait_ge(xT_done, n + 1)
                    for c in range(FK):
                        pe.wait_ge(relu_done, n * FK + c + 1)
                        for k in range(KD):
                            mm = pe.matmul(h_ps[:, c % HBANKS], w1[:, k, c * P:(c + 1) * P], xT[:, k],
                                           start=(k == 0), stop=(k == KD - 1))
                        mm.then_inc(up_done, 1)

                def down(n):
                    pe.wait_ge(sum_done, n + 1)
                    for a in range(TPS):
                        for c in range(FK):
                            if a == 0:
                                pe.wait_ge(relu_done, n * FK + c + 1 + HBANKS)
                            mm = pe.matmul(y_ps[:, a // 2, (a % 2) * D:(a % 2 + 1) * D], h[:, c, a * P:(a + 1) * P],
                                           w2[:, c], start=(c == 0), stop=(c == FK - 1))
                    mm.then_inc(down_done, 1)

                pe.wait_ge(part_done, 3)
                pe.matmul(y_ps[:, 0, 0:2], ones[:], part[:], start=True, stop=True).then_inc(total_done, 1)
                turn(0, 0, 0)
                pe.wait_ge(quantised, 2)
                with pe.Fori(0, NSEG // 2 - 1) as i:
                    for u in range(2):
                        n = i * 2 + u
                        up(n)
                        turn(n + 1, i + u, 1 - u)
                        down(n)
                up(NSEG - 2)
                turn(NSEG - 1, NSEG // 2 - 1, 1)
                down(NSEG - 2)
                up(NSEG - 1)
                down(NSEG - 1)

            @block.scalar
            def _(act):
                def relu(n, c):
                    act.wait_ge(up_done, n * FK + c + 1)
                    act.activation(h[:, c], h_ps[:, c % HBANKS], ACT.Relu, bias=b1[:, c:c + 1]).then_inc(relu_done, 1)

                def copy_x(n):
                    act.wait_ge(turned, n + 1)
                    act.activation(xT[:], t_ps[:], ACT.Copy).then_inc(xT_done, 1)

                act.wait_ge(w_in, 64)
                for w, m in ((w1, 0), (w2, 1)):
                    act.activation(mag[:, m], w[:].rearrange("p k n -> p (k n)"), ACT.Abs).then_inc(mag_done, 1)
                act.sem_inc(relu_done, HBANKS)
                copy_x(0)

                def body(n, u, before, after):
                    for c in range(FK):
                        relu(n, c)
                        if c == 3 and before:
                            layernorm_root(act, ln, n - 1, 1 - u)
                    if after:
                        copy_x(n + 1)

                body(0, 0, False, True)
                with act.Fori(0, NSEG // 2 - 1) as i:
                    body(i * 2 + 1, 1, True, True)
                    body(i * 2 + 2, 0, True, True)
                body(NSEG - 1, 1, True, False)
                layernorm_root(act, ln, NSEG - 1, 1)

            @block.vector
            def _(dve):
                def norm(n, u):
                    dve.wait_ge(down_done, n + 1)
                    dve.wait_ge(biased, n + 1)
                    dve.tensor_tensor(sm[:, u], y_ps[:].rearrange("p c (a d) -> p (c a) d", d=D), xb[:, u], ALU.add
                                      ).then_inc(sum_done, 1)
                    dve.wait_ge(sum_done, n + 2)
                    layernorm(dve, ln, n, u, sm[:, u], out[:, u], TPS)

                dve.memset(ones[:], 1.0).then_inc(part_done, 1)
                for m in range(2):
                    dve.wait_ge(mag_done, m + 1)
                    dve.tensor_reduce(part[:, m:m + 1], mag[:, m], AX.X, ALU.add).then_inc(part_done, 1)
                dve.wait_ge(total_done, 1)
                dve.tensor_scalar(gamma[:], y_ps[:, 0, 0:2], 1.0 / (F * D), EPS, ALU.mult, ALU.add).then_inc(quant, 1)
                dve.sem_inc(sum_done, 1)
                dve.wait_ge(quant, 1)
                dve.reciprocal(scale[:], gamma[:]).then_inc(quant, 1)
                dve.wait_ge(quant, 2)
                flat = [w[:].rearrange("p k n -> p (k n)") for w in (w1, w2)]
                for m, w in enumerate(flat):
                    dve.tensor_scalar(w, w, scale[:, m:m + 1], 1.0, ALU.mult, ALU.min).then_inc(quant, 1)
                for m, w in enumerate(flat):
                    dve.wait_ge(quant, 3 + m)
                    dve.tensor_scalar(w, w, -1.0, ROUND, ALU.max, ALU.add).then_inc(quant, 1)
                for m, w in enumerate(flat):
                    dve.wait_ge(quant, 5 + m)
                    dve.tensor_scalar(w, w, ROUND, None, ALU.subtract).then_inc(quantised, 1)
                for u in range(2):
                    norm(u, u)
                with dve.Fori(1, NSEG // 2) as i:
                    for u in range(2):
                        dve.wait_ge(stored[u], i * 16)
                        norm(i * 2 + u, u)

            @block.gpsimd
            def _(pool):
                def bias(n, u, i):
                    pool.wait_ge(x_in[u], i * 16 + 16)
                    pool.tensor_tensor(xb[:, u], x[:, u], b2[:].unsqueeze(1).broadcast_to([P, TPS, D]), ALU.add
                                       ).then_inc(biased, 1)

                pool.wait_ge(w_in, 64)
                for u in range(2):
                    bias(u, u, 0)
                with pool.Fori(1, NSEG // 2) as i:
                    for u in range(2):
                        n = i * 2 + u
                        pool.wait_ge(sum_done, n)
                        bias(n, u, i)


SLOTS = TILES + E


def build(nc, xT, x_rows, wq, wkv, wo, wr, br, ew1, eb1, ew2, eb2, w_in, conv_w, conv_b, w_x, w_dt, b_dt, a_log, d_par,
          w_out, fw1, fb1, fw2, fb2, c_ident, c_ident_b, c_tri_st, c_tri_ts, c_before, c_ones, c_slots, c_ranks,
          c_keep, c_sel, out_rows):
    def scratch(name, shape, dt=F32):
        return nc.dram_tensor(name, shape, dt).ap()

    qk_parts = scratch("qk_parts", (3, D + GROUPS * HD + 64, TOK), BF16)
    v_rows = scratch("v_rows", (TOK, GROUPS * HD))
    shift_rows = scratch("shift_rows", (3, GS * SBLK, P), BF16)
    ctx_rows = scratch("ctx_rows", (GROUPS, P, TOK))
    inv_rows = scratch("inv_rows", (HEADS, TOK))
    x1_rows = scratch("x1_rows", (TOK, D))
    sorted_rows = scratch("sorted_rows", (SLOTS * P, D))
    done_rows = scratch("done_rows", (SLOTS * P, D))
    x2_rows = scratch("x2_rows", (TOK, D))
    x2T_rows = scratch("x2T_rows", (D, TOK))
    x3_rows = scratch("x3_rows", (TOK, D))

    with ExitStack() as ctx:
        s = Space(nc, ctx, "all")
        ident_f, ident_b = s.sb("ident_f", [P, P]), s.sb("ident_b", [P, P], BF16)
        tri_st, tri_ts = s.sb("tri_st", [P, P], BF16), s.sb("tri_ts", [P, P], BF16)
        before, ones_b = s.sb("before", [P, P], BF16), s.sb("ones_b", [P, P], BF16)
        slots_iota, ranks, br_sb = s.sb("slots", [1, SLOTS]), s.sb("ranks", [P, E]), s.sb("br", [P, TPS, E])
        scores_sb, pos_sb = s.sb("scores", [P, TILES, E]), s.sb("pos", [P, TILES], I32)
        owner_sb = s.sb("owner", [1, SLOTS], I32)
        consts_in, zero_done, zeroed, weights_in = (s.sem(n) for n in ("consts_in", "zero_done", "zeroed", "weights_in"))

        with ExitStack() as early:
            zero = early.enter_context(nc.sbuf_tensor("all_zero", [P, 2048], F32))
            with nc.Block() as block:
                @block.vector
                def _(dve):
                    dve.memset(zero[:], 0.0).then_inc(zero_done, 1)

                @block.sync
                def _(sp):
                    consts = ((ident_f, c_ident), (ident_b, c_ident_b), (tri_st, c_tri_st), (tri_ts, c_tri_ts),
                              (before, c_before), (ones_b, c_ones), (slots_iota, c_slots), (ranks, c_ranks))
                    for t, d in consts:
                        sp.dma_start(t[:], d).then_inc(consts_in, 16)
                    for a in range(TPS):
                        sp.dma_start(br_sb[:, a], br.partition_broadcast(P)).then_inc(consts_in, 16)
                    sp.wait_ge(zero_done, 1)
                    pieces = SLOTS * D // 2048
                    for k in range(pieces):
                        sp.dma_start(sorted_rows.rearrange("(k p r) d -> k p (r d)", k=pieces, p=P)[k], zero[:]
                                     ).then_inc(zeroed, 16)
                    sp.wait_ge(consts_in, 16 * (len(consts) + TPS))
            project_phase(nc, xT, wq, wkv, qk_parts, v_rows)
            with nc.Block() as block:
                @block.sync
                def _(sp):
                    sp.wait_ge(zeroed, 16 * (SLOTS * D // 2048))

        with ExitStack() as experts:
            def sb(name, shape):
                return experts.enter_context(nc.sbuf_tensor(f"moe_{name}", shape, F32))

            e_w1, e_b1 = sb("w1", [P, E * KD, F]), sb("b1", [P, E, F])
            with nc.Block() as block:
                @block.sync
                def _(sp):
                    sp.dma_start(e_w1[:], ew1.rearrange("e (k p) n -> p (e k) n", p=P)).then_inc(weights_in, 16)
                    sp.dma_start(e_b1[:], eb1.partition_broadcast(P)).then_inc(weights_in, 16)
            attention_phase(nc, qk_parts, v_rows, shift_rows, ctx_rows, ident_f, ident_b, tri_st, tri_ts)
            denominators_phase(nc, ctx_rows, inv_rows)
            out_project_phase(nc, ctx_rows, inv_rows, x_rows, wo, wr, br_sb, ident_f, scores_sb, x1_rows)
            e_w2, e_b2 = sb("w2", [P, E * FK, D]), sb("b2", [P, E, D])
            with nc.Block() as block:
                @block.sync
                def _(sp):
                    sp.dma_start(e_w2[:], ew2.rearrange("e (k p) n -> p (e k) n", p=P)).then_inc(weights_in, 16)
                    sp.dma_start(e_b2[:], eb2.partition_broadcast(P)).then_inc(weights_in, 16)
            routing_phase(nc, scores_sb, pos_sb, owner_sb, ident_b, before, ones_b, slots_iota, ranks, SLOTS)
            scatter_phase(nc, x1_rows, pos_sb, sorted_rows, zeroed, 16 * (SLOTS * D // 2048))
            experts_phase(nc, SLOTS, sorted_rows, done_rows, owner_sb, e_w1, e_w2, e_b1, e_b2, weights_in, 64, ident_f)
        combine_phase(nc, x1_rows, done_rows, pos_sb, ident_f, x2_rows, x2T_rows)
        mamba_phase(nc, x2_rows, x2T_rows, x3_rows, w_in, conv_w, conv_b, w_x, w_dt, b_dt, a_log, d_par, w_out,
                    c_keep, c_sel, ident_f)
        ffn_phase(nc, x3_rows, fw1, fw2, fb1, fb2, ident_f, out_rows)


def kernel(L0_attn_x, L0_attn_wq, L0_attn_wk, L0_attn_wv, L0_attn_wo, L0_ffn_wr, L0_ffn_br, L0_ffn_w1, L0_ffn_b1,
           L0_ffn_w2, L0_ffn_b2, L1_attn_W_in, L1_attn_conv_w, L1_attn_conv_b, L1_attn_W_xproj, L1_attn_W_dt,
           L1_attn_b_dt, L1_attn_A_log, L1_attn_D_param, L1_attn_W_out, L1_ffn_W1, L1_ffn_b1, L1_ffn_W2, L1_ffn_b2):
    import concourse.bacc as bacc
    from concourse.bass_utils import run_bass_kernel_spmd

    bf16 = mybir.dt.np(BF16)
    x = np.asarray(L0_attn_x).reshape(TOK, D)
    wo = np.zeros((GROUPS, GS, 32, D), np.float32)
    wo[:, :, :HD] = L0_attn_wo.T.reshape(GROUPS, GS, HD, D)
    after = np.arange(P)[None, :] > np.arange(P)[:, None]
    sel = np.zeros((3, BCROWS, BCROWS, P), bf16)
    sel[:, np.arange(BCROWS), np.arange(BCROWS)] = 1
    keep = np.ones((P, NSEG), np.float32)
    keep[:, NSEG // BATCH - 1::NSEG // BATCH] = 0
    lay = {
        "xT": x.T, "x_rows": x, "wq": L0_attn_wq.T, "wkv": np.concatenate([L0_attn_wk.T, L0_attn_wv.T], 1),
        "wo": wo.reshape(GROUPS, P, D), "wr": L0_ffn_wr, "br": L0_ffn_br, "ew1": L0_ffn_w1, "eb1": L0_ffn_b1,
        "ew2": L0_ffn_w2, "eb2": L0_ffn_b2, "w_in": L1_attn_W_in, "conv_w": L1_attn_conv_w,
        "conv_b": L1_attn_conv_b.reshape(CH, P).T,
        "w_x": np.concatenate([L1_attn_W_xproj[:, DR:], L1_attn_W_xproj[:, :DR]], 1),
        "w_dt": L1_attn_W_dt, "b_dt": L1_attn_b_dt.reshape(CH, P).T, "a_log": L1_attn_A_log,
        "d_par": L1_attn_D_param.reshape(CH, P).T, "w_out": L1_attn_W_out,
        "fw1": L1_ffn_W1.T, "fb1": L1_ffn_b1.reshape(FK, P).T, "fw2": L1_ffn_W2.T, "fb2": L1_ffn_b2,
        "c_ident": np.eye(P, dtype=np.float32), "c_ident_b": np.eye(P, dtype=np.float32).astype(bf16),
        "c_tri_st": np.where(after, MASKED, 0).astype(bf16), "c_tri_ts": np.where(after.T, MASKED, 0).astype(bf16),
        "c_before": after.astype(bf16), "c_ones": np.ones((P, P), bf16),
        "c_slots": np.arange(SLOTS, dtype=np.float32)[None],
        "c_ranks": np.broadcast_to(E - np.arange(E, dtype=np.float32), (P, E)),
        "c_keep": keep, "c_sel": sel.reshape(3 * BCROWS, BCROWS, P),
    }
    nc = bacc.Bacc("TRN2", target_bir_lowering=False, num_devices=1)
    arrays, args = {}, []
    for name, a in lay.items():
        a = np.ascontiguousarray(a)
        arrays[f"in_{name}"] = a
        args.append(nc.dram_tensor(f"in_{name}", a.shape, mybir.dt.from_np(a.dtype), kind="ExternalInput").ap())
    args.append(nc.dram_tensor("out_rows", (TOK, D), F32, kind="ExternalOutput").ap())
    build(nc, *args)
    r = run_bass_kernel_spmd(nc, [arrays], core_ids=[0])
    return r.results[0]["out_rows"].reshape(BATCH, SEQ, D)
```

```python
from contextlib import ExitStack

import numpy as np
import concourse.bass as bass
from concourse import mybir

F32 = mybir.dt.float32
BF16 = mybir.dt.bfloat16
I32 = mybir.dt.int32
ALU = mybir.AluOpType
ACT = mybir.ActivationFunctionType
AX = mybir.AxisListType

P = 128
BATCH, SEQ, D = 2, 2048, 256
TOK = BATCH * SEQ
KD = D // P
SEG = 512
HEADS, GROUPS, HD = 16, 4, 16
GS = HEADS // GROUPS
MASKED = -1.0e30
EPS = 1e-5


class Space:

    def __init__(self, nc, ctx, tag):
        self.nc, self.ctx, self.tag, self.sems = nc, ctx, tag, []
        ctx.callback(self.close)

    def close(self):
        self.nc.clear_and_free_semaphores(self.sems)
        with self.nc.Block():
            pass

    def sb(self, name, shape, dt=F32):
        return self.ctx.enter_context(self.nc.sbuf_tensor(f"{self.tag}_{name}", shape, dt))

    def ps(self, name, shape, dt=F32):
        return self.ctx.enter_context(self.nc.psum_tensor(f"{self.tag}_{name}", shape, dt))

    def sem(self, name):
        self.sems.append(self.nc.alloc_semaphore(f"{self.tag}_{name}"))
        return self.sems[-1]


def project_phase(nc, xT, wq, wkv, qk_parts, v_rows):
    NSEG = TOK // SEG
    with ExitStack() as ctx:
        s = Space(nc, ctx, "proj")
        w_q = s.sb("wq", [P, KD, D])
        w_kv = s.sb("wkv", [P, KD, P])
        xin = s.sb("xin", [P, 2, KD, SEG])
        hi = s.sb("hi", [P, 2, 3, SEG], BF16)
        rest = s.sb("rest", [P, 2, 3, SEG])
        mid = s.sb("mid", [P, 2, 3, SEG], BF16)
        lo = s.sb("lo", [P, 2, 3, SEG], BF16)
        vout = s.sb("vout", [P, 2, 4, 64])
        qk_ps = s.ps("qk", [P, 2, 3, SEG])
        v_ps = s.ps("v", [P, 2, SEG])
        w_in, x_in = s.sem("w_in"), [s.sem("x_in0"), s.sem("x_in1")]
        qk_done, v_done = s.sem("qk_done"), s.sem("v_done")
        hi_done, rest_done, mid_done, lo_done = s.sem("hi"), s.sem("rest"), s.sem("mid"), s.sem("lo")
        v_copied, stored = s.sem("v_copied"), [s.sem("stored0"), s.sem("stored1")]

        with nc.Block() as block:
            @block.sync
            def _(sp):
                def load(n, u):
                    sp.dma_start(xin[:, u], xT.rearrange("(k p) n -> p k n", p=P)[:, :, bass.ds(n * SEG, SEG)]
                                 ).then_inc(x_in[u], 16)

                def store(n, u):
                    for part, (buf, done) in enumerate(((hi, hi_done), (mid, mid_done), (lo, lo_done))):
                        sp.wait_ge(done, n + 1)
                        sp.dma_start(qk_parts[part].rearrange("(c p) n -> p c n", p=P)[:, :, bass.ds(n * SEG, SEG)],
                                     buf[:, u]).then_inc(stored[u], 16)
                    sp.wait_ge(v_copied, n + 1)
                    sp.dma_start(v_rows.rearrange("(a p) n -> p a n", p=P)[:, bass.ds(n * 4, 4), :],
                                 vout[:, u]).then_inc(stored[u], 16)

                sp.dma_start(w_q[:], wq.rearrange("(k p) n -> p k n", p=P)).then_inc(w_in, 16)
                sp.dma_start(w_kv[:], wkv.rearrange("(k p) n -> p k n", p=P)).then_inc(w_in, 16)
                for u in range(2):
                    load(u, u)
                with sp.Fori(0, NSEG // 2 - 1) as i:
                    for u in range(2):
                        sp.wait_ge(v_done, i * 2 + u + 1)
                        load(i * 2 + u + 2, u)
                        store(i * 2 + u, u)
                for u in range(2):
                    store(NSEG - 2 + u, u)
                for u in range(2):
                    sp.wait_ge(stored[u], 64 * (NSEG // 2))

            @block.tensor
            def _(pe):
                def products(n, i, u):
                    pe.wait_ge(x_in[u], i * 16 + 16)
                    for c in range(3):
                        for k in range(KD):
                            w = w_q[:, k, c * P:(c + 1) * P] if c < 2 else w_kv[:, k, :]
                            mm = pe.matmul(qk_ps[:, u, c], w, xin[:, u, k], start=(k == 0), stop=(k == KD - 1))
                    mm.then_inc(qk_done, 1)
                    for a in range(4):
                        for k in range(KD):
                            mm = pe.matmul(v_ps[:, u, a * 64:(a + 1) * 64], xin[:, u, k, a * P:(a + 1) * P],
                                           w_kv[:, k, 64:128], start=(k == 0), stop=(k == KD - 1))
                    mm.then_inc(v_done, 1)

                pe.wait_ge(w_in, 32)
                for u in range(2):
                    products(u, 0, u)
                with pe.Fori(1, NSEG // 2) as i:
                    for u in range(2):
                        pe.wait_ge(rest_done, i * 2 + u - 1)
                        pe.wait_ge(v_copied, i * 2 + u - 1)
                        products(i * 2 + u, i, u)

            @block.scalar
            def _(act):
                def split(n, u):
                    act.wait_ge(qk_done, n + 1)
                    act.activation(hi[:, u], qk_ps[:, u], ACT.Copy).then_inc(hi_done, 1)
                    act.wait_ge(v_done, n + 1)
                    act.activation(vout[:, u], v_ps[:, u, 0:256].rearrange("p (a d) -> p a d", d=64),
                                   ACT.Copy).then_inc(v_copied, 1)
                    act.wait_ge(rest_done, n + 1)
                    act.activation(mid[:, u], rest[:, u], ACT.Copy).then_inc(mid_done, 1)

                for u in range(2):
                    split(u, u)
                with act.Fori(1, NSEG // 2) as i:
                    for u in range(2):
                        act.wait_ge(stored[u], i * 64)
                        split(i * 2 + u, u)

            @block.vector
            def _(dve):
                with dve.Fori(0, NSEG // 2) as i:
                    for u in range(2):
                        n = i * 2 + u
                        dve.wait_ge(hi_done, n + 1)
                        dve.tensor_tensor(rest[:, u], qk_ps[:, u], hi[:, u], ALU.subtract).then_inc(rest_done, 1)

            @block.gpsimd
            def _(pool):
                with pool.Fori(0, NSEG // 2) as i:
                    for u in range(2):
                        n = i * 2 + u
                        pool.wait_ge(mid_done, n + 1)
                        pool.tensor_tensor(lo[:, u], rest[:, u], mid[:, u], ALU.subtract).then_inc(lo_done, 1)


QUADS, SB_PER_QUAD = SEQ // SEG, SEG // P
SBLK = SEQ // P
NG = BATCH * GROUPS
QK_PAIRS = ((0, 0), (0, 1), (1, 0), (1, 1), (0, 2), (2, 0))
KROWS = len(QK_PAIRS) * HD
SROWS = KROWS + 3
PRING = 8
M_LEAD = 1.1
LOADS = 16 * (2 * len(QK_PAIRS) + 1)


def attention_phase(nc, qk_parts, v_rows, shift_rows, ctx_rows, ident_f, ident_b, tri_st, tri_ts, later=()):
    m_units = []
    for i in range(SBLK):
        T = (i + 1) * P
        if T <= SEG:
            m_units += [(i, (m, m + 1), 0, T) for m in (0, 2)]
        else:
            for m in range(GS):
                m_units += [(i, (m,), t, min(1024, T - t)) for t in range(0, T, 1024)]
    NM = len(m_units) + 1
    steps = [(q, t) for q in range(QUADS) for t in range((q + 1) * SB_PER_QUAD)]
    NSTEP = len(steps)
    NE = NSTEP * GS

    def cols(q, t):
        return max(0, t - q * SB_PER_QUAD) * P

    schedule, m_cost, e_cost, mi, turn_at = [], 0, 0, 0, None
    m_total = sum(len(h) * k + 120 for _, h, _, k in m_units)
    e_total = sum(GS * (SEG - cols(q, t) + 150) for q, t in steps)
    for e in range(NE):
        q, t = steps[e // GS]
        e_cost += SEG - cols(q, t) + 150
        schedule.append(("scores", e))
        if mi < len(m_units) and m_cost / m_total < M_LEAD * e_cost / e_total:
            m_cost += len(m_units[mi][1]) * m_units[mi][3] + 120
            schedule.append(("max", mi))
            mi += 1
        if mi == len(m_units) and turn_at is None:
            turn_at = len(schedule) + 6
        if e % GS == 3 and e > GS:
            schedule.append(("values", e // GS - 1))
            if steps[e // GS - 1][1] == (steps[e // GS - 1][0] + 1) * SB_PER_QUAD - 1:
                schedule.append(("norm", steps[e // GS - 1][0]))
    schedule += [("values", NSTEP - 1), ("norm", QUADS - 1)]
    schedule.insert(turn_at, ("turn", 0))
    only_max = [("max", u) for u in range(len(m_units))] + [("turn", 0)]

    with ExitStack() as ctx:
        s = Space(nc, ctx, "att")
        NB = 3
        qa = [s.sb(f"qa{j}", [P, GS, SEQ], BF16) for j in range(NB)]
        ka = [s.sb(f"ka{j}", [P, SEQ], BF16) for j in range(NB)]
        va = [s.sb(f"va{j}", [P, SBLK, 2 * HD]) for j in range(NB)]
        prob = s.sb("prob", [P, PRING, SEG])
        mx = s.sb("mx", [P, GS, SBLK, 2])
        mrow = s.sb("mrow", [P, P])
        sh = s.sb("sh", [GS * SBLK, 3, P], BF16)
        sh_rest = s.sb("sh_rest", [GS * SBLK, P])
        num = s.sb("num", [P, 2, SEG])
        mx_ps = s.ps("mx_ps", [P, 2, 1024])
        st_ps = s.ps("st_ps", [P, 3, SEG])
        acc_ps = s.ps("acc_ps", [P, SEG])

        consts = s.sem("consts")
        loaded = [s.sem(f"loaded{j}") for j in range(NB)]
        mx_filled, mx_read = s.sem("mx_filled"), s.sem("mx_read")
        row_max, sh_hi, sh_res, sh_mid, sh_done = (s.sem(n) for n in ("row_max", "sh_hi", "sh_res", "sh_mid", "sh_done"))
        sh_out, sh_in = s.sem("sh_out"), [s.sem(f"sh_in{j}") for j in range(NB)]
        st_filled, exp_done, pv_done = s.sem("st_filled"), s.sem("exp_done"), s.sem("pv_done")
        num_done = s.sem("num_done")
        out_stored = [s.sem("out_stored0"), s.sem("out_stored1")]

        def groups(loop, run):
            run(0, None, 0, None)
            with loop(0, 2) as r:
                for u in range(3):
                    run(r * 3 + u + 1, r * 3 + u, (u + 1) % NB, u)
            run(NG - 1, NG - 2, (NG - 1) % NB, (NG - 2) % NB)
            run(None, NG - 1, None, (NG - 1) % NB)

        def order(jm, je):
            if je is None:
                return only_max
            return [x for x in schedule if jm is not None or x[0] not in ("max", "turn")]

        with nc.Block() as block:
            @block.sync
            def _(sp):
                def load(j, u):
                    b_, g_ = j // GROUPS, j % GROUPS
                    tok = b_ * SEQ
                    for r, (qp, kp) in enumerate(QK_PAIRS):
                        sp.dma_start(qa[u][r * HD:(r + 1) * HD],
                                     qk_parts[qp, bass.ds(g_ * GS * HD, GS * HD), bass.ds(tok, SEQ)]
                                     .rearrange("(m d) n -> d m n", d=HD)).then_inc(loaded[u], 16)
                        sp.dma_start(ka[u][r * HD:(r + 1) * HD],
                                     qk_parts[kp, bass.ds(D + g_ * HD, HD), bass.ds(tok, SEQ)]
                                     ).then_inc(loaded[u], 16)
                    sp.dma_start(va[u][:, :, 0:HD],
                                 v_rows[bass.ds(tok, SEQ), bass.ds(g_ * HD, HD)]
                                 .rearrange("(a p) d -> p a d", p=P)).then_inc(loaded[u], 16)

                def shift(j, u):
                    sp.wait_ge(sh_done, j + 1)
                    sp.dma_start(shift_rows.rearrange("k a p -> a k p"), sh[:]).then_inc(sh_out, 16)
                    sp.wait_ge(sh_out, 16 * j + 16)
                    sp.dma_start(qa[u][KROWS:SROWS], shift_rows.rearrange("k (m i) p -> k m (i p)", m=GS)
                                 ).then_inc(sh_in[u], 16)

                def store(j, q):
                    b_, g_ = j // GROUPS, j % GROUPS
                    sp.wait_ge(num_done, j * QUADS + q + 2)
                    sp.dma_start(ctx_rows[g_, :, bass.ds(b_ * SEQ + q * SEG, SEG)] if isinstance(j, int) else
                                 ctx_rows[bass.ds(g_, 1), :, bass.ds(b_ * SEQ + q * SEG, SEG)]
                                 .rearrange("o p n -> (o p) n"), num[:, q % 2]).then_inc(out_stored[q % 2], 16)

                load(0, 0)
                load(1, 1)
                load(2, 2)

                def run(jm, je, um, ue):
                    if je is not None:
                        for q in range(QUADS - 1):
                            store(je, q)
                    if jm is not None:
                        shift(jm, um)
                    if je is not None:
                        store(je, QUADS - 1)
                        if je + NB < NG:
                            load(je + NB, ue)

                for r in range(NG + 1):
                    run(r if r < NG else None, r - 1 if r else None, r % NB, (r - 1) % NB)
                for u in range(2):
                    sp.wait_ge(out_stored[u], 16 + 16 * NG * QUADS // 2)

            @block.tensor
            def _(pe):
                def masked(ps, at, tri, stop=True):
                    return pe.matmul(ps[:, at:at + P], ident_b[:], tri[:], start=False, stop=stop)

                def max_unit(j, u, n):
                    i, heads, t0, T = m_units[n]
                    if n == 0:
                        pe.wait_ge(mx_read, j * NM + 1)
                    elif n >= 2:
                        pe.wait_ge(mx_read, j * NM + n)
                    for x, m in enumerate(heads):
                        for c in range(0, T, SEG):
                            w = min(SEG, T - c)
                            ps = mx_ps[:, n % 2, x * SEG + c:x * SEG + c + w]
                            diagonal = t0 + c + w == (i + 1) * P
                            mm = pe.matmul(ps, qa[u][0:KROWS, m, i * P:(i + 1) * P], ka[u][0:KROWS, t0 + c:t0 + c + w],
                                           start=True, stop=not diagonal)
                            if diagonal:
                                mm = masked(ps, w - P, tri_st)
                    mm.then_inc(mx_filled, 1)

                def turn_max(j):
                    pe.wait_ge(row_max, j + 1)
                    pe.wait_ge(mx_read, j * NM + NM - 1)
                    pe.transpose(mx_ps[:, 0, 0:P], mrow[:], ident_f[:]).then_inc(mx_filled, 1)

                def scores(j, u, e):
                    q, t = steps[e // GS]
                    c0, m = cols(q, t), e % GS
                    pe.wait_ge(exp_done, j * NE + (e - 2 if e >= 3 else 0) + 1)
                    ps = st_ps[:, e % 3, c0:SEG]
                    diagonal = t >= q * SB_PER_QUAD
                    mm = pe.matmul(ps, ka[u][0:SROWS, t * P:(t + 1) * P], qa[u][0:SROWS, m, q * SEG + c0:(q + 1) * SEG],
                                   start=True, stop=not diagonal)
                    if diagonal:
                        mm = masked(ps, 0, tri_ts)
                    mm.then_inc(st_filled, 1)

                def values(j, u, n):
                    q, t = steps[n]
                    c0 = cols(q, t)
                    if t == 0:
                        pe.wait_ge(num_done, j * QUADS + q + 1)
                    pe.wait_ge(exp_done, j * NE + (n + 1) * GS + 1)
                    for m in range(GS):
                        mm = pe.matmul(acc_ps[32 * m:32 * m + 32, c0:SEG], va[u][:, t, :],
                                       prob[:, (n * GS + m) % PRING, c0:SEG], start=(t == 0),
                                       stop=(t == (q + 1) * SB_PER_QUAD - 1))
                    mm.then_inc(pv_done, 1)

                def run(jm, je, um, ue):
                    if jm is not None:
                        pe.wait_ge(loaded[um], LOADS * (jm // NB + 1) if isinstance(jm, int) else LOADS * ((jm + 0) // NB + 1))
                    if je is not None:
                        pe.wait_ge(sh_in[ue], 16 * (je // NB + 1))
                    for kind, n in order(jm, je):
                        if kind == "max":
                            max_unit(jm, um, n)
                        elif kind == "turn":
                            turn_max(jm)
                        elif kind == "scores":
                            scores(je, ue, n)
                        elif kind == "values":
                            values(je, ue, n)

                pe.sem_inc(pv_done, 2)
                pe.wait_ge(consts, 3)
                groups(pe.Fori, run)

            @block.scalar
            def _(act):
                act.sem_inc(exp_done, 1)
                act.sem_inc(num_done, 1)
                for u in range(2):
                    act.sem_inc(out_stored[u], 16)
                for u in range(NB):
                    act.wait_ge(loaded[u], LOADS)
                for dst, src, done in later:
                    act.dma_start(dst, src).then_inc(done, 16)

                def exps(j, e):
                    c0 = cols(*steps[e // GS])
                    if e % GS == 0:
                        act.wait_ge(pv_done, j * NSTEP + e // GS + 1)
                    act.wait_ge(st_filled, j * NE + e + 1)
                    act.activation(prob[:, e % PRING, c0:SEG], st_ps[:, e % 3, c0:SEG], ACT.Exp,
                                   scale=HD ** -0.5).then_inc(exp_done, 1)

                def norm(j, q):
                    act.wait_ge(pv_done, j * NSTEP + (q + 1) * (q + 2) * SB_PER_QUAD // 2 + 2)
                    act.wait_ge(out_stored[q % 2], (j * (QUADS // 2) + q // 2) * 16 + 16)
                    act.activation(num[:, q % 2], acc_ps[:], ACT.Copy).then_inc(num_done, 1)

                def run(jm, je, um, ue):
                    if je is not None:
                        for kind, n in order(jm, je):
                            if kind == "scores":
                                exps(je, n)
                            elif kind == "norm":
                                norm(je, n)

                groups(act.Fori, run)

            @block.vector
            def _(dve):
                dve.sem_inc(mx_read, 1)
                for u in range(NB):
                    dve.memset(ka[u][KROWS:SROWS], 1.0)
                    dve.memset(va[u][:, :, HD:2 * HD], 1.0)
                dve.memset(mrow[:], 0.0)
                dve.memset(mx[:], -3.0e38).then_inc(consts, 3)

                def max_unit(j, n):
                    i, heads, t0, T = m_units[n]
                    dve.wait_ge(mx_filled, j * NM + n + 1)
                    if len(heads) == 2:
                        src = mx_ps[:, n % 2].rearrange("p (h n) -> p h n", n=SEG)[:, :, 0:T]
                    else:
                        src = mx_ps[:, n % 2:n % 2 + 1, 0:T]
                    dve.tensor_reduce(mx[:, heads[0]:heads[-1] + 1, i, int(t0 > 0)], src, AX.X, ALU.max).then_inc(mx_read, 1)

                def shift(j):
                    dve.wait_ge(mx_read, j * NM + NM)
                    dve.tensor_reduce(mrow[:, 0:GS * SBLK], mx[:].rearrange("p m i c -> p (m i) c"), AX.X, ALU.max).then_inc(row_max, 1)
                    dve.wait_ge(mx_filled, j * NM + NM)
                    if not (isinstance(j, int) and j == 0):
                        dve.wait_ge(sh_out, 16 * j)
                    t = mx_ps[0:GS * SBLK, 0, 0:P]
                    dve.tensor_scalar(sh[:, 0], t, -1.0, None, ALU.mult).then_inc(sh_hi, 1)
                    dve.wait_ge(sh_hi, j + 1)
                    dve.scalar_tensor_tensor(sh_rest[:], t, -1.0, sh[:, 0], ALU.mult, ALU.subtract).then_inc(mx_read, 1)
                    dve.wait_ge(mx_read, j * NM + NM + 1)
                    dve.tensor_copy(sh[:, 1], sh_rest[:]).then_inc(sh_mid, 1)
                    dve.wait_ge(sh_mid, j + 1)
                    dve.tensor_tensor(sh[:, 2], sh_rest[:], sh[:, 1], ALU.subtract).then_inc(sh_done, 1)

                def run(jm, je, um, ue):
                    for kind, n in order(jm, je):
                        if kind == "max":
                            max_unit(jm, n)
                        elif kind == "turn":
                            shift(jm)

                groups(dve.Fori, run)


NSEG = TOK // SEG
TPS = SEG // P
TILES = TOK // P
E = 8


def denominators_phase(nc, ctx_rows, inv_rows):
    with ExitStack() as ctx:
        s = Space(nc, ctx, "den")
        den = s.sb("den", [P, SEG])
        inv = s.sb("inv", [P, SEG])
        den_in, inv_done, inv_out = s.sem("den_in"), s.sem("inv_done"), s.sem("inv_out")
        with nc.Block() as block:
            @block.sync
            def _(sp):
                sp.dma_start(den[:],
                             ctx_rows.rearrange("g (m r) (a n) -> r (g m) a n", r=32, n=SEG)[HD]).then_inc(den_in, 16)
                sp.wait_ge(inv_done, 1)
                sp.dma_start(inv_rows.rearrange("h (a n) -> (h a) n", n=SEG), inv[:]).then_inc(inv_out, 16)
                sp.wait_ge(inv_out, 16)

            @block.vector
            def _(dve):
                dve.wait_ge(den_in, 16)
                dve.reciprocal(inv[:], den[:]).then_inc(inv_done, 1)


def out_project_phase(nc, ctx_rows, inv_rows, x_rows, wo, wr, br_sb, ident_f, scores_sb, x1_rows):
    with ExitStack() as ctx:
        s = Space(nc, ctx, "wo")
        w_o = s.sb("w_o", [P, GROUPS, D])
        w_r = s.sb("w_r", [P, KD, E])
        num = [s.sb(f"num{u}", [P, GROUPS, SEG]) for u in range(2)]
        inv = [s.sb(f"inv{u}", [P, GROUPS, SEG]) for u in range(2)]
        cn = [s.sb(f"cn{u}", [P, GROUPS, SEG]) for u in range(2)]
        xr = [s.sb(f"xr{u}", [P, TPS, D]) for u in range(2)]
        y = s.sb("y", [P, 2, TPS, D])
        stats = s.sb("stats", [P, 2, TPS, 6])
        mv = s.sb("mv", [P, 2, TPS, 2])
        var = s.sb("var", [P, 2, TPS])
        std = s.sb("std", [P, 2, TPS])
        rstd = s.sb("rstd", [P, 2, TPS])
        rough, nr, nr2 = (s.sb(n, [P, 2, TPS]) for n in ("rough", "nr", "nr2"))
        st_seen, newton = s.sem("st_seen"), s.sem("newton")
        x1 = s.sb("x1", [P, 2, TPS, D])
        x1T = s.sb("x1T", [P, 2, KD, SEG])
        y_ps = s.ps("y_ps", [P, 2, 2, SEG])
        t_ps = s.ps("t_ps", [P, KD, SEG])
        r_ps = s.ps("r_ps", [P, 2, SEG])
        w_in, seg_in, xr_in = s.sem("w_in"), [s.sem("seg_in0"), s.sem("seg_in1")], [s.sem("xr_in0"), s.sem("xr_in1")]
        cn_done, y_done, sum_done, st_done, mv_done, var_done, std_done, rstd_done, x1_done = (
            s.sem(n) for n in ("cn", "y", "sum", "st", "mv", "var", "std", "rstd", "x1"))
        t_done, xT_done, r_done, r_read = (s.sem(n) for n in ("t", "xT", "r", "r_read"))
        stored = [s.sem("stored0"), s.sem("stored1")]

        with nc.Block() as block:
            @block.sync
            def _(sp):
                def load_ctx(n, u):
                    sp.dma_start(num[u][:], ctx_rows[:, :, bass.ds(n * SEG, SEG)].rearrange("g p n -> p g n")
                                 ).then_inc(seg_in[u], 16)
                    for m in range(GS):
                        sp.dma_start(inv[u][32 * m:32 * m + 32],
                                     inv_rows.rearrange("(g m) n -> m g n", m=GS)[m:m + 1, :, bass.ds(n * SEG, SEG)]
                                     .broadcast_to([32, GROUPS, SEG])).then_inc(seg_in[u], 16)

                def load_x(n, u):
                    sp.dma_start(xr[u][:], x_rows[bass.ds(n * SEG, SEG)].rearrange("(a p) d -> p a d", p=P)
                                 ).then_inc(xr_in[u], 16)

                def store(n, u):
                    sp.wait_ge(x1_done, (n + 1) * TPS)
                    sp.dma_start(x1_rows[bass.ds(n * SEG, SEG)].rearrange("(a p) d -> p a d", p=P), x1[:, u]
                                 ).then_inc(stored[u], 16)

                sp.dma_start(w_o[:], wo.rearrange("g p n -> p g n")).then_inc(w_in, 16)
                sp.dma_start(w_r[:], wr.rearrange("(k p) e -> p k e", p=P)).then_inc(w_in, 16)
                for u in range(2):
                    load_ctx(u, u)
                    load_x(u, u)
                with sp.Fori(0, NSEG // 2 - 1) as i:
                    for u in range(2):
                        sp.wait_ge(cn_done, i * 2 + u + 1)
                        load_ctx(i * 2 + u + 2, u)
                        sp.wait_ge(sum_done, i * 2 + u + 1)
                        load_x(i * 2 + u + 2, u)
                        store(i * 2 + u, u)
                for u in range(2):
                    store(NSEG - 2 + u, u)
                for u in range(2):
                    sp.wait_ge(stored[u], 16 * NSEG // 2)

            @block.vector
            def _(dve):
                def scale(n, u, i):
                    dve.wait_ge(seg_in[u], i * 80 + 80)
                    dve.tensor_tensor(cn[u][:], num[u][:], inv[u][:], ALU.mult).then_inc(cn_done, 1)

                def norm(n, u, i):
                    dve.wait_ge(y_done, n + 1)
                    dve.wait_ge(xr_in[u], i * 16 + 16)
                    dve.tensor_tensor(y[:, u], y_ps[:, u].rearrange("p c (a d) -> p (c a) d", d=D), xr[u][:], ALU.add
                                      ).then_inc(sum_done, 1)
                    dve.wait_ge(sum_done, n + 1)
                    for a in range(TPS):
                        dve.bn_stats(stats[:, u, a], y[:, u, a]).then_inc(st_done, 1)
                    dve.wait_ge(st_done, n * TPS + TPS)
                    dve.sem_inc(st_seen, 1)
                    for a in range(TPS):
                        dve.bn_aggr(mv[:, u, a], stats[:, u, a]).then_inc(mv_done, 1)
                    dve.wait_ge(mv_done, n * TPS + TPS)
                    dve.tensor_scalar(var[:, u], mv[:, u, :, 1], EPS, None, ALU.add).then_inc(var_done, 1)
                    dve.wait_ge(std_done, n + 1)
                    dve.reciprocal(rough[:, u], std[:, u]).then_inc(newton, 1)
                    dve.wait_ge(newton, n * 4 + 1)
                    dve.tensor_tensor(nr[:, u], var[:, u], rough[:, u], ALU.mult).then_inc(newton, 1)
                    dve.wait_ge(newton, n * 4 + 2)
                    dve.tensor_tensor(nr2[:, u], nr[:, u], rough[:, u], ALU.mult).then_inc(newton, 1)
                    dve.wait_ge(newton, n * 4 + 3)
                    dve.tensor_scalar(nr[:, u], nr2[:, u], -0.5, 1.5, ALU.mult, ALU.add).then_inc(newton, 1)
                    dve.wait_ge(newton, n * 4 + 4)
                    dve.tensor_tensor(rstd[:, u], rough[:, u], nr[:, u], ALU.mult).then_inc(rstd_done, 1)
                    dve.wait_ge(rstd_done, n + 1)
                    for a in range(TPS):
                        dve.tensor_scalar(x1[:, u, a], y[:, u, a], mv[:, u, a, 0:1], rstd[:, u, a:a + 1],
                                          ALU.subtract, ALU.mult).then_inc(x1_done, 1)

                def route(n, u):
                    dve.wait_ge(r_done, n + 1)
                    dve.tensor_tensor(scores_sb[:, bass.ds(n * TPS, TPS), :],
                                      r_ps[:, u, 0:TPS * E].rearrange("p (a e) -> p a e", e=E),
                                      br_sb[:], ALU.add).then_inc(r_read, 1)

                scale(0, 0, 0)
                scale(1, 1, 0)
                norm(0, 0, 0)
                scale(2, 0, 1)
                norm(1, 1, 0)
                with dve.Fori(1, NSEG // 2 - 1) as i:
                    for u in range(2):
                        n = i * 2 + u
                        scale(n + 1, 1 - u, i + u)
                        route(n - 2, u)
                        dve.wait_ge(stored[u], i * 16)
                        norm(n, u, i)
                for n in (NSEG - 2, NSEG - 1):
                    if n == NSEG - 2:
                        scale(n + 1, 1, NSEG // 2 - 1)
                    route(n - 2, n % 2)
                    dve.wait_ge(stored[n % 2], (NSEG // 2 - 1) * 16)
                    norm(n, n % 2, NSEG // 2 - 1)
                for u in range(2):
                    route(NSEG - 2 + u, u)

            @block.tensor
            def _(pe):
                def out(n, u):
                    pe.wait_ge(cn_done, n + 1)
                    for a in range(TPS):
                        for g in range(GROUPS):
                            mm = pe.matmul(y_ps[:, u, a // 2, (a % 2) * D:(a % 2 + 1) * D], cn[u][:, g, a * P:(a + 1) * P],
                                           w_o[:, g], start=(g == 0), stop=(g == GROUPS - 1))
                    mm.then_inc(y_done, 1)

                def turn(n, u):
                    pe.wait_ge(x1_done, n * TPS + TPS)
                    for k in range(KD):
                        for a in range(TPS):
                            mm = pe.transpose(t_ps[:, k, a * P:(a + 1) * P], x1[:, u, a, k * P:(k + 1) * P], ident_f[:])
                    mm.then_inc(t_done, 1)

                def route(n, u):
                    pe.wait_ge(xT_done, n + 1)
                    for a in range(TPS):
                        for k in range(KD):
                            mm = pe.matmul(r_ps[:, u, a * E:(a + 1) * E], x1T[:, u, k, a * P:(a + 1) * P], w_r[:, k],
                                           start=(k == 0), stop=(k == KD - 1))
                    mm.then_inc(r_done, 1)

                pe.wait_ge(w_in, 32)
                out(0, 0)
                out(1, 1)
                with pe.Fori(0, NSEG // 2 - 1) as i:
                    for u in range(2):
                        n = i * 2 + u
                        turn(n, u)
                        pe.wait_ge(sum_done, n + 1)
                        out(n + 2, u)
                        route(n, u)
                for u in range(2):
                    turn(NSEG - 2 + u, u)
                    route(NSEG - 2 + u, u)

            @block.scalar
            def _(act):
                with act.Fori(0, NSEG // 2) as i:
                    for u in range(2):
                        n = i * 2 + u
                        act.wait_ge(var_done, n + 1)
                        act.activation(std[:, u], var[:, u], ACT.Sqrt).then_inc(std_done, 1)
                        act.wait_ge(t_done, n + 1)
                        act.activation(x1T[:, u], t_ps[:], ACT.Copy).then_inc(xT_done, 1)


def routing_phase(nc, scores_sb, pos_sb, owner_sb, ident_b, before, ones_b, slots_iota, ranks, n_slots):
    with ExitStack() as ctx:
        s = Space(nc, ctx, "route")
        best = s.sb("best", [P, TILES])
        hit = s.sb("hit", [P, TILES, E])
        first = s.sb("first", [P, TILES])
        chosen = s.sb("chosen", [P, TILES, E])
        chosen_b = s.sb("chosen_b", [P, TILES, E], BF16)
        total = s.sb("total", [P, TILES, E])
        upto = s.sb("upto", [P, TILES, E])
        one = s.sb("one", [P, TILES])
        cnt = s.sb("cnt", [P, E], I32)
        cnt2 = s.sb("cnt2", [P, E], I32)
        tiles = s.sb("tiles", [P, E])
        end = s.sb("end", [P, E])
        start = s.sb("start", [P, E])
        row = s.sb("row", [P, TILES, E])
        posf = s.sb("posf", [P, TILES])
        own = [s.sb(f"own{i}", [1, n_slots]) for i in range(2)]
        before_ps = s.ps("before_ps", [P, SEG])
        total_ps = s.ps("total_ps", [P, SEG])
        chain, counted, chosen_done = s.sem("chain"), s.sem("counted"), s.sem("chosen")

        with nc.Block() as block:
            @block.tensor
            def _(pe):
                pe.wait_ge(chosen_done, 1)
                c = chosen_b[:].rearrange("p t e -> p (t e)")
                pe.matmul(before_ps[:, 0:TILES * E], before[:], c, start=True, stop=True).then_inc(counted, 1)
                pe.matmul(total_ps[:, 0:TILES * E], ones_b[:], c, start=True, stop=True).then_inc(counted, 1)

            @block.vector
            def _(dve):
                n = [0]

                def then(ins):
                    n[0] += 1
                    ins.then_inc(chain, 1)
                    dve.wait_ge(chain, n[0])

                def over_e(ap):
                    return ap.unsqueeze(2).broadcast_to([P, TILES, E])

                then(dve.tensor_reduce(best[:], scores_sb[:], AX.X, ALU.max))
                then(dve.tensor_tensor(hit[:], scores_sb[:], over_e(best[:]), ALU.is_ge))
                then(dve.tensor_tensor(hit[:], hit[:], ranks[:].unsqueeze(1).broadcast_to([P, TILES, E]), ALU.mult))
                then(dve.tensor_reduce(first[:], hit[:], AX.X, ALU.max))
                then(dve.tensor_tensor(chosen[:], hit[:], over_e(first[:]), ALU.is_equal))
                dve.tensor_copy(chosen_b[:], chosen[:]).then_inc(chosen_done, 1)
                then(dve.memset(one[:], 1.0))
                dve.wait_ge(counted, 2)
                then(dve.tensor_copy(total[:].rearrange("p t e -> p (t e)"), total_ps[:, 0:TILES * E]))
                for e in range(E):
                    i = dve.tensor_tensor_scan(upto[:, :, e], one[:], total[:, :, e], 0.0, ALU.mult, ALU.add)
                then(i)
                then(dve.tensor_scalar(cnt[:], upto[:, TILES - 1, :], float(P - 1), None, ALU.add))
                then(dve.tensor_scalar(cnt2[:], cnt[:], 7, None, ALU.logical_shift_right))
                then(dve.tensor_copy(tiles[:], cnt2[:]))
                then(dve.tensor_tensor_scan(end[:], one[:, 0:E], tiles[:], 0.0, ALU.mult, ALU.add))
                then(dve.tensor_tensor(start[:], end[:], tiles[:], ALU.subtract))
                then(dve.tensor_scalar(start[:], start[:], float(P), None, ALU.mult))
                then(dve.tensor_tensor(row[:], upto[:], total[:], ALU.subtract))
                then(dve.tensor_tensor(row[:], row[:], start[:].unsqueeze(1).broadcast_to([P, TILES, E]), ALU.add))
                then(dve.tensor_tensor(row[:].rearrange("p t e -> p (t e)"), row[:].rearrange("p t e -> p (t e)"),
                                       before_ps[:, 0:TILES * E], ALU.add))
                then(dve.tensor_tensor(row[:], row[:], chosen[:], ALU.mult))
                then(dve.tensor_reduce(posf[:], row[:], AX.X, ALU.add))
                then(dve.tensor_copy(pos_sb[:], posf[:]))
                then(dve.tensor_scalar(own[0][:], slots_iota[:], end[0:1, 0:1], None, ALU.is_ge))
                for e in range(1, E):
                    then(dve.scalar_tensor_tensor(own[e % 2][:], slots_iota[:], end[0:1, e:e + 1], own[(e - 1) % 2][:],
                                                  ALU.is_ge, ALU.add))
                then(dve.tensor_scalar(own[0][:], own[1][:], float(E - 1), None, ALU.min))
                then(dve.tensor_copy(owner_sb[:], own[0][:]))


F = 1024
FK = F // P


def scatter_phase(nc, x1, x1_in, pos_sb, sorted_rows, sorted_zeroed, zeroed_value):
    with ExitStack() as ctx:
        s = Space(nc, ctx, "scat")
        placed = s.sem("placed")
        with nc.Block() as block:
            @block.gpsimd
            def _(pool):
                pool.wait_ge(x1_in, 16)
                pool.wait_ge(sorted_zeroed, zeroed_value)
                for t in range(TILES):
                    pool.indirect_dma_start(sorted_rows, bass.IndirectOffsetOnAxis(pos_sb[:, t:t + 1], 0),
                                            x1[:, t], None).then_inc(placed, 16)
                pool.wait_ge(placed, 16 * TILES)


def experts_phase(nc, n_slots, sorted_rows, done_rows, owner_sb, w1, w2, b1, b2, weights_in, weights_value, b2_in, ident_f):
    with ExitStack() as ctx:
        s = Space(nc, ctx, "moe")
        x = s.sb("x", [P, 2, D])
        xT = s.sb("xT", [P, 2, KD, P])
        hb = s.sb("hb", [P, 2, F])
        h = s.sb("h", [P, 2, F])
        hT = s.sb("hT", [P, 2, FK, P])
        y = s.sb("y", [P, 2, D])
        x_ps = s.ps("x_ps", [P, SEG])
        h_ps = s.ps("h_ps", [P, 2, F])
        hT_ps = s.ps("hT_ps", [P, 2, SEG])
        y_ps = s.ps("y_ps", [P, SEG])
        x_in = [s.sem("x_in0"), s.sem("x_in1")]
        x_turned, xT_done, up_done, bias_done, h_done, h_turned, hT_lo, hT_hi, down_done, y_done = (
            s.sem(n) for n in ("x_turned", "xT", "up", "bias", "h", "h_turned", "hT_lo", "hT_hi", "down", "y"))
        y_out = [s.sem("y_out0"), s.sem("y_out1")]
        N = n_slots
        PAIRS = (N - 2) // 2
        TAIL = range(2 * PAIRS, N)

        with nc.Block() as block:
            @block.sync
            def _(sp):
                def load(row, u):
                    sp.dma_start(x[:, u], sorted_rows[bass.ds(row, P)]).then_inc(x_in[u], 16)

                def store(j, row, u):
                    sp.wait_ge(y_done, j + 2)
                    sp.dma_start(done_rows[bass.ds(row, P)], y[:, u]).then_inc(y_out[u], 16)

                load(0, 0)
                load(P, 1)
                with sp.Fori(0, PAIRS) as i:
                    for u in range(2):
                        row, row2 = sp.snap(i * 2 * P + u * P), sp.snap(i * 2 * P + (u + 2) * P)
                        sp.wait_ge(x_turned, i * 2 + u + 1)
                        load(row2, u)
                        store(i * 2 + u, row, u)
                for j in TAIL:
                    if j + 2 < N:
                        sp.wait_ge(x_turned, j + 1)
                        load((j + 2) * P, j % 2)
                    store(j, j * P, j % 2)
                for u in range(2):
                    sp.wait_ge(y_out[u], 16 + 16 * len(range(u, N, 2)))

            @block.tensor
            def _(pe):
                def turn_x(j, u, i):
                    pe.wait_ge(x_in[u], i * 16 + 16)
                    for k in range(KD):
                        mm = pe.transpose(x_ps[:, k * P:(k + 1) * P], x[:, u, k * P:(k + 1) * P], ident_f[:])
                    mm.then_inc(x_turned, 1)

                def up(j, u):
                    e = pe.value_load(owner_sb[0:1, bass.ds(j, 1)], min_val=0, max_val=E - 1)
                    pe.wait_ge(xT_done, j + 1)
                    for c in range(F // SEG):
                        for k in range(KD):
                            mm = pe.matmul(h_ps[:, u, c * SEG:(c + 1) * SEG], xT[:, u, k],
                                           w1[:, bass.ds(e * KD + k, 1), c * SEG:(c + 1) * SEG].rearrange("p o n -> p (o n)"),
                                           start=(k == 0), stop=(k == KD - 1))
                    mm.then_inc(up_done, 1)

                def turn_h(j, u):
                    pe.wait_ge(h_done, j + 1)
                    for c in range(FK):
                        mm = pe.transpose(hT_ps[:, c // 4, (c % 4) * P:(c % 4 + 1) * P], h[:, u, c * P:(c + 1) * P], ident_f[:])
                        if c % 4 == 3:
                            mm.then_inc(h_turned, 1)

                def down(j, u):
                    e = pe.value_load(owner_sb[0:1, bass.ds(j, 1)], min_val=0, max_val=E - 1)
                    pe.wait_ge(y_done, j + 1)
                    for c in range(FK):
                        if c % 4 == 0:
                            pe.wait_ge(hT_hi if c else hT_lo, j + 1)
                        mm = pe.matmul(y_ps[:, 0:D], hT[:, u, c],
                                       w2[:, bass.ds(e * FK + c, 1), :].rearrange("p o n -> p (o n)"),
                                       start=(c == 0), stop=(c == FK - 1))
                    mm.then_inc(down_done, 1)

                def cycle(j, u, i, up_next, turn_next):
                    turn_h(j, u)
                    if up_next:
                        up(j + 1, 1 - u)
                    if turn_next:
                        turn_x(j + 2, u, i + 1)
                    down(j, u)

                pe.wait_ge(weights_in, weights_value)
                turn_x(0, 0, 0)
                up(0, 0)
                turn_x(1, 1, 0)
                with pe.Fori(0, PAIRS) as i:
                    for u in range(2):
                        cycle(i * 2 + u, u, i, True, True)
                for j in TAIL:
                    cycle(j, j % 2, j // 2, j + 1 < N, j + 2 < N)

            @block.scalar
            def _(act):
                def copy_x(j, u):
                    act.wait_ge(x_turned, j + 1)
                    act.activation(xT[:, u].rearrange("p k n -> p (k n)"), x_ps[:, 0:KD * P], ACT.Copy).then_inc(xT_done, 1)

                def copy_h(j, u):
                    act.wait_ge(h_turned, j * 2 + 1)
                    act.activation(hT[:, u, 0:4].rearrange("p c n -> p (c n)"), hT_ps[:, 0], ACT.Copy).then_inc(hT_lo, 1)

                def gelu(j, u):
                    act.wait_ge(bias_done, j + 1)
                    act.activation(h[:, u], hb[:, u], ACT.Gelu).then_inc(h_done, 1)

                copy_x(0, 0)
                copy_x(1, 1)
                gelu(0, 0)
                with act.Fori(0, PAIRS) as i:
                    for u in range(2):
                        j = i * 2 + u
                        copy_h(j, u)
                        copy_x(j + 2, u)
                        gelu(j + 1, 1 - u)
                for j in TAIL:
                    copy_h(j, j % 2)
                    if j + 2 < N:
                        copy_x(j + 2, j % 2)
                    if j + 1 < N:
                        gelu(j + 1, 1 - j % 2)

            @block.vector
            def _(dve):
                def bias(j, u):
                    e = dve.value_load(owner_sb[0:1, bass.ds(j, 1)], min_val=0, max_val=E - 1)
                    dve.wait_ge(up_done, j + 1)
                    dve.tensor_tensor(hb[:, u], h_ps[:, u], b1[:, bass.ds(e, 1), :].rearrange("p o n -> p (o n)"), ALU.add
                                      ).then_inc(bias_done, 1)

                def copy_h(j, u):
                    dve.wait_ge(h_turned, j * 2 + 2)
                    dve.tensor_copy(hT[:, u, 4:8].rearrange("p c n -> p (c n)"), hT_ps[:, 1]).then_inc(hT_hi, 1)

                def out(j, u, i):
                    e = dve.value_load(owner_sb[0:1, bass.ds(j, 1)], min_val=0, max_val=E - 1)
                    dve.wait_ge(down_done, j + 1)
                    dve.wait_ge(y_out[u], i * 16 + 16)
                    dve.tensor_tensor(y[:, u], y_ps[:, 0:D], b2[:, bass.ds(e, 1), :].rearrange("p o n -> p (o n)"), ALU.add
                                      ).then_inc(y_done, 1)

                dve.sem_inc(y_done, 1)
                for u in range(2):
                    dve.sem_inc(y_out[u], 16)
                dve.wait_ge(weights_in, weights_value)
                bias(0, 0)
                dve.wait_ge(b2_in, 16)
                with dve.Fori(0, PAIRS) as i:
                    for u in range(2):
                        j = i * 2 + u
                        copy_h(j, u)
                        bias(j + 1, 1 - u)
                        out(j, u, i)
                for j in TAIL:
                    copy_h(j, j % 2)
                    if j + 1 < N:
                        bias(j + 1, 1 - j % 2)
                    out(j, j % 2, j // 2)


def layernorm_buffers(s, width):
    b = {"stats": s.sb("ln_stats", [P, 2, width, 6]), "mv": s.sb("ln_mv", [P, 2, width, 2])}
    for n in ("var", "std", "rough", "nr", "nr2", "rstd"):
        b[n] = s.sb(f"ln_{n}", [P, 2, width])
    for n in ("st_done", "st_seen", "mv_done", "var_done", "std_done", "newton", "rstd_done", "out_done"):
        b[n] = s.sem(f"ln_{n}")
    return b


def layernorm(dve, b, n, u, y, out, width):
    layernorm_stats(dve, b, n, u, y, width)
    layernorm_apply(dve, b, n, u, y, out, width)


def layernorm_stats(dve, b, n, u, y, width):
    for a in range(width):
        dve.bn_stats(b["stats"][:, u, a], y[:, a]).then_inc(b["st_done"], 1)
    dve.wait_ge(b["st_done"], n * width + width)
    dve.sem_inc(b["st_seen"], 1)
    for a in range(width):
        dve.bn_aggr(b["mv"][:, u, a], b["stats"][:, u, a]).then_inc(b["mv_done"], 1)
    dve.wait_ge(b["mv_done"], n * width + width)
    dve.tensor_scalar(b["var"][:, u], b["mv"][:, u, :, 1], EPS, None, ALU.add).then_inc(b["var_done"], 1)


def layernorm_apply(dve, b, n, u, y, out, width):
    layernorm_scale(dve, b, n, u)
    for a in range(width):
        dve.tensor_scalar(out[:, a], y[:, a], b["mv"][:, u, a, 0:1], b["rstd"][:, u, a:a + 1],
                          ALU.subtract, ALU.mult).then_inc(b["out_done"], 1)


def layernorm_scale(dve, b, n, u):
    var, rough, nr, nr2, rstd = (b[x][:, u] for x in ("var", "rough", "nr", "nr2", "rstd"))
    dve.wait_ge(b["std_done"], n + 1)
    dve.reciprocal(rough, b["std"][:, u]).then_inc(b["newton"], 1)
    dve.wait_ge(b["newton"], n * 4 + 1)
    dve.tensor_tensor(nr, var, rough, ALU.mult).then_inc(b["newton"], 1)
    dve.wait_ge(b["newton"], n * 4 + 2)
    dve.tensor_tensor(nr2, nr, rough, ALU.mult).then_inc(b["newton"], 1)
    dve.wait_ge(b["newton"], n * 4 + 3)
    dve.tensor_scalar(nr, nr2, -0.5, 1.5, ALU.mult, ALU.add).then_inc(b["newton"], 1)
    dve.wait_ge(b["newton"], n * 4 + 4)
    dve.tensor_tensor(rstd, rough, nr, ALU.mult).then_inc(b["rstd_done"], 1)
    dve.wait_ge(b["rstd_done"], n + 1)


def layernorm_root(act, b, n, u):
    act.wait_ge(b["var_done"], n + 1)
    act.activation(b["std"][:, u], b["var"][:, u], ACT.Sqrt).then_inc(b["std_done"], 1)


def combine_phase(nc, x1_rows, done_rows, pos_sb, ident_f, x2_rows, x2T_rows, later=()):
    with ExitStack() as ctx:
        s = Space(nc, ctx, "comb")
        y = s.sb("y", [P, 2, TPS, D])
        x1 = s.sb("x1", [P, 2, TPS, D])
        sm = s.sb("sm", [P, 2, TPS, D])
        x2 = s.sb("x2", [P, 2, TPS, D])
        x2T = s.sb("x2T", [P, 2, KD, SEG])
        ln = layernorm_buffers(s, TPS)
        t_ps = s.ps("t_ps", [P, 2, KD, SEG])
        y_in, x_in = [s.sem("y_in0"), s.sem("y_in1")], [s.sem("x_in0"), s.sem("x_in1")]
        sum_done, turned, copied = s.sem("sum_done"), s.sem("turned"), s.sem("copied")
        stored = [s.sem("stored0"), s.sem("stored1")]
        with nc.Block() as block:
            @block.gpsimd
            def _(pool):
                for n in range(NSEG):
                    u = n % 2
                    if n >= 2:
                        pool.wait_ge(sum_done, n - 1)
                    for a in range(TPS):
                        t = n * TPS + a
                        pool.indirect_dma_start(y[:, u, a], None, done_rows,
                                                bass.IndirectOffsetOnAxis(pos_sb[:, t:t + 1], 0)).then_inc(y_in[u], 16)

            @block.sync
            def _(sp):
                def load(n, u):
                    sp.dma_start(x1[:, u], x1_rows[bass.ds(n * SEG, SEG)].rearrange("(a p) d -> p a d", p=P)
                                 ).then_inc(x_in[u], 16)

                def store(n, u):
                    sp.wait_ge(copied, n + 1)
                    sp.dma_start(x2_rows[bass.ds(n * SEG, SEG)].rearrange("(a p) d -> p a d", p=P), x2[:, u]
                                 ).then_inc(stored[u], 16)
                    sp.dma_start(x2T_rows.rearrange("(k p) n -> p k n", p=P)[:, :, bass.ds(n * SEG, SEG)], x2T[:, u]
                                 ).then_inc(stored[u], 16)

                load(0, 0)
                load(1, 1)
                with sp.Fori(0, NSEG // 2 - 1) as i:
                    for u in range(2):
                        sp.wait_ge(sum_done, i * 2 + u + 1)
                        load(i * 2 + u + 2, u)
                        store(i * 2 + u, u)
                for u in range(2):
                    store(NSEG - 2 + u, u)
                for u in range(2):
                    sp.wait_ge(stored[u], 32 * NSEG // 2)

            @block.vector
            def _(dve):
                def norm(n, u, i):
                    dve.wait_ge(y_in[u], (i + 1) * 16 * TPS)
                    dve.wait_ge(x_in[u], (i + 1) * 16)
                    dve.tensor_tensor(sm[:, u], y[:, u], x1[:, u], ALU.add).then_inc(sum_done, 1)
                    dve.wait_ge(sum_done, n + 1)
                    layernorm(dve, ln, n, u, sm[:, u], x2[:, u], TPS)

                for u in range(2):
                    norm(u, u, 0)
                with dve.Fori(1, NSEG // 2) as i:
                    for u in range(2):
                        dve.wait_ge(stored[u], i * 32)
                        norm(i * 2 + u, u, i)

            @block.tensor
            def _(pe):
                def turn(n, u):
                    pe.wait_ge(ln["out_done"], n * TPS + TPS)
                    for k in range(KD):
                        for a in range(TPS):
                            mm = pe.transpose(t_ps[:, u, k, a * P:(a + 1) * P], x2[:, u, a, k * P:(k + 1) * P], ident_f[:])
                    mm.then_inc(turned, 1)

                for u in range(2):
                    turn(u, u)
                with pe.Fori(1, NSEG // 2) as i:
                    for u in range(2):
                        pe.wait_ge(copied, i * 2 + u - 1)
                        turn(i * 2 + u, u)

            @block.scalar
            def _(act):
                act.wait_ge(x_in[1], 16)
                for dst, src, done in later:
                    act.dma_start(dst, src).then_inc(done, 16)

                def step(n, u):
                    layernorm_root(act, ln, n, u)
                    act.wait_ge(turned, n + 1)
                    act.activation(x2T[:, u], t_ps[:, u], ACT.Copy).then_inc(copied, 1)

                for u in range(2):
                    step(u, u)
                with act.Fori(1, NSEG // 2) as i:
                    for u in range(2):
                        act.wait_ge(stored[u], i * 32)
                        step(i * 2 + u, u)


DI, DS, DR, DC = 512, 16, 16, 4
CH = DI // P
UNITS = DS * CH
RING = 8
HRING = 4
BRING = 4
BCROWS = 2 * DS

SSM_STEPS = {
    "PE": [(1, "X", 0), (3, "X", 1), (5, "X", 2), (7, "X", 3), (9, "Z", 0), (11, "Z", 1), (13, "Z", 2), (15, "Z", 3),
           (15, "direct", 0), (16, "direct", 1), (17, "direct", 2), (18, "direct", 3), (22, "P", 0), (26, "T", 0),
           (28, "T", 1), (30, "T", 2), (32, "T", 3), (39, "O", 0), (44, "O", 1)],
    "ACT": [(10, "X", 0), (12, "X", 1), (15, "X", 2), (16, "X", 3), (16, "Z", 0), (18, "Z", 1), (20, "Z", 2),
            (22, "Z", 3), (28, "silu", 0), (31, "P", 0), (33, "T", 0), (38, "T", 1), (40, "T", 2), (42, "T", 3),
            (44, "exp", 0), (49, "ln", 0), (58, "root", 0), (60, "scale", 0), (61, "scale", 1), (62, "scale", 2),
            (63, "scale", 3), (63, "apply", 0)],
    "DVE": [(2, "skip", 0), (2, "skip", 1), (2, "skip", 2), (2, "skip", 3), (12, "conv", 0), (13, "conv", 1),
            (16, "conv", 2), (27, "P", 0), (42, "O", 0), (46, "soft", 0), (47, "O", 1), (47, "soft", 1),
            (49, "LN", 0), (50, "soft", 2), (54, "LN", 1)],
    "Pool": [(55, "u", 0), (56, "u", 1), (57, "u", 2), (58, "u", 3)],
}
SSM_BEHIND = ("skip", "O", "LN", "root", "apply")
SSM_OWN = ("direct",)


SSM_WEIGHTS = 11


def ssm_weights(nc, ctx, loaded, w_in_d, conv_w_d, conv_b_d, w_x_d, w_dt_d, b_dt_d, a_log_d, d_d, w_out_d, keep_d, sel_d):
    def sb(name, shape, dt=F32):
        return ctx.enter_context(nc.sbuf_tensor(f"ssmw_{name}", shape, dt))

    w = {"w_in": sb("w_in", [P, KD, 2 * DI]), "conv_w": sb("conv_w", [P, CH, DC]), "conv_b": sb("conv_b", [P, CH]),
         "w_x": sb("w_x", [P, CH, BCROWS + DR]), "w_dt": sb("w_dt", [BCROWS + DR, DI]), "b_dt": sb("b_dt", [P, CH]),
         "a_log": sb("a_log", [P, CH, DS]), "d_par": sb("d_par", [P, CH]), "w_out": sb("w_out", [P, CH, D]),
         "keep": sb("keep", [P, NSEG]), "sel": sb("sel", [3 * BCROWS, BCROWS, P], BF16)}
    loads = [(t, d, loaded) for t, d in (
             (w["w_in"][:], w_in_d.rearrange("(k p) n -> p k n", p=P)),
             (w["conv_w"][:], conv_w_d.rearrange("(c p) k -> p c k", p=P)),
             (w["conv_b"][:], conv_b_d),
             (w["w_x"][:], w_x_d.rearrange("(c p) n -> p c n", p=P)),
             (w["w_dt"][BCROWS:BCROWS + DR], w_dt_d),
             (w["b_dt"][:], b_dt_d),
             (w["a_log"][:], a_log_d.rearrange("(c p) s -> p c s", p=P)),
             (w["d_par"][:], d_d),
             (w["w_out"][:], w_out_d.rearrange("(c p) n -> p c n", p=P)),
             (w["keep"][:], keep_d), (w["sel"][:], sel_d))]
    return w, loads


def mamba_phase(nc, x2_rows, x2T_rows, x3_rows, w, weights, ident_f):
    with ExitStack() as ctx:
        s = Space(nc, ctx, "ssm")
        w_in, conv_w, conv_b, w_x, w_dt, b_dt, a_log, d_par, w_out, keep, sel = (w[n] for n in (
            "w_in", "conv_w", "conv_b", "w_x", "w_dt", "b_dt", "a_log", "d_par", "w_out", "keep", "sel"))
        a_exp = s.sb("a_exp", [P, CH, DS])
        a_neg = s.sb("a_neg", [P, CH, DS])
        xT = s.sb("xT", [P, KD, SEG])
        x2 = s.sb("x2", [P, TPS, D])
        xb = s.sb("xb", [P, CH, DC - 1 + SEG])
        xc = [s.sb(f"xc{v}", [P, CH, SEG]) for v in range(2)]
        sz = [s.sb(f"sz{v}", [P, CH, SEG]) for v in range(2)]
        delta = [s.sb(f"delta{v}", [P, CH, SEG]) for v in range(2)]
        du = [s.sb(f"du{v}", [P, CH, SEG]) for v in range(2)]
        bc = [s.sb(f"bc{v}", [3 * BCROWS, SEG], BF16) for v in range(2)]
        bc_rest = s.sb("bc_rest", [BCROWS, SEG])
        bc_mid = s.sb("bc_mid", [BCROWS, SEG], BF16)
        d_raw = s.sb("d_raw", [BCROWS + DR, SEG])
        pre = s.sb("pre", [P, CH, SEG])
        ex = s.sb("ex", [P, CH, SEG])
        decay = s.sb("decay", [P, RING, SEG])
        drive = s.sb("drive", [P, RING, SEG])
        h = s.sb("h", [P, RING, SEG])
        hc = s.sb("hc", [P, HRING, SEG])
        b_sb = s.sb("b_sb", [P, BRING, SEG])
        carry = s.sb("carry", [P, UNITS])
        yt = s.sb("yt", [P, CH, SEG])
        sm = s.sb("sm", [P, TPS, D])
        ln = layernorm_buffers(s, TPS)
        ln_shift = s.sb("ln_shift", [P, 2, TPS])
        f_ps = s.ps("f_ps", [P, SEG])
        b_ps = s.ps("b_ps", [P, SEG])
        c_ps = s.ps("c_ps", [P, 2, SEG])
        y_ps = s.ps("y_ps", [P, CH, SEG])

        ready, direct_done, direct_added, shift_done = (s.sem(n) for n in ("ready", "direct", "direct_added", "shift"))
        xT_in, x2_in, stored = s.sem("xT_in"), s.sem("x2_in"), s.sem("stored")
        (x_filled, x_copied, halo_done, conv_done, z_filled, z_copied, silu_done, p_filled, hi_done, rest_done,
         mid_done, lo_done, raw_done, t_filled, pre_done, abs_done, exp_done, one_done, ln_done, soft_done,
         u_done, o_filled, sum_done) = (s.sem(n) for n in (
             "x_filled", "x_copied", "halo", "conv", "z_filled", "z_copied", "silu", "p_filled", "hi", "rest", "mid",
             "lo", "raw", "t_filled", "pre", "abs", "exp", "one", "ln_one", "soft", "u", "o_filled", "sum"))
        (b_filled, c_filled, b_copied, decay_done, drive_done, scan_done, hc_done, add_done, carry_done,
         skip_done) = (s.sem(n) for n in ("b_filled", "c_filled", "b_copied", "decay", "drive", "scan", "hc", "add", "carry",
                                        "skip"))

        def bodies(loop, body, engine):
            for _, *x in SSM_STEPS[engine]:
                if x[0] not in SSM_BEHIND + SSM_OWN:
                    body.ahead(x, 0, 0)
            body.start()
            segment(body, engine, 0, 0, False, True)
            with loop(0, NSEG // 2 - 1) as r:
                segment(body, engine, r * 2 + 1, 1, True, True)
                segment(body, engine, r * 2 + 2, 0, True, True)
            segment(body, engine, NSEG - 1, 1, True, False)
            for _, *x in SSM_STEPS[engine]:
                if x[0] in SSM_BEHIND:
                    body.behind(x, NSEG - 1, 1)

        def segment(body, engine, n, v, behind, ahead):
            for k in range(UNITS):
                body.unit(n, v, k, ahead)
                for at, *x in SSM_STEPS[engine]:
                    if at == k and x[0] in SSM_BEHIND and behind:
                        body.behind(x, n - 1, 1 - v)
                    if at == k and x[0] in SSM_OWN:
                        body.own(x, n, v)
                    if at == k and x[0] not in SSM_BEHIND + SSM_OWN and ahead:
                        body.ahead(x, n + 1, 1 - v)
            body.finish(n, v)

        class Nothing:
            def start(self): pass
            def unit(self, n, v, k, more): pass
            def ahead(self, x, n, v): pass
            def own(self, x, n, v): pass
            def behind(self, x, n, v): pass
            def finish(self, n, v): pass

        with nc.Block() as block:
            @block.sync
            def _(sp):
                def load_xT(n):
                    sp.dma_start(xT[:], x2T_rows.rearrange("(k p) n -> p k n", p=P)[:, :, bass.ds(n * SEG, SEG)]
                                 ).then_inc(xT_in, 16)

                def load_x2(n):
                    sp.dma_start(x2[:], x2_rows[bass.ds(n * SEG, SEG)].rearrange("(a p) d -> p a d", p=P)
                                 ).then_inc(x2_in, 16)

                def store(n):
                    sp.wait_ge(ln["out_done"], n * TPS + TPS)
                    sp.dma_start(x3_rows[bass.ds(n * SEG, SEG)].rearrange("(a p) d -> p a d", p=P), sm[:]
                                 ).then_inc(stored, 16)

                sp.sem_inc(stored, 16)
                load_xT(0)
                load_x2(0)
                sp.wait_ge(z_filled, CH)
                load_xT(1)
                with sp.Fori(0, NSEG - 2) as n:
                    sp.wait_ge(z_filled, n * CH + 2 * CH)
                    load_xT(n + 2)
                    store(n)
                    load_x2(n + 1)
                store(NSEG - 2)
                load_x2(NSEG - 1)
                store(NSEG - 1)
                sp.wait_ge(stored, 16 * NSEG + 16)

            @block.tensor
            def _(pe):
                class Body(Nothing):
                    def start(self):
                        pe.wait_ge(lo_done, 1)
                        self.spread_c(0, 0, 0)
                        for st in range(4):
                            self.spread_b(0, 0, st)

                    def unit(self, n, v, k, more):
                        st = k // CH
                        if k % CH == 0 and st + 1 < DS:
                            self.spread_c(n, v, st + 1)
                        elif k % CH == 0 and more:
                            self.spread_c(n + 1, 1 - v, 0)
                        elif k % CH == 1 and st + 4 < DS:
                            self.spread_b(n, v, st + 4)
                        elif k % CH == 1 and more:
                            if st + 4 == DS:
                                pe.wait_ge(lo_done, n + 2)
                            self.spread_b(n + 1, 1 - v, st + 4 - DS)
                        if k >= 2:
                            self.add(n, k - 2)

                    def spread_b(self, n, v, st):
                        pe.wait_ge(b_copied, n * DS + st + 1)
                        pe.matmul(b_ps[:], sel[:, st], bc[v][:], start=True, stop=True).then_inc(b_filled, 1)

                    def spread_c(self, n, v, st):
                        pe.wait_ge(hc_done, n * UNITS + st * CH + CH)
                        pe.matmul(c_ps[:, st % 2], sel[:, DS + st], bc[v][:], start=True, stop=True).then_inc(c_filled, 1)

                    def add(self, n, k):
                        st, c = k // CH, k % CH
                        pe.wait_ge(hc_done, n * UNITS + k + 1 + RING)
                        if st == 0 and not (isinstance(n, int) and n == 0):
                            pe.wait_ge(skip_done, n * CH + c + 1 - CH)
                        pe.matmul(y_ps[:, c], ident_f[:], hc[:, k % HRING], start=(st == 0), stop=(st == DS - 1)
                                  ).then_inc(add_done, 1)

                    def finish(self, n, v):
                        for k in (UNITS - 2, UNITS - 1):
                            self.add(n, k)

                    def ahead(self, x, n, v):
                        kind, c = x
                        first = isinstance(n, int) and n == 0
                        if kind in ("X", "Z"):
                            if kind == "X":
                                pe.wait_ge(xT_in, n * 16 + 16)
                                if c:
                                    pe.wait_ge(x_copied, n * 2 * CH + 2 * c)
                                elif not first:
                                    pe.wait_ge(pre_done, n * CH)
                                    if not isinstance(n, int):
                                        pe.wait_ge(sum_done, n * 2 - 3)
                            else:
                                pe.wait_ge(z_copied if c else x_copied, n * CH + c if c else n * 2 * CH + 2 * CH)
                            col = (CH * (kind == "Z") + c) * P
                            for k in range(KD):
                                mm = pe.matmul(f_ps[:], w_in[:, k, col:col + P], xT[:, k], start=(k == 0), stop=(k == KD - 1))
                            mm.then_inc(x_filled if kind == "X" else z_filled, 1)
                        elif kind == "P":
                            pe.wait_ge(z_copied, n * CH + CH)
                            pe.wait_ge(silu_done, n * 2 + 1)
                            for k in range(CH):
                                mm = pe.matmul(f_ps[0:BCROWS + DR], w_x[:, k], xc[v][:, k], start=(k == 0), stop=(k == CH - 1))
                            mm.then_inc(p_filled, 1)
                        elif kind == "T":
                            if c == 0:
                                pe.wait_ge(rest_done, n + 1)
                                pe.wait_ge(raw_done, n + 1)
                            else:
                                pe.wait_ge(pre_done, n * CH + c)
                            pe.matmul(f_ps[:], w_dt[BCROWS:BCROWS + DR, c * P:(c + 1) * P], d_raw[BCROWS:BCROWS + DR],
                                      start=True, stop=True).then_inc(t_filled, 1)

                    def own(self, x, n, v):
                        c = x[1]
                        pe.wait_ge(direct_done, n * CH + c + 1)
                        pe.matmul(y_ps[:, c], ident_f[:], pre[:, c], start=False, stop=False).then_inc(direct_added, 1)

                    def behind(self, x, n, v):
                        kind, half = x
                        if kind == "O":
                            if half == 0:
                                pe.wait_ge(skip_done, n * CH + CH)
                                if isinstance(n, int):
                                    pe.wait_ge(sum_done, 2 * n + 1)
                                else:
                                    pe.wait_ge(pre_done, n * CH + 3 * CH)
                            else:
                                pe.wait_ge(sum_done, n * 2 + 2)
                            for a in (0, 1):
                                t = 2 * half + a
                                for k in range(CH):
                                    mm = pe.matmul(f_ps[:, a * D:(a + 1) * D], yt[:, k, t * P:(t + 1) * P], w_out[:, k],
                                                   start=(k == 0), stop=(k == CH - 1))
                            mm.then_inc(o_filled, 1)

                pe.wait_ge(weights, 16 * SSM_WEIGHTS)
                pe.sem_inc(add_done, HRING)
                pe.sem_inc(o_filled, 1)
                bodies(pe.Fori, Body(), "PE")

            @block.scalar
            def _(act):
                class Body(Nothing):
                    def start(self):
                        self.copy_b(0, 0)

                    def unit(self, n, v, k, more):
                        st, c = k // CH, k % CH
                        if c == 0:
                            if st == 0:
                                act.wait_ge(soft_done, n * 3 + 3)
                            if st + 1 < DS:
                                self.copy_b(n, st + 1)
                            elif more:
                                self.copy_b(n + 1, 0)
                        act.wait_ge(scan_done, n * UNITS + k + 1)
                        act.activation(decay[:, k % RING], delta[v][:, c], ACT.Exp, scale=a_neg[:, c, st:st + 1]
                                       ).then_inc(decay_done, 1)

                    def copy_b(self, n, st):
                        act.wait_ge(b_filled, n * DS + st + 1)
                        act.wait_ge(drive_done, n * UNITS + st * CH + CH)
                        act.activation(b_sb[:, st % BRING], b_ps[:], ACT.Copy).then_inc(b_copied, 1)

                    def ahead(self, x, n, v):
                        kind, c = x
                        first = isinstance(n, int) and n == 0
                        if kind == "X":
                            if c == 0:
                                act.wait_ge(halo_done, n + 1)
                            act.wait_ge(x_filled, n * CH + c + 1)
                            act.activation(xb[:, c, DC - 1:], f_ps[:], ACT.Copy).then_inc(x_copied, 1)
                            act.activation(xc[v][:, c], f_ps[:], ACT.Identity, bias=conv_b[:, c:c + 1],
                                           scale=conv_w[:, c, DC - 1:DC]).then_inc(x_copied, 1)
                        elif kind == "Z":
                            if c == 0 and not first and not (isinstance(n, int) and n == 1):
                                act.wait_ge(skip_done, n * CH - CH)
                            act.wait_ge(z_filled, n * CH + c + 1)
                            act.activation(sz[v][:, c], f_ps[:], ACT.Copy).then_inc(z_copied, 1)
                        elif kind == "silu":
                            act.wait_ge(conv_done, n * (DC - 1) * CH + (DC - 1) * CH)
                            act.activation(xc[v][:], xc[v][:], ACT.Silu).then_inc(silu_done, 1)
                            act.wait_ge(z_copied, n * CH + CH)
                            act.activation(sz[v][:], sz[v][:], ACT.Silu).then_inc(silu_done, 1)
                        elif kind == "P":
                            act.wait_ge(p_filled, n + 1)
                            act.activation(bc[v][0:BCROWS], f_ps[0:BCROWS], ACT.Copy).then_inc(hi_done, 1)
                            act.activation(d_raw[BCROWS:BCROWS + DR], f_ps[BCROWS:BCROWS + DR], ACT.Copy).then_inc(raw_done, 1)
                        elif kind == "T":
                            if c == 0 and not first:
                                act.wait_ge(direct_added, n * CH)
                            act.wait_ge(t_filled, n * CH + c + 1)
                            act.activation(pre[:, c], f_ps[:], ACT.Identity, bias=b_dt[:, c:c + 1]).then_inc(pre_done, 1)
                        elif kind == "exp":
                            act.wait_ge(pre_done, n * CH + CH)
                            act.activation(ex[:], pre[:], ACT.Abs).then_inc(abs_done, 1)
                            act.wait_ge(abs_done, n + 1)
                            act.activation(ex[:], ex[:], ACT.Exp, scale=-1.0).then_inc(exp_done, 1)
                            act.wait_ge(exp_done, n + 1)
                            act.activation(du[v][:], ex[:], ACT.Copy, bias=1.0).then_inc(one_done, 1)
                        elif kind == "ln":
                            act.wait_ge(one_done, n + 1)
                            act.activation(delta[v][:], du[v][:], ACT.Ln).then_inc(ln_done, 1)

                        elif kind == "scale":
                            act.wait_ge(silu_done, n * 2 + 1)
                            act.wait_ge(soft_done, n * 3 + 3)
                            act.activation(pre[:, c], xc[v][:, c], ACT.Copy, scale=d_par[:, c:c + 1]).then_inc(direct_done, 1)

                    def behind(self, x, n, v):
                        if x[0] == "root":
                            layernorm_root(act, ln, n, v)
                        else:
                            act.wait_ge(shift_done, n + 1)
                            for a in range(TPS):
                                act.activation(sm[:, a], sm[:, a], ACT.Identity, bias=ln_shift[:, v, a:a + 1],
                                               scale=ln["rstd"][:, v, a:a + 1]).then_inc(ln["out_done"], 1)

                act.wait_ge(weights, 16 * SSM_WEIGHTS)
                act.activation(a_exp[:], a_log[:], ACT.Exp).then_inc(ready, 1)
                act.sem_inc(b_copied, 1)
                act.wait_ge(ready, 3)
                bodies(act.Fori, Body(), "ACT")

            @block.vector
            def _(dve):
                class Body(Nothing):
                    def unit(self, n, v, k, more):
                        st, c = k // CH, k % CH
                        first = isinstance(n, int) and n == 0
                        if c == 0 and not first:
                            dve.wait_ge(carry_done, n * DS + st + 1 - DS)
                        dve.wait_ge(decay_done, n * UNITS + k + 1)
                        dve.wait_ge(drive_done, n * UNITS + k + 1 + BRING * CH)
                        dve.tensor_tensor_scan(h[:, k % RING], decay[:, k % RING], drive[:, k % RING],
                                               0.0 if first else carry[:, k:k + 1], ALU.mult, ALU.add).then_inc(scan_done, 1)
                        if k >= 1:
                            self.weigh(n, k - 1)

                    def weigh(self, n, k):
                        st, c = k // CH, k % CH
                        dve.wait_ge(scan_done, n * UNITS + k + 1 + RING)
                        if c == 0:
                            dve.wait_ge(c_filled, n * DS + st + 1)
                        dve.wait_ge(add_done, n * UNITS + k + 1)
                        dve.tensor_tensor(hc[:, k % HRING], h[:, k % RING], c_ps[:, st % 2], ALU.mult).then_inc(hc_done, 1)
                        if c == CH - 1:
                            r = (k - c) % RING
                            dve.tensor_scalar(carry[:, k - c:k + 1], h[:, r:r + CH, SEG - 1], keep[:, bass.ds(n, 1)], None,
                                              ALU.mult).then_inc(carry_done, 1)

                    def finish(self, n, v):
                        self.weigh(n, UNITS - 1)
                    def ahead(self, x, n, v):
                        kind, c = x
                        if kind == "conv":
                            tap = c
                            for c in range(CH):
                                if tap == 0:
                                    dve.wait_ge(x_copied, (n * CH + c) * 2 + 2)
                                else:
                                    dve.wait_ge(conv_done, (n * (DC - 1) + tap - 1) * CH + c + 1)
                                dve.scalar_tensor_tensor(xc[v][:, c], xb[:, c, tap:tap + SEG], conv_w[:, c, tap:tap + 1],
                                                         xc[v][:, c], ALU.mult, ALU.add).then_inc(conv_done, 1)
                            if tap == DC - 2:
                                dve.wait_ge(conv_done, (n + 1) * (DC - 1) * CH)
                                dve.tensor_scalar(xb[:, :, 0:DC - 1], xb[:, :, SEG:SEG + DC - 1], keep[:, bass.ds(n, 1)], None,
                                                  ALU.mult).then_inc(halo_done, 1)
                        elif kind == "P":
                            dve.wait_ge(hi_done, n + 1)
                            dve.tensor_tensor(bc_rest[:], f_ps[0:BCROWS], bc[v][0:BCROWS], ALU.subtract).then_inc(rest_done, 1)
                            dve.wait_ge(rest_done, n + 1)
                            dve.tensor_copy(bc_mid[:], bc_rest[:]).then_inc(mid_done, 1)
                            dve.tensor_copy(bc[v][BCROWS:2 * BCROWS], bc_rest[:]).then_inc(mid_done, 1)
                            dve.wait_ge(mid_done, n * 2 + 2)
                            dve.tensor_tensor(bc[v][2 * BCROWS:], bc_rest[:], bc_mid[:], ALU.subtract).then_inc(lo_done, 1)
                        elif kind == "soft":
                            if c == 0:
                                dve.wait_ge(ln_done, n + 1)
                                dve.scalar_tensor_tensor(du[v][:], du[v][:], 1.0, ex[:], ALU.subtract, ALU.subtract
                                                         ).then_inc(soft_done, 1)
                            elif c == 1:
                                dve.wait_ge(soft_done, n * 3 + 1)
                                dve.scalar_tensor_tensor(pre[:], pre[:], 0.0, du[v][:], ALU.max, ALU.subtract
                                                         ).then_inc(soft_done, 1)
                            else:
                                dve.wait_ge(soft_done, n * 3 + 2)
                                dve.tensor_tensor(delta[v][:], delta[v][:], pre[:], ALU.add).then_inc(soft_done, 1)

                    def behind(self, x, n, v):
                        kind, half = x
                        if kind == "skip":
                            c = half
                            dve.wait_ge(add_done, n * UNITS + UNITS - CH + c + 1 + HRING)
                            if c == 0 and not (isinstance(n, int) and n == 0):
                                dve.wait_ge(o_filled, n * 2 + 1)
                            dve.wait_ge(silu_done, n * 2 + 2)
                            dve.tensor_tensor(yt[:, c], y_ps[:, c], sz[v][:, c], ALU.mult).then_inc(skip_done, 1)
                        elif kind == "O":
                            if half == 0:
                                dve.wait_ge(x2_in, n * 16 + 16)
                                dve.wait_ge(stored, n * 16 + 16)
                            dve.wait_ge(o_filled, n * 2 + half + 2)
                            dve.tensor_tensor(sm[:, 2 * half:2 * half + 2], f_ps[:].rearrange("p (a d) -> p a d", d=D),
                                              x2[:, 2 * half:2 * half + 2], ALU.add).then_inc(sum_done, 1)
                        elif half == 0:
                            dve.wait_ge(sum_done, n * 2 + 3)
                            layernorm_stats(dve, ln, n, v, sm[:], TPS)
                        else:
                            layernorm_scale(dve, ln, n, v)
                            dve.scalar_tensor_tensor(ln_shift[:, v], ln["mv"][:, v, :, 0], -1.0, ln["rstd"][:, v], ALU.mult,
                                                     ALU.mult).then_inc(shift_done, 1)

                dve.wait_ge(weights, 16 * SSM_WEIGHTS)
                dve.memset(xb[:, :, 0:DC - 1], 0.0).then_inc(halo_done, 1)
                dve.wait_ge(ready, 1)
                dve.tensor_scalar(a_neg[:], a_exp[:], -1.0, None, ALU.mult).then_inc(ready, 2)
                dve.sem_inc(scan_done, RING)
                dve.sem_inc(sum_done, 1)
                dve.sem_inc(hc_done, RING)
                bodies(dve.Fori, Body(), "DVE")

            @block.gpsimd
            def _(pool):
                class Body(Nothing):
                    def unit(self, n, v, k, more):
                        st, c = k // CH, k % CH
                        if k == 0:
                            pool.wait_ge(u_done, n * CH + CH)
                        if c == 0:
                            pool.wait_ge(b_copied, n * DS + st + 2)
                        pool.wait_ge(scan_done, n * UNITS + k + 1)
                        pool.tensor_tensor(drive[:, k % RING], du[v][:, c], b_sb[:, st % BRING], ALU.mult).then_inc(drive_done, 1)

                    def ahead(self, x, n, v):
                        c = x[1]
                        if c == 0:
                            pool.wait_ge(soft_done, n * 3 + 3)
                        pool.tensor_tensor(du[v][:, c], delta[v][:, c], xc[v][:, c], ALU.mult).then_inc(u_done, 1)

                pool.sem_inc(drive_done, BRING * CH)
                bodies(pool.Fori, Body(), "Pool")


ROUND = 1.5 * 2.0 ** 23
HBANKS = 4


def ffn_phase(nc, x3_rows, w1T_d, w2T_d, b1_d, b2_d, ident_f, out_rows):
    with ExitStack() as ctx:
        s = Space(nc, ctx, "ffn")
        w1 = s.sb("w1", [P, KD, F])
        w2 = s.sb("w2", [P, FK, D])
        w1q = s.sb("w1q", [P, KD, F], BF16)
        w2q = s.sb("w2q", [P, FK, D], BF16)
        mag = s.sb("mag", [P, 2, KD * F])
        part = s.sb("part", [P, 2])
        ones = s.sb("ones", [P, P])
        gamma = s.sb("gamma", [P, 2])
        scale = s.sb("scale", [P, 2])
        b1 = s.sb("b1", [P, FK])
        b2 = s.sb("b2", [P, D])
        x = s.sb("x", [P, 2, TPS, D])
        xb = s.sb("xb", [P, 2, TPS, D])
        xp = s.sb("xp", [P, 2, 3, KD, SEG], BF16)
        x_rest = s.sb("x_rest", [P, KD, SEG])
        h = s.sb("h", [P, FK, SEG])
        h_rest = s.sb("h_rest", [P, FK, SEG])
        hp = s.sb("hp", [P, 2, 3, FK, SEG], BF16)
        sm = s.sb("sm", [P, 2, TPS, D])
        out = s.sb("out", [P, 2, TPS, D])
        ln = layernorm_buffers(s, TPS)
        t_ps = s.ps("t_ps", [P, KD, SEG])
        h_ps = s.ps("h_ps", [P, HBANKS, SEG])
        y_ps = s.ps("y_ps", [P, 2, SEG])
        w_in, mag_done, part_done, total_done, quant, quantised = (
            s.sem(n) for n in ("w_in", "mag", "part", "total", "quant", "quantised"))
        x_in, stored = [s.sem("x_in0"), s.sem("x_in1")], [s.sem("stored0"), s.sem("stored1")]
        turned, xhi, xrest, xmid, xlo = (s.sem(n) for n in ("turned", "xhi", "xrest", "xmid", "xlo"))
        up_done, relu_done, hhi, hrest, hmid, hlo = (s.sem(n) for n in ("up", "relu", "hhi", "hrest", "hmid", "hlo"))
        down_done, biased, sum_done = (s.sem(n) for n in ("down", "biased", "sum"))

        def steps(loop, step):
            step(0, 0, 0)
            step(1, 0, 1)
            with loop(1, NSEG // 2 - 1) as i:
                for u in range(2):
                    step(i * 2 + u, i, u)
            for n in range(NSEG - 2, NSEG + 2):
                step(n, n // 2, n % 2)

        def within(n, first, last):
            return not isinstance(n, int) or first <= n <= last

        with nc.Block() as block:
            @block.sync
            def _(sp):
                def load(n, u):
                    sp.dma_start(x[:, u], x3_rows[bass.ds(n * SEG, SEG)].rearrange("(a p) d -> p a d", p=P)
                                 ).then_inc(x_in[u], 16)

                def store(n, u):
                    sp.wait_ge(ln["out_done"], (n + 1) * TPS)
                    sp.dma_start(out_rows[bass.ds(n * SEG, SEG)].rearrange("(a p) d -> p a d", p=P), out[:, u]
                                 ).then_inc(stored[u], 16)

                sp.dma_start(w1[:], w1T_d.rearrange("(k p) n -> p k n", p=P)).then_inc(w_in, 16)
                sp.dma_start(w2[:], w2T_d.rearrange("(k p) n -> p k n", p=P)).then_inc(w_in, 16)
                sp.dma_start(b1[:], b1_d).then_inc(w_in, 16)
                sp.dma_start(b2[:], b2_d.partition_broadcast(P)).then_inc(w_in, 16)
                load(0, 0)
                load(1, 1)
                with sp.Fori(0, NSEG // 2 - 1) as i:
                    for u in range(2):
                        n = i * 2 + u
                        sp.wait_ge(turned, n + 1)
                        sp.wait_ge(biased, n + 1)
                        load(n + 2, u)
                        store(n, u)
                for u in range(2):
                    store(NSEG - 2 + u, u)
                for u in range(2):
                    sp.wait_ge(stored[u], 16 + 16 * NSEG // 2)

            @block.tensor
            def _(pe):
                def turn(n, i, u):
                    pe.wait_ge(x_in[u], i * 16 + 16)
                    for k in range(KD):
                        for a in range(TPS):
                            mm = pe.transpose(t_ps[:, k, a * P:(a + 1) * P], x[:, u, a, k * P:(k + 1) * P], ident_f[:])
                    mm.then_inc(turned, 1)

                def up(n, u):
                    pe.wait_ge(xlo, n + 2)
                    for c in range(FK):
                        pe.wait_ge(relu_done, n * FK + c + 1)
                        for part in range(3):
                            for k in range(KD):
                                mm = pe.matmul(h_ps[:, c % HBANKS], w1q[:, k, c * P:(c + 1) * P], xp[:, u, part, k],
                                               start=(part + k == 0), stop=(part == 2 and k == KD - 1))
                        mm.then_inc(up_done, 1)

                def down(n, u):
                    pe.wait_ge(sum_done, n + 1)
                    for a in range(TPS):
                        for c in range(FK):
                            if a == 0:
                                pe.wait_ge(hlo, n * FK + c + 1 + FK)
                            for part in range(3):
                                mm = pe.matmul(y_ps[:, a // 2, (a % 2) * D:(a % 2 + 1) * D],
                                               hp[:, u, part, c, a * P:(a + 1) * P], w2q[:, c],
                                               start=(c + part == 0), stop=(c == FK - 1 and part == 2))
                    mm.then_inc(down_done, 1)

                def step(n, i, u):
                    if within(n, 0, NSEG - 1):
                        up(n, u)
                    if within(n, 0, NSEG - 2):
                        turn(n + 1, i + u, 1 - u)
                    if isinstance(n, int) and n == 1:
                        pe.wait_ge(quantised, 2)
                    if within(n, 1, NSEG):
                        down(n - 1, 1 - u)

                pe.wait_ge(part_done, 3)
                pe.matmul(y_ps[:, 0, 0:2], ones[:], part[:], start=True, stop=True).then_inc(total_done, 1)
                turn(0, 0, 0)
                pe.wait_ge(quantised, 1)
                steps(pe.Fori, step)

            @block.scalar
            def _(act):
                def relu(n, c):
                    act.wait_ge(up_done, n * FK + c + 1)
                    act.wait_ge(hrest, n * FK + c + 1)
                    act.activation(h[:, c], h_ps[:, c % HBANKS], ACT.Relu, bias=b1[:, c:c + 1]).then_inc(relu_done, 1)

                def mid(n, u, c):
                    act.wait_ge(hrest, n * FK + c + 1 + FK)
                    act.activation(hp[:, u, 1, c], h_rest[:, c], ACT.Copy).then_inc(hmid, 1)

                def split_x(n, u):
                    act.wait_ge(turned, n + 1)
                    act.activation(xp[:, u, 0], t_ps[:], ACT.Copy).then_inc(xhi, 1)
                    act.wait_ge(xrest, n + 1)
                    act.activation(xp[:, u, 1], x_rest[:], ACT.Copy).then_inc(xmid, 1)

                def step(n, i, u):
                    if within(n, 0, NSEG - 1):
                        relu(n, 0)
                        relu(n, 1)
                    if within(n, 2, NSEG + 1):
                        layernorm_root(act, ln, n - 2, u)
                    if within(n, 0, NSEG - 1):
                        for c in range(2, FK):
                            relu(n, c)
                            if c >= HBANKS:
                                mid(n, u, c - HBANKS)
                        for c in range(FK - HBANKS, FK):
                            mid(n, u, c)
                    if within(n, 0, NSEG - 2):
                        split_x(n + 1, 1 - u)

                act.wait_ge(w_in, 64)
                for w, m in ((w1, 0), (w2, 1)):
                    act.activation(mag[:, m], w[:].rearrange("p k n -> p (k n)"), ACT.Abs).then_inc(mag_done, 1)
                act.sem_inc(relu_done, HBANKS)
                split_x(0, 0)
                steps(act.Fori, step)

            @block.vector
            def _(dve):
                def rest_x(n, u):
                    dve.wait_ge(xhi, n + 1)
                    dve.wait_ge(xlo, n + 1)
                    dve.tensor_tensor(x_rest[:], t_ps[:], xp[:, u, 0], ALU.subtract).then_inc(xrest, 1)

                def split_h(n, u, c):
                    dve.wait_ge(relu_done, n * FK + c + 1 + HBANKS)
                    dve.tensor_copy(hp[:, u, 0, c], h[:, c]).then_inc(hhi, 1)
                    dve.wait_ge(hhi, n * FK + c + 1)
                    dve.wait_ge(hlo, n * FK + c + 1)
                    dve.tensor_tensor(h_rest[:, c], h[:, c], hp[:, u, 0, c], ALU.subtract).then_inc(hrest, 1)

                def step(n, i, u):
                    if within(n, 2, NSEG + 1):
                        norm_at(n - 2, i, u)
                    if within(n, 0, NSEG - 1):
                        for c in range(FK):
                            split_h(n, u, c)
                    if within(n, 0, NSEG - 2):
                        rest_x(n + 1, 1 - u)

                def norm_at(n, i, u):
                    dve.wait_ge(down_done, n + 1)
                    dve.wait_ge(biased, n + 1)
                    dve.tensor_tensor(sm[:, u], y_ps[:].rearrange("p c (a d) -> p (c a) d", d=D), xb[:, u], ALU.add
                                      ).then_inc(sum_done, 1)
                    dve.wait_ge(sum_done, n + 2)
                    dve.wait_ge(stored[u], i * 16)
                    layernorm(dve, ln, n, u, sm[:, u], out[:, u], TPS)

                dve.memset(ones[:], 1.0).then_inc(part_done, 1)
                for m in range(2):
                    dve.wait_ge(mag_done, m + 1)
                    dve.tensor_reduce(part[:, m:m + 1], mag[:, m], AX.X, ALU.add).then_inc(part_done, 1)
                dve.wait_ge(total_done, 1)
                dve.tensor_scalar(gamma[:], y_ps[:, 0, 0:2], 1.0 / (F * D), EPS, ALU.mult, ALU.add).then_inc(quant, 1)
                dve.sem_inc(sum_done, 1)
                dve.sem_inc(hrest, FK)
                for u in range(2):
                    dve.sem_inc(stored[u], 16)
                dve.wait_ge(quant, 1)
                dve.reciprocal(scale[:], gamma[:]).then_inc(quant, 1)
                dve.wait_ge(quant, 2)
                flat = [w[:].rearrange("p k n -> p (k n)") for w in (w1, w2)]
                flat_q = [w[:].rearrange("p k n -> p (k n)") for w in (w1q, w2q)]
                for m, (w, q) in enumerate(zip(flat, flat_q)):
                    dve.tensor_scalar(w, w, scale[:, m:m + 1], 1.0, ALU.mult, ALU.min).then_inc(quant, 1)
                    dve.wait_ge(quant, 3 + 2 * m)
                    dve.tensor_scalar(w, w, -1.0, ROUND, ALU.max, ALU.add).then_inc(quant, 1)
                    dve.wait_ge(quant, 4 + 2 * m)
                    dve.tensor_scalar(q, w, ROUND, None, ALU.subtract).then_inc(quantised, 1)
                    if m == 0:
                        rest_x(0, 0)
                steps(dve.Fori, step)

            @block.gpsimd
            def _(pool):
                def lo_x(n, u):
                    pool.wait_ge(xmid, n + 1)
                    pool.tensor_tensor(xp[:, u, 2], x_rest[:], xp[:, u, 1], ALU.subtract).then_inc(xlo, 1)

                def step(n, i, u):
                    if within(n, 1, NSEG):
                        bias_at(n - 1, i, u)
                    if within(n, 0, NSEG - 1):
                        for c in range(FK):
                            pool.wait_ge(hmid, n * FK + c + 1)
                            pool.tensor_tensor(hp[:, u, 2, c], h_rest[:, c], hp[:, u, 1, c], ALU.subtract).then_inc(hlo, 1)
                    if within(n, 0, NSEG - 2):
                        lo_x(n + 1, 1 - u)

                def bias_at(n, i, u):
                    pool.wait_ge(x_in[1 - u], (i + u) * 16)
                    if within(n, 2, NSEG):
                        pool.wait_ge(sum_done, n)
                    pool.tensor_tensor(xb[:, 1 - u], x[:, 1 - u], b2[:].unsqueeze(1).broadcast_to([P, TPS, D]), ALU.add
                                       ).then_inc(biased, 1)

                pool.sem_inc(xlo, 1)
                pool.sem_inc(hlo, FK)
                pool.wait_ge(w_in, 64)
                lo_x(0, 0)
                steps(pool.Fori, step)


SLOTS = TILES + E - 1
SORTED = (SLOTS + 1) * P
ZEROINGS = SORTED * D // (P * 2048)


def build(nc, xT, x_rows, wq, wkv, wo, wr, br, ew1, eb1, ew2, eb2, w_in, conv_w, conv_b, w_x, w_dt, b_dt, a_log, d_par,
          w_out, fw1, fb1, fw2, fb2, c_ident, c_ident_b, c_tri_st, c_tri_ts, c_before, c_ones, c_slots, c_ranks,
          c_keep, c_sel, out_rows):
    def scratch(name, shape, dt=F32):
        return nc.dram_tensor(name, shape, dt).ap()

    qk_parts = scratch("qk_parts", (3, D + GROUPS * HD + 64, TOK), BF16)
    v_rows = scratch("v_rows", (TOK, GROUPS * HD))
    shift_rows = scratch("shift_rows", (3, GS * SBLK, P), BF16)
    ctx_rows = scratch("ctx_rows", (GROUPS, P, TOK))
    inv_rows = scratch("inv_rows", (HEADS, TOK))
    x1_rows = scratch("x1_rows", (TOK, D))
    sorted_rows = scratch("sorted_rows", (SORTED, D))
    done_rows = scratch("done_rows", (SLOTS * P, D))
    x2_rows = scratch("x2_rows", (TOK, D))
    x2T_rows = scratch("x2T_rows", (D, TOK))
    x3_rows = scratch("x3_rows", (TOK, D))

    with ExitStack() as ctx:
        s = Space(nc, ctx, "all")
        ident_f, ident_b = s.sb("ident_f", [P, P]), s.sb("ident_b", [P, P], BF16)
        tri_st, tri_ts = s.sb("tri_st", [P, P], BF16), s.sb("tri_ts", [P, P], BF16)
        before, ones_b = s.sb("before", [P, P], BF16), s.sb("ones_b", [P, P], BF16)
        slots_iota, ranks, br_sb = s.sb("slots", [1, SLOTS]), s.sb("ranks", [P, E]), s.sb("br", [P, TPS, E])
        scores_sb, pos_sb = s.sb("scores", [P, TILES, E]), s.sb("pos", [P, TILES], I32)
        owner_sb = s.sb("owner", [1, SLOTS], I32)
        consts_in, zero_done, zeroed, weights_in, x1_in, b2_in, ssm_in = (
            s.sem(n) for n in ("consts_in", "zero_done", "zeroed", "weights_in", "x1_in", "b2_in", "ssm_in"))

        with nc.Block() as block:
            @block.sync
            def _(sp):
                consts = ((ident_f, c_ident), (ident_b, c_ident_b), (tri_st, c_tri_st), (tri_ts, c_tri_ts),
                          (before, c_before), (ones_b, c_ones), (slots_iota, c_slots), (ranks, c_ranks))
                for t, d in consts:
                    sp.dma_start(t[:], d).then_inc(consts_in, 16)
                for a in range(TPS):
                    sp.dma_start(br_sb[:, a], br.partition_broadcast(P)).then_inc(consts_in, 16)
                sp.wait_ge(consts_in, 16 * (len(consts) + TPS))
        project_phase(nc, xT, wq, wkv, qk_parts, v_rows)

        with ExitStack() as experts:
            def sb(name, shape):
                return experts.enter_context(nc.sbuf_tensor(f"moe_{name}", shape, F32))

            e_w1, e_b1 = sb("w1", [P, E * KD, F]), sb("b1", [P, E, F])
            zero_ctx = experts.enter_context(ExitStack())
            zero = zero_ctx.enter_context(nc.sbuf_tensor("all_zero", [P, 2048], F32))
            with nc.Block() as block:
                @block.vector
                def _(dve):
                    dve.memset(zero[:], 0.0).then_inc(zero_done, 1)

                @block.sync
                def _(sp):
                    sp.wait_ge(zero_done, 1)
            later = [(e_w1[:], ew1.rearrange("e (k p) n -> p (e k) n", p=P), weights_in),
                     (e_b1[:], eb1.partition_broadcast(P), weights_in)]
            later += [(sorted_rows.rearrange("(k p r) d -> k p (r d)", k=ZEROINGS, p=P)[k], zero[:], zeroed)
                      for k in range(ZEROINGS)]
            attention_phase(nc, qk_parts, v_rows, shift_rows, ctx_rows, ident_f, ident_b, tri_st, tri_ts, later)
            with nc.Block() as block:
                @block.sync
                def _(sp):
                    sp.wait_ge(zeroed, 16 * ZEROINGS)
            zero_ctx.close()
            denominators_phase(nc, ctx_rows, inv_rows)
            out_project_phase(nc, ctx_rows, inv_rows, x_rows, wo, wr, br_sb, ident_f, scores_sb, x1_rows)
            e_w2 = sb("w2", [P, E * FK, D])
            x1_ctx = experts.enter_context(ExitStack())
            x1 = x1_ctx.enter_context(nc.sbuf_tensor("all_x1", [P, TILES, D], F32))
            with nc.Block() as block:
                @block.sync
                def _(sp):
                    sp.dma_start(x1[:], x1_rows.rearrange("(t p) d -> p t d", p=P)).then_inc(x1_in, 16)
                    sp.dma_start(e_w2[:], ew2.rearrange("e (k p) n -> p (e k) n", p=P)).then_inc(weights_in, 16)
            routing_phase(nc, scores_sb, pos_sb, owner_sb, ident_b, before, ones_b, slots_iota, ranks, SLOTS)
            scatter_phase(nc, x1, x1_in, pos_sb, sorted_rows, zeroed, 16 * ZEROINGS)
            x1_ctx.close()
            e_b2 = sb("b2", [P, E, D])
            with nc.Block() as block:
                @block.sync
                def _(sp):
                    sp.dma_start(e_b2[:], eb2.partition_broadcast(P)).then_inc(b2_in, 16)
            experts_phase(nc, SLOTS, sorted_rows, done_rows, owner_sb, e_w1, e_w2, e_b1, e_b2, weights_in, 48, b2_in, ident_f)
        with ExitStack() as ssm:
            weights, later = ssm_weights(nc, ssm, ssm_in, w_in, conv_w, conv_b, w_x, w_dt, b_dt, a_log, d_par, w_out, c_keep, c_sel)
            combine_phase(nc, x1_rows, done_rows, pos_sb, ident_f, x2_rows, x2T_rows, later)
            mamba_phase(nc, x2_rows, x2T_rows, x3_rows, weights, ssm_in, ident_f)
        ffn_phase(nc, x3_rows, fw1, fw2, fb1, fb2, ident_f, out_rows)


def kernel(L0_attn_x, L0_attn_wq, L0_attn_wk, L0_attn_wv, L0_attn_wo, L0_ffn_wr, L0_ffn_br, L0_ffn_w1, L0_ffn_b1,
           L0_ffn_w2, L0_ffn_b2, L1_attn_W_in, L1_attn_conv_w, L1_attn_conv_b, L1_attn_W_xproj, L1_attn_W_dt,
           L1_attn_b_dt, L1_attn_A_log, L1_attn_D_param, L1_attn_W_out, L1_ffn_W1, L1_ffn_b1, L1_ffn_W2, L1_ffn_b2):
    import concourse.bacc as bacc
    from concourse.bass_utils import run_bass_kernel_spmd

    bf16 = mybir.dt.np(BF16)
    x = np.asarray(L0_attn_x).reshape(TOK, D)
    wo = np.zeros((GROUPS, GS, 32, D), np.float32)
    wo[:, :, :HD] = L0_attn_wo.T.reshape(GROUPS, GS, HD, D)
    after = np.arange(P)[None, :] > np.arange(P)[:, None]
    sel = np.zeros((3, BCROWS, BCROWS, P), bf16)
    sel[:, np.arange(BCROWS), np.arange(BCROWS)] = 1
    keep = np.ones((P, NSEG), np.float32)
    keep[:, NSEG // BATCH - 1::NSEG // BATCH] = 0
    lay = {
        "xT": x.T, "x_rows": x, "wq": L0_attn_wq.T, "wkv": np.concatenate([L0_attn_wk.T, L0_attn_wv.T], 1),
        "wo": wo.reshape(GROUPS, P, D), "wr": L0_ffn_wr, "br": L0_ffn_br, "ew1": L0_ffn_w1, "eb1": L0_ffn_b1,
        "ew2": L0_ffn_w2, "eb2": L0_ffn_b2, "w_in": L1_attn_W_in, "conv_w": L1_attn_conv_w,
        "conv_b": L1_attn_conv_b.reshape(CH, P).T,
        "w_x": np.concatenate([L1_attn_W_xproj[:, DR:], L1_attn_W_xproj[:, :DR]], 1),
        "w_dt": L1_attn_W_dt, "b_dt": L1_attn_b_dt.reshape(CH, P).T, "a_log": L1_attn_A_log,
        "d_par": L1_attn_D_param.reshape(CH, P).T, "w_out": L1_attn_W_out,
        "fw1": L1_ffn_W1.T, "fb1": L1_ffn_b1.reshape(FK, P).T, "fw2": L1_ffn_W2.T, "fb2": L1_ffn_b2,
        "c_ident": np.eye(P, dtype=np.float32), "c_ident_b": np.eye(P, dtype=np.float32).astype(bf16),
        "c_tri_st": np.where(after, MASKED, 0).astype(bf16), "c_tri_ts": np.where(after.T, MASKED, 0).astype(bf16),
        "c_before": after.astype(bf16), "c_ones": np.ones((P, P), bf16),
        "c_slots": np.arange(SLOTS, dtype=np.float32)[None],
        "c_ranks": np.broadcast_to(E - np.arange(E, dtype=np.float32), (P, E)),
        "c_keep": keep, "c_sel": sel.reshape(3 * BCROWS, BCROWS, P),
    }
    nc = bacc.Bacc("TRN2", target_bir_lowering=False, num_devices=1)
    arrays, args = {}, []
    for name, a in lay.items():
        a = np.ascontiguousarray(a)
        arrays[f"in_{name}"] = a
        args.append(nc.dram_tensor(f"in_{name}", a.shape, mybir.dt.from_np(a.dtype), kind="ExternalInput").ap())
    args.append(nc.dram_tensor("out_rows", (TOK, D), F32, kind="ExternalOutput").ap())
    build(nc, *args)
    r = run_bass_kernel_spmd(nc, [arrays], core_ids=[0])
    return r.results[0]["out_rows"].reshape(BATCH, SEQ, D)
```
